# Optimizing a Trainium2 kernel written in Bass

```python
import numpy as np
import jax
import jax.numpy as jnp

def _softmax(x, axis=-1):
    return jax.nn.softmax(x, axis=axis)

def _gelu(x):
    return jax.nn.gelu(x, approximate=True)

def _silu(x):
    return jax.nn.silu(x)

def _sigmoid(x):
    return jax.nn.sigmoid(x)

def _layernorm(x, axis=-1, eps=1e-05):
    m = jnp.mean(x, axis=axis, keepdims=True)
    v = jnp.var(x, axis=axis, keepdims=True)
    return (x - m) / jnp.sqrt(v + eps)

def _scatter_add(tgt, idx, src, axis=0):
    return tgt.at[idx].add(src)

def _segment_sum(src, seg, n):
    return jax.ops.segment_sum(src, seg, n)
kernel_name = 'mk_xattn_ffn_d2_seqx_r4_e4d80d'

def setup_inputs(seed: int=0):
    np.random.seed(seed)
    _w = jnp.asarray

    def _rec_inputs():
        import jax
        import jax.numpy as jnp
        _rk = jax.random.key(seed)
        x = -7.109e-05 + 0.9999 * jax.random.normal(jax.random.fold_in(_rk, 1), (2, 1024, 256), jnp.float32)
        _lenS = 1024 - jax.random.randint(jax.random.fold_in(_rk, 7), (2,), 0, max(1, 1024 // 4) + 1, jnp.int32)
        _lenS2 = 77 - jax.random.randint(jax.random.fold_in(_rk, 8), (2,), 0, max(1, 77 // 4) + 1, jnp.int32)
        _ctx_768P = jax.random.normal(jax.random.fold_in(_rk, 11), (2, 16, 192), jnp.float32)
        _ctx_768c = jax.random.dirichlet(jax.random.fold_in(_rk, 511), 0.3 * jnp.ones((16,), jnp.float32), (2, 77))
        _ctx_768t = jnp.einsum('bsk,bkd->bsd', _ctx_768c, _ctx_768P)
        _ctx_768t = _ctx_768t * jax.lax.rsqrt(jnp.mean(jnp.square(_ctx_768t)) + 1e-12) * 0.953939
        ctx_768 = 0.000486113 + 1.00014 * (_ctx_768t + 0.3 * jax.random.normal(jax.random.fold_in(_rk, 611), (2, 77, 192), jnp.float32))
        _validS = jnp.arange(1024)[None, :] < _lenS[:, None]
        _validS2 = jnp.arange(77)[None, :] < _lenS2[:, None]
        _causal = jnp.tril(jnp.ones((1024, 1024), dtype=bool))
        mask_BxS2_bk0 = jnp.logical_not(jnp.broadcast_to(_validS2[:, :], (2, 77)))
        return (x, ctx_768, mask_BxS2_bk0)
    x, ctx_768, mask_BxS2_bk0 = _rec_inputs()

    def _L0_xattn_setup():
        import jax, jax.numpy as jnp
        import numpy as np
        N_HEADS = 8
        D_EMBED = 256
        D_CROSS = 192
        D_HEAD = D_EMBED // N_HEADS
        key = jax.random.key(seed)
        ks = jax.random.split(key, 10)
        B, Lq, Lkv = (16, 1024, 77)
        s_e = 1.0 / np.sqrt(D_EMBED)
        s_c = 1.0 / np.sqrt(D_CROSS)
        return {'x': jax.random.normal(ks[0], (B, Lq, D_EMBED), jnp.float32), 'y': jax.random.normal(ks[1], (B, Lkv, D_CROSS), jnp.float32), 'Wq': jax.random.normal(ks[2], (D_EMBED, D_EMBED), jnp.float32) * s_e, 'bq': jnp.zeros((D_EMBED,), jnp.float32), 'Wk': jax.random.normal(ks[3], (D_CROSS, D_EMBED), jnp.float32) * s_c, 'bk': jnp.zeros((D_EMBED,), jnp.float32), 'Wv': jax.random.normal(ks[4], (D_CROSS, D_EMBED), jnp.float32) * s_c, 'bv': jnp.zeros((D_EMBED,), jnp.float32), 'Wo': jax.random.normal(ks[5], (D_EMBED, D_EMBED), jnp.float32) * s_e, 'bo': jnp.zeros((D_EMBED,), jnp.float32)}
    _L0_xattn_all = _L0_xattn_setup()
    _L0_xattn_in = {k: v for k, v in _L0_xattn_all.items() if k in ('Wq', 'bq', 'Wk', 'bk', 'Wv', 'bv', 'Wo', 'bo')}
    del _L0_xattn_all

    def _L0_ffn_setup():
        import jax, jax.numpy as jnp
        import numpy as np
        QB = 127.0
        EPS = 1e-05

        def _ste(x, q):
            return x + jax.lax.stop_gradient(q - x)

        def bitlinear(x, W, b):
            w_scale = jnp.clip(jnp.mean(jnp.abs(W)), EPS, None)
            Wq = _ste(W, jnp.clip(jnp.round(W / w_scale), -1.0, 1.0) * w_scale)
            x_scale = jnp.clip(jnp.max(jnp.abs(x), axis=-1, keepdims=True), EPS, None)
            xq = _ste(x, jnp.clip(jnp.round(x * (QB / x_scale)), -QB - 1.0, QB) * (x_scale / QB))
            return jnp.einsum('bnd,hd->bnh', xq, Wq) + b
        key = jax.random.key(seed)
        k0, k1, k2 = jax.random.split(key, 3)
        B, N, D = (8, 1024, 256)
        H = int(D * 4.0)
        x = jax.random.normal(k0, (B, N, D), dtype=jnp.float32)
        W1 = jax.random.normal(k1, (H, D), dtype=jnp.float32) * 0.02
        b1 = jnp.zeros((H,), dtype=jnp.float32)
        W2 = jax.random.normal(k2, (D, H), dtype=jnp.float32) * 0.02
        b2 = jnp.zeros((D,), dtype=jnp.float32)
        return {'x': x, 'W1': W1, 'b1': b1, 'W2': W2, 'b2': b2}
    _L0_ffn_all = _L0_ffn_setup()
    _L0_ffn_in = {k: v for k, v in _L0_ffn_all.items() if k in ('W1', 'b1', 'W2', 'b2')}
    del _L0_ffn_all

    def _L1_xattn_setup():
        import jax, jax.numpy as jnp
        import numpy as np
        DIM_IN, DIM_LAT, DIM_HEAD = (192, 256, 64)
        INNER = max(DIM_LAT, DIM_IN)
        HEADS = INNER // DIM_HEAD
        SCALE = DIM_HEAD ** (-0.5)
        RMS_EPS = 1e-08
        LN_EPS = 1e-05

        def layernorm(x, g, b):
            mu = jnp.mean(x, axis=-1, keepdims=True)
            var = jnp.mean((x - mu) ** 2, axis=-1, keepdims=True)
            return (x - mu) * jax.lax.rsqrt(var + LN_EPS) * g + b

        def rmsnorm(x, gamma):
            norm = jnp.sqrt(jnp.sum(x * x, axis=-1, keepdims=True)) * x.shape[-1] ** (-0.5)
            return x / jnp.maximum(norm, RMS_EPS) * gamma
        key = jax.random.key(seed)
        ks = jax.random.split(key, 12)
        b, n, m = (4, 1024, 128)
        x = jax.random.normal(ks[0], (b, n, DIM_IN), jnp.float32)
        latents = jax.random.normal(ks[1], (b, m, DIM_LAT), jnp.float32)
        mask = jax.random.randint(ks[2], (b, n), 0, 2).astype(bool)
        s = lambda k, sh, fan: jax.random.normal(k, sh, jnp.float32) * fan ** (-0.5)
        return {'x': x, 'latents': latents, 'mask': mask, 'ln_x_g': jnp.ones((DIM_IN,), jnp.float32), 'ln_x_b': jnp.zeros((DIM_IN,), jnp.float32), 'ln_l_g': jnp.ones((DIM_LAT,), jnp.float32), 'ln_l_b': jnp.zeros((DIM_LAT,), jnp.float32), 'qn_g': jnp.ones((DIM_HEAD,), jnp.float32), 'kn_g': jnp.ones((DIM_HEAD,), jnp.float32), 'Wq': s(ks[3], (INNER, DIM_LAT), DIM_LAT), 'Wkv': s(ks[4], (2 * INNER, DIM_IN), DIM_IN), 'Wlkv': s(ks[5], (2 * INNER, DIM_LAT), DIM_LAT), 'Wo': s(ks[6], (DIM_LAT, INNER), INNER), 'bo': jnp.zeros((DIM_LAT,), jnp.float32)}
    _L1_xattn_all = _L1_xattn_setup()
    _L1_xattn_in = {k: v for k, v in _L1_xattn_all.items() if k in ('ln_x_g', 'ln_x_b', 'ln_l_g', 'ln_l_b', 'qn_g', 'kn_g', 'Wq', 'Wkv', 'Wlkv', 'Wo', 'bo')}
    del _L1_xattn_all

    def _L1_ffn_setup():
        import jax, jax.numpy as jnp
        import numpy as np
        ALPHA = 1.702
        LIMIT = 7.0
        TOPK = 2
        D, I, E = (256, 512, 8)
        B, S = (2, 512)

        def swiglu(x):
            g = x[..., ::2]
            l = x[..., 1::2]
            g = jnp.minimum(g, LIMIT)
            l = jnp.clip(l, -LIMIT, LIMIT)
            return g * jax.nn.sigmoid(ALPHA * g) * (l + 1.0)
        key = jax.random.key(seed)
        ks = jax.random.split(key, 16)
        sc = 0.02
        n = lambda k, shape, s=sc: jax.random.normal(k, shape, dtype=jnp.float32) * s
        return {'x': jax.random.normal(ks[0], (B, S, D), dtype=jnp.float32), 'gate_w': n(ks[1], (E, D)), 'gate_b': n(ks[2], (E,)), 'w1': n(ks[3], (E, D, 2 * I)), 'b1': n(ks[4], (E, 2 * I)), 'w3': n(ks[5], (E, D, 2 * I)), 'b3': n(ks[6], (E, 2 * I)), 'w2': n(ks[7], (E, I, D)), 'b2': n(ks[8], (E, D)), 'sw1': n(ks[9], (D, 2 * I)), 'sb1': n(ks[10], (2 * I,)), 'sw3': n(ks[11], (D, 2 * I)), 'sb3': n(ks[12], (2 * I,)), 'sw2': n(ks[13], (I, D)), 'sb2': n(ks[14], (D,))}
    _L1_ffn_all = _L1_ffn_setup()
    _L1_ffn_in = {k: v for k, v in _L1_ffn_all.items() if k in ('gate_w', 'gate_b', 'w1', 'b1', 'w3', 'b3', 'w2', 'b2', 'sw1', 'sb1', 'sw3', 'sb3', 'sw2', 'sb2')}
    del _L1_ffn_all
    return {'x': x, 'ctx_768': ctx_768, 'mask_BxS2_bk0': mask_BxS2_bk0, 'L0_xattn_Wq': _L0_xattn_in['Wq'], 'L0_xattn_bq': _L0_xattn_in['bq'], 'L0_xattn_Wk': _L0_xattn_in['Wk'], 'L0_xattn_bk': _L0_xattn_in['bk'], 'L0_xattn_Wv': _L0_xattn_in['Wv'], 'L0_xattn_bv': _L0_xattn_in['bv'], 'L0_xattn_Wo': _L0_xattn_in['Wo'], 'L0_xattn_bo': _L0_xattn_in['bo'], 'L0_ffn_W1': _L0_ffn_in['W1'], 'L0_ffn_b1': _L0_ffn_in['b1'], 'L0_ffn_W2': _L0_ffn_in['W2'], 'L0_ffn_b2': _L0_ffn_in['b2'], 'L1_xattn_ln_x_g': _L1_xattn_in['ln_x_g'], 'L1_xattn_ln_x_b': _L1_xattn_in['ln_x_b'], 'L1_xattn_ln_l_g': _L1_xattn_in['ln_l_g'], 'L1_xattn_ln_l_b': _L1_xattn_in['ln_l_b'], 'L1_xattn_qn_g': _L1_xattn_in['qn_g'], 'L1_xattn_kn_g': _L1_xattn_in['kn_g'], 'L1_xattn_Wq': _L1_xattn_in['Wq'], 'L1_xattn_Wkv': _L1_xattn_in['Wkv'], 'L1_xattn_Wlkv': _L1_xattn_in['Wlkv'], 'L1_xattn_Wo': _L1_xattn_in['Wo'], 'L1_xattn_bo': _L1_xattn_in['bo'], 'L1_ffn_gate_w': _L1_ffn_in['gate_w'], 'L1_ffn_gate_b': _L1_ffn_in['gate_b'], 'L1_ffn_w1': _L1_ffn_in['w1'], 'L1_ffn_b1': _L1_ffn_in['b1'], 'L1_ffn_w3': _L1_ffn_in['w3'], 'L1_ffn_b3': _L1_ffn_in['b3'], 'L1_ffn_w2': _L1_ffn_in['w2'], 'L1_ffn_b2': _L1_ffn_in['b2'], 'L1_ffn_sw1': _L1_ffn_in['sw1'], 'L1_ffn_sb1': _L1_ffn_in['sb1'], 'L1_ffn_sw3': _L1_ffn_in['sw3'], 'L1_ffn_sb3': _L1_ffn_in['sb3'], 'L1_ffn_sw2': _L1_ffn_in['sw2'], 'L1_ffn_sb2': _L1_ffn_in['sb2']}

def reference(x, ctx_768, mask_BxS2_bk0, L0_xattn_Wq, L0_xattn_bq, L0_xattn_Wk, L0_xattn_bk, L0_xattn_Wv, L0_xattn_bv, L0_xattn_Wo, L0_xattn_bo, L0_ffn_W1, L0_ffn_b1, L0_ffn_W2, L0_ffn_b2, L1_xattn_ln_x_g, L1_xattn_ln_x_b, L1_xattn_ln_l_g, L1_xattn_ln_l_b, L1_xattn_qn_g, L1_xattn_kn_g, L1_xattn_Wq, L1_xattn_Wkv, L1_xattn_Wlkv, L1_xattn_Wo, L1_xattn_bo, L1_ffn_gate_w, L1_ffn_gate_b, L1_ffn_w1, L1_ffn_b1, L1_ffn_w3, L1_ffn_b3, L1_ffn_w2, L1_ffn_b2, L1_ffn_sw1, L1_ffn_sb1, L1_ffn_sw3, L1_ffn_sb3, L1_ffn_sw2, L1_ffn_sb2):
    import jax
    import jax.numpy as jnp

    def _L0_xattn_ref(x, y, Wq, bq, Wk, bk, Wv, bv, Wo, bo):
        import jax, jax.numpy as jnp
        import numpy as np
        N_HEADS = 8
        D_EMBED = 256
        D_CROSS = 192
        D_HEAD = D_EMBED // N_HEADS
        q = jnp.einsum('bqd,de->bqe', x, Wq) + bq
        k = jnp.einsum('bkc,ce->bke', y, Wk) + bk
        v = jnp.einsum('bkc,ce->bke', y, Wv) + bv
        scale = 1.0 / np.sqrt(D_HEAD)
        scores = jnp.einsum('bqe,bke->bqk', q, k) * scale
        attn = jax.nn.softmax(scores, axis=-1)
        out = jnp.einsum('bqk,bke->bqe', attn, v)
        return jnp.einsum('bqe,ef->bqf', out, Wo) + bo

    def _L0_ffn_ref(x, W1, b1, W2, b2):
        import jax, jax.numpy as jnp
        import numpy as np
        QB = 127.0
        EPS = 1e-05

        def _ste(x, q):
            return x + jax.lax.stop_gradient(q - x)

        def bitlinear(x, W, b):
            w_scale = jnp.clip(jnp.mean(jnp.abs(W)), EPS, None)
            Wq = _ste(W, jnp.clip(jnp.round(W / w_scale), -1.0, 1.0) * w_scale)
            x_scale = jnp.clip(jnp.max(jnp.abs(x), axis=-1, keepdims=True), EPS, None)
            xq = _ste(x, jnp.clip(jnp.round(x * (QB / x_scale)), -QB - 1.0, QB) * (x_scale / QB))
            return jnp.einsum('bnd,hd->bnh', xq, Wq) + b
        h = bitlinear(x, W1, b1)
        h = jax.nn.gelu(h, approximate=False)
        return bitlinear(h, W2, b2)

    def _L1_xattn_ref(x, latents, mask, ln_x_g, ln_x_b, ln_l_g, ln_l_b, qn_g, kn_g, Wq, Wkv, Wlkv, Wo, bo):
        import jax, jax.numpy as jnp
        import numpy as np
        DIM_IN, DIM_LAT, DIM_HEAD = (192, 256, 64)
        INNER = max(DIM_LAT, DIM_IN)
        HEADS = INNER // DIM_HEAD
        SCALE = DIM_HEAD ** (-0.5)
        RMS_EPS = 1e-08
        LN_EPS = 1e-05

        def layernorm(x, g, b):
            mu = jnp.mean(x, axis=-1, keepdims=True)
            var = jnp.mean((x - mu) ** 2, axis=-1, keepdims=True)
            return (x - mu) * jax.lax.rsqrt(var + LN_EPS) * g + b

        def rmsnorm(x, gamma):
            norm = jnp.sqrt(jnp.sum(x * x, axis=-1, keepdims=True)) * x.shape[-1] ** (-0.5)
            return x / jnp.maximum(norm, RMS_EPS) * gamma
        b, n, _ = x.shape
        m = latents.shape[1]
        xn = layernorm(x, ln_x_g, ln_x_b)
        ln = layernorm(latents, ln_l_g, ln_l_b)
        q = ln @ Wq.T
        kv = jnp.concatenate([xn @ Wkv.T, ln @ Wlkv.T], axis=1)
        k, v = (kv[..., :INNER], kv[..., INNER:])
        split_heads = lambda t: t.reshape(t.shape[0], t.shape[1], HEADS, DIM_HEAD).transpose(0, 2, 1, 3)
        q, k, v = (split_heads(q), split_heads(k), split_heads(v))
        qn = rmsnorm(q, qn_g) * SCALE
        kn = rmsnorm(k, kn_g)
        attn = jnp.einsum('bhid,bhjd->bhij', qn, kn)
        full_mask = jnp.pad(mask, ((0, 0), (0, m)), constant_values=True)
        attn = jnp.where(full_mask[:, None, None, :], attn, -jnp.finfo(attn.dtype).max)
        attn = jax.nn.softmax(attn, axis=-1)
        out = jnp.einsum('bhij,bhjd->bhid', attn, v)
        out = out.transpose(0, 2, 1, 3).reshape(b, m, INNER)
        return out @ Wo.T + bo

    def _L1_ffn_ref(x, gate_w, gate_b, w1, b1, w3, b3, w2, b2, sw1, sb1, sw3, sb3, sw2, sb2):
        import jax, jax.numpy as jnp
        import numpy as np
        ALPHA = 1.702
        LIMIT = 7.0
        TOPK = 2
        D, I, E = (256, 512, 8)
        B, S = (2, 512)

        def swiglu(x):
            g = x[..., ::2]
            l = x[..., 1::2]
            g = jnp.minimum(g, LIMIT)
            l = jnp.clip(l, -LIMIT, LIMIT)
            return g * jax.nn.sigmoid(ALPHA * g) * (l + 1.0)
        b, s, d = x.shape
        xt = x.reshape(-1, d)
        scores = jax.nn.softmax(xt @ gate_w.T, axis=-1)
        biased = scores + gate_b
        _, idx = jax.lax.top_k(biased, TOPK)
        weights = jnp.take_along_axis(scores, idx, axis=-1)
        comb = (weights[..., None] * jax.nn.one_hot(idx, E, dtype=xt.dtype)).sum(1)

        def body(acc, p):
            ew1, eb1, ew3, eb3, ew2, eb2, ce = p
            h = swiglu((xt @ ew1 + eb1) * (xt @ ew3 + eb3))
            return (acc + ce[:, None] * (h @ ew2 + eb2), None)
        routed, _ = jax.lax.scan(body, jnp.zeros_like(xt), (w1, b1, w3, b3, w2, b2, comb.T))
        shared = swiglu((xt @ sw1 + sb1) * (xt @ sw3 + sb3)) @ sw2 + sb2
        return (routed + shared).reshape(b, s, d)
    x = x + _L0_xattn_ref(_layernorm(x, axis=-1), ctx_768, L0_xattn_Wq, L0_xattn_bq, L0_xattn_Wk, L0_xattn_bk, L0_xattn_Wv, L0_xattn_bv, L0_xattn_Wo, L0_xattn_bo)
    x = x + _L0_ffn_ref(_layernorm(x, axis=-1), L0_ffn_W1, L0_ffn_b1, L0_ffn_W2, L0_ffn_b2)
    x = x + _L1_xattn_ref(ctx_768, _layernorm(x, axis=-1), mask_BxS2_bk0, L1_xattn_ln_x_g, L1_xattn_ln_x_b, L1_xattn_ln_l_g, L1_xattn_ln_l_b, L1_xattn_qn_g, L1_xattn_kn_g, L1_xattn_Wq, L1_xattn_Wkv, L1_xattn_Wlkv, L1_xattn_Wo, L1_xattn_bo)
    x = x + _L1_ffn_ref(_layernorm(x, axis=-1), L1_ffn_gate_w, L1_ffn_gate_b, L1_ffn_w1, L1_ffn_b1, L1_ffn_w3, L1_ffn_b3, L1_ffn_w2, L1_ffn_b2, L1_ffn_sw1, L1_ffn_sb1, L1_ffn_sw3, L1_ffn_sb3, L1_ffn_sw2, L1_ffn_sb2)
    return x

_drawn_inputs = setup_inputs


def setup_inputs(seed=0):
    import zlib

    import numpy as np

    out = dict(_drawn_inputs(seed))
    spreads = {'L0_xattn_bq': (0.0, 0.1),
     'L0_xattn_bk': (0.0, 2.0),
     'L0_xattn_bv': (0.0, 0.1),
     'L0_xattn_bo': (0.0, 0.1),
     'L0_ffn_b1': (0.0, 0.368),
     'L0_ffn_b2': (0.0, 0.1),
     'L1_xattn_ln_x_g': (1.0, 0.6),
     'L1_xattn_ln_x_b': (0.0, 0.8),
     'L1_xattn_ln_l_g': (1.0, 0.2),
     'L1_xattn_ln_l_b': (0.0, 0.1),
     'L1_xattn_qn_g': (1.0, 0.6),
     'L1_xattn_kn_g': (1.0, 0.6),
     'L1_xattn_bo': (0.0, 0.1)}
    factors = {'L1_xattn_Wkv': 4.497,
     'L1_ffn_gate_w': 8.0,
     'L1_ffn_gate_b': 8.0,
     'L1_ffn_w1': 8.0,
     'L1_ffn_b1': 8.0,
     'L1_ffn_w3': 8.0,
     'L1_ffn_b3': 8.0,
     'L1_ffn_w2': 8.0,
     'L1_ffn_b2': 64.0,
     'L1_ffn_sw1': 3.355,
     'L1_ffn_sb1': 41.402,
     'L1_ffn_sw3': 3.369,
     'L1_ffn_sb3': 41.886,
     'L1_ffn_sw2': 3.334,
     'L1_ffn_sb2': 90.206}
    for name, (base, spread) in spreads.items():
        noise = np.random.default_rng([zlib.crc32(name.encode()), seed]).standard_normal(out[name].shape)
        drawn = base * np.exp(spread * noise) if base else spread * noise
        out[name] = jnp.asarray(drawn.astype(out[name].dtype))
    for name, factor in factors.items():
        out[name] = (out[name] * factor).astype(out[name].dtype)
    return out
```

```python
import concourse.bass as bass
from concourse import mybir
from contextlib import ExitStack
import numpy as np

_INS = ['x', 'ctx_768', 'mask_BxS2_bk0', 'L0_xattn_Wq', 'L0_xattn_bq', 'L0_xattn_Wk', 'L0_xattn_bk', 'L0_xattn_Wv',
        'L0_xattn_bv', 'L0_xattn_Wo', 'L0_xattn_bo', 'L0_ffn_W1', 'L0_ffn_b1', 'L0_ffn_W2', 'L0_ffn_b2',
        'L1_xattn_ln_x_g', 'L1_xattn_ln_x_b', 'L1_xattn_ln_l_g', 'L1_xattn_ln_l_b', 'L1_xattn_qn_g', 'L1_xattn_kn_g',
        'L1_xattn_Wq', 'L1_xattn_Wkv', 'L1_xattn_Wlkv', 'L1_xattn_Wo', 'L1_xattn_bo', 'L1_ffn_gate_w', 'L1_ffn_gate_b',
        'L1_ffn_w1', 'L1_ffn_b1', 'L1_ffn_w3', 'L1_ffn_b3', 'L1_ffn_w2', 'L1_ffn_b2', 'L1_ffn_sw1', 'L1_ffn_sb1',
        'L1_ffn_sw3', 'L1_ffn_sb3', 'L1_ffn_sw2', 'L1_ffn_sb2']


class Chain:

    def __init__(self, eng, sem):
        self.eng, self.sem, self.base, self.n, self.at, self.per = eng, sem, 0, 0, None, 0

    def loop(self, at, per):
        self.at, self.per, self.n = at, per, 0

    def done(self, turns):
        assert self.n == self.per, (self.n, self.per)
        self.base += turns * self.per
        self.at, self.n = None, 0

    def __call__(self, instruction):
        instruction.then_inc(self.sem, 1)
        self.n += 1
        if self.at is None:
            self.base, self.n = self.base + 1, 0
            self.eng.wait_ge(self.sem, self.base)
        else:
            self.eng.wait_ge(self.sem, self.at * self.per + (self.base + self.n))


def program(nc, ins, out):
    f32, bf16, i32 = mybir.dt.float32, mybir.dt.bfloat16, mybir.dt.int32
    ALU, ACT, AX = mybir.AluOpType, mybir.ActivationFunctionType, mybir.AxisListType
    P = 128
    B, S, D = ins['x'].shape
    SK, DC = ins['ctx_768'].shape[1:]
    T = B * S // P
    TB = S // P
    KC = D // P
    SKB = B * SK
    HID = ins['L0_ffn_W1'].shape[0]
    HC = HID // P
    DH = ins['L1_xattn_qn_g'].shape[0]
    NH = D // DH
    QKV = 3 * D
    E = ins['L1_ffn_gate_w'].shape[0]
    I2 = ins['L1_ffn_w1'].shape[2]
    I = I2 // 2
    IC = I // P
    TOPK = 2
    SLOTS = (B * S * TOPK - E) // P + E
    DCR = DC - P
    DA = DH + 1
    SCALE0 = 1.0 / float(np.sqrt(D // 8))
    LN_EPS, RMS_EPS, QB, QEPS = 1e-5, 1e-8, 127.0, 1e-5
    MAGIC = 12582912.0
    BIG = 1e30
    ALPHA, LIMIT = 1.702, 7.0
    WEXP = 2 * KC * I2 + IC * D
    OFF1, OFF3, OFF2 = 0, KC * I2, 2 * KC * I2
    SHARED = E
    SHARED_AT = E - 1
    NB = 2 * I2 + D

    ctx = ExitStack()
    with ctx:
        ctx.enter_context(nc.allow_non_contiguous_dma(reason="short bias columns"))

        def sb(name, shape, dt=f32):
            return ctx.enter_context(nc.sbuf_tensor(name, shape, dt))

        def sem(name):
            return ctx.enter_context(nc.semaphore(name))

        moe_in = nc.dram_tensor("moe_in", (SLOTS * P, D), f32, kind="Internal").ap()
        moe_x = nc.dram_tensor("moe_x", (T * P, D), f32, kind="Internal").ap()
        moe_out = nc.dram_tensor("moe_out", (SLOTS * P, D), f32, kind="Internal").ap()
        moe_sh = nc.dram_tensor("moe_sh", (T * P, D), f32, kind="Internal").ap()

        x_sb = sb("x_sb", [P, T, D])
        wexp = sb("wexp", [P, E * WEXP])
        aux = sb("aux", [P, 5250])
        small = sb("small", [P, 800])

        class Words:

            def __init__(self, buf, at, end):
                self.buf, self.at, self.end = buf, at, end

            def take(self, n, parts=None, dt=None):
                a, words = self.at, n if dt is None else (n + 1) // 2
                self.at += words
                assert self.at <= self.end, (self.at, self.end)
                v = self.buf[:, a:a + words]
                if dt is not None:
                    v = v.bitcast(dt)
                return v if parts is None else v.rearrange("p (a b) -> p a b", a=parts)

        scr = Words(wexp, WEXP, SHARED_AT * WEXP)
        qkv = scr.take(T * QKV, T)
        mark = scr.at
        scr.at = WEXP
        w1_raw = scr.take(HC * D, HC)
        w2_raw = scr.take(KC * HID, KC)
        w1T = scr.take(KC * HID, KC, bf16)
        w2T = scr.take(HC * D, HC, bf16)
        b1_all = scr.take(HID)
        h_f = [scr.take(HID) for _ in range(2)]
        h_q = [scr.take(HID, dt=bf16) for _ in range(2)]
        h_qT = [scr.take(HID, HC, bf16) for _ in range(2)]
        assert scr.at <= mark
        w1_t = h_f[0].bitcast(bf16).rearrange("p (a b) -> p a b", a=HC)
        w2_t = h_f[1].bitcast(bf16).rearrange("p (a b) -> p a b", a=KC)
        scr.at = mark
        wT = scr.take(KC * QKV, KC)
        wcT = scr.take(KC * 2 * D, KC)
        woT = scr.take(NH * (D + 1), NH)
        zeros = scr.take(D)
        mask_u = scr.take(SKB).bitcast(i32)
        first = scr.at
        QT = [scr.take(S) for _ in range(2)]
        KT = [scr.take(S + SK) for _ in range(2)]
        vh = [scr.take((TB + 1) * DA, TB + 1) for _ in range(2)]
        pT = [scr.take(512) for _ in range(3)]
        oT = [scr.take(S) for _ in range(2)]
        qs = [scr.take(TB * DH, TB) for _ in range(2)]
        ks = [scr.take((TB + 1) * DH, TB + 1) for _ in range(2)]
        ax = Words(wexp, first, scr.at)
        l0_wq = ax.take(KC * D, KC)
        l0_wk = ax.take(2 * D, 2)
        l0_wv = ax.take(2 * D, 2)
        l0_wo = ax.take(KC * D, KC)
        l0_wqT = ax.take(KC * D, KC)
        ctx_sb = ax.take(B * DC, B)
        ctxT = ax.take(2 * SKB, 2)
        kT0 = ax.take(KC * SKB, KC)
        vT0 = ax.take(KC * SKB, KC)
        m0 = ax.take(KC * SKB, KC)
        c0 = ax.take(SKB)
        vv0 = ax.take(B * D, B)
        bo0 = ax.take(D)
        wq_raw = scr.take(KC * D, KC)
        wlkv_raw = scr.take(2 * KC * D, 2 * KC)
        wkv_raw = scr.take(2 * KC * DC, 2 * KC)
        wo_raw = scr.take(KC * D, KC)

        ax = Words(aux, 0, 5250)
        xn = ax.take(4 * D, 4)
        xnT = ax.take(KC * 512, KC)
        xq = [ax.take(D, dt=bf16) for _ in range(2)]
        xqT = [ax.take(D, KC, bf16) for _ in range(2)]
        p0 = ax.take(4 * SK, 4)
        ckv = ax.take(B * 2 * D, B)
        b2_all, bo1_all, gate_raw = ax.take(D), ax.take(D), ax.take(D)[0:E]
        ax.at = 0
        x_in = [ax.take(D) for _ in range(2)]
        x_inT = [ax.take(D, KC) for _ in range(2)]
        lift = [ax.take(I) for _ in range(2)]
        gate = ax.take(I)
        line = ax.take(I)
        sig = ax.take(I)
        h_moe = ax.take(I)
        h_moeT = ax.take(I, IC)
        y_sb = [ax.take(D) for _ in range(2)]
        hot_t = [ax.take(P, dt=bf16) for _ in range(2)]
        ya, yb, ys = ([v[:, u * D:(u + 1) * D] for u in range(2)] for v in (*lift, gate))

        ident = sb("ident", [P, P])
        ident_b = sb("ident_b", [P, P], bf16)
        ones = sb("ones", [P, P])
        ones_b = sb("ones_b", [P, P], bf16)
        before = sb("before", [P, P], bf16)
        bias_b = sb("bias_b", [96, NB], bf16)
        hot_sh = sb("hot_sh", [96, P], bf16)

        sm = Words(small, 0, 800)
        stats = sm.take(T * 6, T)
        mv = sm.take((T + B) * 2, T + B)
        root_a, root_s, root_t, rstd = (sm.take(T * 2 * NH + 2 * NH) for _ in range(4))
        ss = root_a
        rn = rstd
        gateT = sb("gateT", [P, KC, E])
        gateb = sb("gateb", [P, E])
        cols = sm.take(40)
        bk0, bv0, bq0 = cols[:, 0:2], cols[:, 2:4], cols[:, 4:6]
        lg, lb, xg, xb = cols[:, 6:8], cols[:, 8:10], cols[:, 10:12], cols[:, 12:14]
        qg, kg = cols[:, 14:15], cols[:, 15:16]
        wsum, wsc, winv = cols[:, 16:18], cols[:, 18:20], cols[:, 20:22]
        amax, aden, arow = cols[:, 22:24], cols[:, 24:26], cols[:, 26:28]
        hmax, hden, hrow = cols[:, 28:30], cols[:, 30:32], cols[:, 32:34]
        yden = cols[:, 34:36]
        maskc_u = sb("maskc_u", [SK, B], i32)
        mask_row = sb("mask_row", [P, B, SK])
        mask_col = sb("mask_col", [SK, B])
        mask_now = sb("mask_now", [SK, 1])
        mx4, sums4 = sm.take(4), sm.take(4)
        mx3 = sm.take(TB * 3, TB)
        negm = sm.take(TB)
        p0T = xnT[:, 0, :]
        cmask = p0[:, 0, :]
        pb = [ctx.enter_context(nc.psum_tensor(f"bank{n}", [P, 512], f32)) for n in range(8)]
        rt = Words(wexp, SHARED_AT * WEXP - 7200, SHARED_AT * WEXP)
        NORM_AT = 4
        xm = wexp[:, NORM_AT * WEXP:NORM_AT * WEXP + T * D].rearrange("p (a b) -> p a b", a=T)
        score, biased, sel, cum, pos, row, tmp8 = (rt.take(T * E, T) for _ in range(7))
        big1, big2 = rt.take(T * E * E, T * E), rt.take(T * E * E, T * E)
        sel_b, cum_b, inc_b = (rt.take(T * E, T, bf16) for _ in range(3))
        lower = rt.take(E * E, E)
        cnt, cnt_i, ntile, tend, tstart = (rt.take(E) for _ in range(5))
        slot_no = rt.take(SLOTS)
        slot_cmp = rt.take(SLOTS * E, SLOTS)
        den16 = rt.take(T)
        bias_f = rt.take(NB)
        bias_part = rt.take(NB, dt=bf16)
        route = sb("route", [P, 4, T])
        route_i = sb("route_i", [P, 2, T], i32)
        slot_e = rt.take(SLOTS)
        slot_i = sb("slot_i", [1, SLOTS], i32)
        hot = sb("hot", [96, SLOTS], bf16)
        eno_i = sb("eno_i", [P, 1], i32)
        eno = sb("eno", [P, 1])

        names = """ld_x ld_l0 ld_ffn ld_l1 ld_route ld_shared ld_e0 ld_mid ld_last const prep_full prep_free
            root_in root_out chain chain_pool
            g_xn g_xnT_full g_xnT g_sc g_sh g_p g_pT_full g_pT g_av
            f_xq f_xqT_full f_xqT f_acc f_pre f_h f_amax f_h127 f_hq f_hqT_full f_hqT f_y f_yout f_b2
            l_xh l_xT_full l_xT l_qkv l_qk l_v l_sq l_ss l_bo
            a_qk a_v t_full t_free a_mx_full a_mx_free a_negm a_rows a_s_full a_p a_pv a_o a_oT
            r_norm r_x r_xT_full r_xT r_logit r_e r_exp r_sel r_pos r_done r_slot r_hot r_bias
            zero xdram scat
            """.split()
        s = {n: sem(n) for n in names}
        st_in = [sem(f"ym_in{u}") for u in range(2)]
        mnames = "xin xinT_full xinT prod lifted gated sigd lined hid hT_full hT y ysb hot yout".split()
        m = [{n: sem(f"m{k}_{n}") for n in mnames} for k in range(2)]
        m_x = [[sem(f"m{k}_x{u}") for u in range(2)] for k in range(2)]
        m_st = [[sem(f"m{k}_st{u}") for u in range(2)] for k in range(2)]
        c_y = [sem(f"c_y{u}") for u in range(2)]
        c_s = [sem(f"c_s{u}") for u in range(2)]
        c_used, c_acc, c_out = sem("c_used"), sem("c_acc"), sem("c_out")

        W = ins
        NLD = {}

        block = ctx.enter_context(nc.Block())

        def halves(e, off, kc):
            v = wexp[:, bass.ds(e + (off + kc * I2), I2)]
            return v.rearrange("p (n two) -> p n two", two=2)

        @block.sync
        def _(sp):
            def load(dst, src, to):
                sp.dma_start(dst, src).then_inc(s[to], 16)
                NLD[to] = NLD.get(to, 0) + 16

            load(x_sb[:], W['x'].rearrange("b (t p) d -> p (b t) d", p=P), 'ld_x')
            load(l0_wq[:], W['L0_xattn_Wq'].rearrange("(c p) n -> p c n", p=P), 'ld_l0')
            load(ctx_sb[0:SK], W['ctx_768'].rearrange("b k c -> k b c"), 'ld_l0')
            for dst, w in ((l0_wk, 'L0_xattn_Wk'), (l0_wv, 'L0_xattn_Wv')):
                load(dst[:, 0, :], W[w][0:P, :], 'ld_l0')
                load(dst[0:DCR, 1, :], W[w][P:DC, :], 'ld_l0')
            load(l0_wo[:], W['L0_xattn_Wo'].rearrange("(c p) n -> p c n", p=P), 'ld_l0')
            for dst, w in ((bk0, 'L0_xattn_bk'), (bv0, 'L0_xattn_bv'), (bq0, 'L0_xattn_bq')):
                load(dst, W[w].rearrange("(c p) -> p c", p=P), 'ld_l0')
            load(bo0[0:1, :], W['L0_xattn_bo'].rearrange("(a n) -> a n", a=1), 'ld_l0')
            load(w1_raw[:], W['L0_ffn_W1'].rearrange("(t p) n -> p t n", p=P), 'ld_ffn')
            load(w2_raw[:], W['L0_ffn_W2'].rearrange("(t p) n -> p t n", p=P), 'ld_ffn')
            load(b1_all[:], W['L0_ffn_b1'].partition_broadcast(P), 'ld_ffn')
            load(b2_all[:], W['L0_ffn_b2'].partition_broadcast(P), 'ld_ffn')
            load(wq_raw[:], W['L1_xattn_Wq'].rearrange("(t p) n -> p t n", p=P), 'ld_l1')
            load(wlkv_raw[:], W['L1_xattn_Wlkv'].rearrange("(t p) n -> p t n", p=P), 'ld_l1')
            load(wkv_raw[:], W['L1_xattn_Wkv'].rearrange("(t p) n -> p t n", p=P), 'ld_l1')
            load(wo_raw[:], W['L1_xattn_Wo'].rearrange("(t p) n -> p t n", p=P), 'ld_l1')
            for dst, w in ((lg, 'L1_xattn_ln_l_g'), (lb, 'L1_xattn_ln_l_b')):
                load(dst, W[w].rearrange("(c p) -> p c", p=P), 'ld_l1')
            for dst, w in ((xg, 'L1_xattn_ln_x_g'), (xb, 'L1_xattn_ln_x_b')):
                load(dst[:, 0:1], W[w][0:P].rearrange("(p a) -> p a", a=1), 'ld_l1')
                load(dst[0:DCR, 1:2], W[w][P:DC].rearrange("(p a) -> p a", a=1), 'ld_l1')
            for dst, w in ((qg, 'L1_xattn_qn_g'), (kg, 'L1_xattn_kn_g')):
                load(dst[0:DH], W[w].rearrange("(p a) -> p a", a=1), 'ld_l1')
            load(bo1_all[:], W['L1_xattn_bo'].partition_broadcast(P), 'ld_l1')
            load(mask_u, W['mask_BxS2_bk0'].rearrange("b k -> (b k)").partition_broadcast(P), 'ld_l1')
            load(maskc_u[:], W['mask_BxS2_bk0'].rearrange("b k -> k b"), 'ld_l1')
            load(gate_raw[:], W['L1_ffn_gate_w'], 'ld_l1')
            load(gateb[:], W['L1_ffn_gate_b'].partition_broadcast(P), 'ld_l1')

            def expert(at, w1, w3, w2, to):
                base = at * WEXP
                for off, w, c in ((OFF1, w1, KC), (OFF3, w3, KC), (OFF2, w2, IC)):
                    n = w.shape[-1]
                    load(wexp[:, base + off:base + off + c * n].rearrange("p (c n) -> p c n", c=c),
                         w.rearrange("(c p) n -> p c n", p=P), to)

            expert(SHARED_AT, W['L1_ffn_sw1'], W['L1_ffn_sw3'], W['L1_ffn_sw2'], 'ld_shared')
            expert(0, W['L1_ffn_w1'][0], W['L1_ffn_w3'][0], W['L1_ffn_w2'][0], 'ld_e0')
            sp.wait_ge(s['const'], 1)
            for n in range(SLOTS):
                sp.dma_start(moe_in[n * P:(n + 1) * P, :], zeros[:]).then_inc(s['zero'], 16)
            sp.wait_ge(s['zero'], 16 * SLOTS)
            sp.wait_ge(s['r_bias'], 1)
            for k in range(3):
                r = slice(32 * k, 32 * k + E)
                q = slice(32 * k + E, 32 * k + E + 1)
                for a, b, wn, sn in ((0, I2, 'L1_ffn_b1', 'L1_ffn_sb1'), (I2, 2 * I2, 'L1_ffn_b3', 'L1_ffn_sb3'),
                                     (2 * I2, NB, 'L1_ffn_b2', 'L1_ffn_sb2')):
                    load(bias_f[r, a:b], W[wn], 'ld_route')
                    load(bias_f[q, a:b], W[sn].rearrange("(a n) -> a n", a=1), 'ld_route')
            def routed(e, to):
                expert(e, W['L1_ffn_w1'][e], W['L1_ffn_w3'][e], W['L1_ffn_w2'][e], to)

            sp.wait_ge(s['a_oT'], 1)
            for e in range(1, NORM_AT):
                routed(e, 'ld_mid')
            sp.wait_ge(s['r_norm'], T)
            sp.dma_start(moe_x.rearrange("(t p) d -> p t d", p=P), xm[:]).then_inc(s['xdram'], 16)
            sp.wait_ge(s['xdram'], 16)
            sp.wait_ge(s['r_hot'], 3)
            for e in range(NORM_AT + 1, E - 1):
                routed(e, 'ld_mid')

            def tiles(k, n, src, dst):
                def turn(t, u, first):
                    if not first:
                        sp.wait_ge(m[k]['xinT_full'], t - 1)
                    sp.dma_start(x_in[u], src[bass.ds(t * P, P), :]).then_inc(m_x[k][u], 16)

                def store(t, u):
                    sp.wait_ge(m[k]['ysb'], t + 1)
                    sp.dma_start(dst[bass.ds(t * P, P), :], y_sb[u]).then_inc(m_st[k][u], 16)

                turn(0, 0, True)
                turn(1, 1, True)
                with sp.Fori(0, (n - 2) // 2) as i:
                    for u in range(2):
                        turn(i * 2 + (u + 2), u, False)
                        store(i * 2 + u, u)
                done = (n - 2) // 2 * 2
                for t in range(done, n):
                    if t + 2 < n:
                        turn(t + 2, t % 2, False)
                    store(t, t % 2)

            tiles(0, T, moe_x, moe_sh)
            for u in range(2):
                sp.wait_ge(m_st[0][u], 16 * (T // 2))
            routed(E - 1, 'ld_last')
            sp.wait_ge(s['scat'], 16 * 2 * T)
            routed(NORM_AT, 'ld_last')
            tiles(1, SLOTS, moe_in, moe_out)
            for u in range(2):
                sp.wait_ge(m_st[1][u], 16 * ((SLOTS + 1 - u) // 2))
            outv = out.rearrange("b (t p) d -> p (b t) d", p=P)
            for t in range(T):
                u = t % 2
                if t >= 2:
                    sp.wait_ge(c_used, t - 1)
                sp.dma_start(ys[u], moe_sh[t * P:(t + 1) * P, :]).then_inc(c_s[u], 16)
                if t >= 1:
                    sp.wait_ge(c_used, t)
                    sp.dma_start(outv[:, t - 1, :], x_sb[:, t - 1, :]).then_inc(c_out, 16)
            sp.wait_ge(c_used, T)
            sp.dma_start(outv[:, T - 1, :], x_sb[:, T - 1, :]).then_inc(c_out, 16)
            sp.wait_ge(c_out, 16 * T)

        @block.gpsimd
        def _(pool):
            g = nc.gpsimd
            link = Chain(pool, s['chain_pool'])
            g.memset(zeros[:], 0.0).then_inc(s['const'], 1)
            g.memset(ones[:], 1.0)
            g.memset(ones_b[:], 1.0)
            link(g.memset(ident[:], 0.0))
            link(g.affine_select(out=ident[:], in_=ident[:], compare_op=ALU.not_equal, fill=1.0, base=0,
                                 pattern=[[-1, P]], channel_multiplier=1))
            g.tensor_copy(ident_b[:], ident[:])
            link(g.affine_select(out=before[:], in_=ones_b[:], compare_op=ALU.is_gt, fill=0.0, base=0,
                                 pattern=[[1, P]], channel_multiplier=-1))
            link(g.memset(mv[:], 1.0))
            link(g.memset(ctxT[:], 0.0))
            link(g.memset(woT[:], 0.0))
            link(g.memset(woT[DH:DA, :, D:D + 1], 1.0))
            g.iota(eno_i[:], pattern=[[0, 1]], base=0, channel_multiplier=1).then_inc(s['const'], 1)

            with pool.Fori(0, T) as t:
                pool.wait_ge(s['f_xq'], t + 1)
                g.tensor_tensor(x_sb[:, bass.ds(t, 1), :].rearrange("p a d -> p (a d)"),
                                x_sb[:, bass.ds(t, 1), :].rearrange("p a d -> p (a d)"),
                                b2_all[:], ALU.add).then_inc(s['f_b2'], 1)

            with pool.Fori(0, T) as t:
                pool.wait_ge(s['l_xh'], t + 1)
                g.tensor_tensor(x_sb[:, bass.ds(t, 1), :].rearrange("p a d -> p (a d)"),
                                x_sb[:, bass.ds(t, 1), :].rearrange("p a d -> p (a d)"),
                                bo1_all[:], ALU.add).then_inc(s['l_bo'], 1)

            pool.wait_ge(s['l_bo'], T)
            for u in range(2):
                link(g.memset(KT[u][DH:DA, :], 1.0))
                link(g.memset(vh[u][:, :, DH:DA], 1.0))
            with pool.Fori(0, B) as b:
                with pool.Fori(0, NH // 2) as hp:
                    it = b * (NH // 2) + hp
                    for u in range(2):
                        pool.wait_ge(s['a_o'], it * 2)
                        col = hp * (2 * DH) + (2 * D + u * DH)
                        g.tensor_copy(vh[u][:, 0:TB, 0:DH], qkv[:, bass.ds(b * TB, TB), bass.ds(col, DH)])
                        colc = hp * (2 * DH) + (D + u * DH)
                        g.tensor_copy(vh[u][0:SK, TB, 0:DH],
                                      ckv[0:SK, bass.ds(b, 1), bass.ds(colc, DH)].rearrange("p a d -> p (a d)"))\
                            .then_inc(s['a_v'], 1)

            pool.wait_ge(s['r_norm'], T)
            with pool.Fori(0, T // 2) as i:
                for u in range(2):
                    pool.wait_ge(s['r_xT'], i * 2 + u)
                    g.tensor_copy(xn[:, u, :], xm[:, bass.ds(i * 2 + u, 1), :].rearrange("p a d -> p (a d)"))\
                        .then_inc(s['r_x'], 1)
            link(g.memset(lower[:], 1.0))
            lw = lower[:]
            link(g.affine_select(out=lw, in_=lw, compare_op=ALU.is_gt, fill=0.0, base=0,
                                 pattern=[[1, E], [-1, E]], channel_multiplier=0))
            link(g.memset(bias_f[:], 0.0))
            g.iota(slot_no[:], pattern=[[1, SLOTS]], base=0, channel_multiplier=0,
                   allow_small_or_imprecise_dtypes=True).then_inc(s['r_bias'], 1)

            pool.wait_ge(s['r_done'], 1)
            pool.wait_ge(s['zero'], 16 * SLOTS)
            for t in range(T):
                for c in range(2):
                    g.indirect_dma_start(out=moe_in, out_offset=bass.IndirectOffsetOnAxis(ap=route_i[:, c, t:t + 1], axis=0),
                                         in_=xm[:, t, :], in_offset=None,
                                         bounds_check=SLOTS * P - 1, oob_is_err=False).then_inc(s['scat'], 16)
            pool.wait_ge(s['scat'], 16 * 2 * T)
            def pick(t, u):
                g.tensor_copy(hot_t[u][0:96, :], hot[:, bass.ds(t, 1)].to_broadcast([96, P])).then_inc(m[1]['hot'], 1)

            pool.wait_ge(s['r_hot'], 3)
            pick(0, 0)
            pick(1, 1)
            with pool.Fori(0, (SLOTS - 3) // 2) as i:
                for u in range(2):
                    pool.wait_ge(m[1]['y'], i * 2 + (u + 1))
                    pick(i * 2 + (2 + u), u)
            pool.wait_ge(m[1]['y'], SLOTS - 2)
            pick(SLOTS - 1, 0)

            for u in range(2):
                pool.wait_ge(m_st[1][u], 16 * ((SLOTS + 1 - u) // 2))
            for t in range(T):
                u = t % 2
                if t >= 2:
                    pool.wait_ge(c_used, t - 1)
                for c, y in ((0, ya), (1, yb)):
                    g.indirect_dma_start(out=y[u], out_offset=None, in_=moe_out,
                                         in_offset=bass.IndirectOffsetOnAxis(ap=route_i[:, c, t:t + 1], axis=0),
                                         bounds_check=SLOTS * P - 1, oob_is_err=False).then_inc(c_y[u], 16)

        @block.tensor
        def _(pe):
            mm = nc.tensor.matmul
            tr = nc.tensor.transpose
            unit = [0]

            def bank():
                if unit[0] >= 2:
                    pe.wait_ge(s['prep_free'], unit[0] - 1)
                unit[0] += 1
                return pb[(unit[0] - 1) % 2]

            pe.wait_ge(s['const'], 2)
            pe.wait_ge(s['ld_l0'], NLD['ld_l0'])
            o = bank()
            for ec in range(KC):
                for dc in range(KC):
                    a = (ec * KC + dc) * P
                    last = tr(o[:, a:a + P], l0_wq[:, dc, ec * P:(ec + 1) * P], ident[:])
            last.then_inc(s['prep_full'], 1)
            o = bank()
            for b in range(B):
                tr(o[:, b * SK:(b + 1) * SK], ctx_sb[0:SK, b, 0:P], ident[0:SK, 0:SK])
                last = tr(o[0:DCR, SKB + b * SK:SKB + (b + 1) * SK], ctx_sb[0:SK, b, P:DC], ident[0:SK, 0:SK])
            last.then_inc(s['prep_full'], 1)
            pe.wait_ge(s['prep_free'], 2)
            for w in (l0_wk, l0_wv):
                o = bank()
                for ec in range(KC):
                    mm(o[:, ec * SKB:(ec + 1) * SKB], w[:, 0, ec * P:(ec + 1) * P], ctxT[:, 0, :], start=True, stop=False)
                    last = mm(o[:, ec * SKB:(ec + 1) * SKB], w[0:DCR, 1, ec * P:(ec + 1) * P], ctxT[0:DCR, 1, :],
                              start=False, stop=True)
                last.then_inc(s['prep_full'], 1)
            pe.wait_ge(s['prep_free'], 3)
            o = bank()
            for dc in range(KC):
                for ec in range(KC):
                    mm(o[:, dc * SKB:(dc + 1) * SKB], l0_wqT[:, ec, dc * P:(dc + 1) * P], kT0[:, ec, :],
                       start=ec == 0, stop=ec == KC - 1)
            for ec in range(KC):
                last = mm(o[0:1, KC * SKB:(KC + 1) * SKB], bq0[:, ec:ec + 1], kT0[:, ec, :], start=ec == 0, stop=ec == KC - 1)
            last.then_inc(s['prep_full'], 1)
            pe.wait_ge(s['prep_free'], 4)
            o = bank()
            for b in range(B):
                for ec in range(KC):
                    mm(o[0:SK, b * D:(b + 1) * D], vT0[:, ec, b * SK:(b + 1) * SK], l0_wo[:, ec, :], start=ec == 0, stop=False)
                last = mm(o[0:SK, b * D:(b + 1) * D], ones[0:1, 0:SK], bo0[0:1, :], start=False, stop=True)
            last.then_inc(s['prep_full'], 1)
            pe.wait_ge(s['f_pre'], 1)
            o = bank()
            mm(o[:, 0:2], ones[:], wsum, start=True, stop=True).then_inc(s['prep_full'], 1)
            pe.wait_ge(s['f_pre'], 2)
            for kc in range(KC):
                o = bank()[:].bitcast(bf16)
                for hc in range(HC):
                    last = tr(o[:, hc * P:(hc + 1) * P], w1_t[:, hc, kc * P:(kc + 1) * P], ident_b[:])
                last.then_inc(s['prep_full'], 1)
            pe.wait_ge(s['f_pre'], 3)
            for half in range(2):
                o = bank()[:].bitcast(bf16)
                for j in range(HC // 2):
                    hc = half * (HC // 2) + j
                    for oc in range(KC):
                        last = tr(o[:, (j * KC + oc) * P:(j * KC + oc + 1) * P], w2_t[:, oc, hc * P:(hc + 1) * P], ident_b[:])
                last.then_inc(s['prep_full'], 1)
            pe.wait_ge(s['ld_l1'], NLD['ld_l1'])
            o = bank()
            for kc in range(KC):
                for oc in range(KC):
                    a = (kc * KC + oc) * P
                    last = tr(o[:, a:a + P], wq_raw[:, oc, kc * P:(kc + 1) * P], ident[:])
            last.then_inc(s['prep_full'], 1)
            for kc in range(KC):
                o = bank()
                for oc in range(2 * KC):
                    last = tr(o[:, oc * P:(oc + 1) * P], wlkv_raw[:, oc, kc * P:(kc + 1) * P], ident[:])
                last.then_inc(s['prep_full'], 1)
            for a, b in ((0, P), (P, DC)):
                o = bank()
                for oc in range(2 * KC):
                    last = tr(o[0:b - a, oc * P:(oc + 1) * P], wkv_raw[:, oc, a:b], ident[:])
                last.then_inc(s['prep_full'], 1)
            for hp in range(NH // 2):
                o = bank()
                for j in range(2):
                    h = hp * 2 + j
                    for lc in range(KC):
                        last = tr(o[0:DH, (j * KC + lc) * P:(j * KC + lc + 1) * P], wo_raw[:, lc, h * DH:(h + 1) * DH], ident[:])
                last.then_inc(s['prep_full'], 1)
            o = bank()
            for kc in range(KC):
                last = tr(o[:, kc * E:(kc + 1) * E], gate_raw[:, kc * P:(kc + 1) * P], ident[0:E, 0:E])
            last.then_inc(s['prep_full'], 1)
            pe.wait_ge(s['f_pre'], 4)
            o = bank()
            for b in range(B):
                tr(o[:, b * SK:(b + 1) * SK], xn[0:SK, b, 0:P], ident[0:SK, 0:SK])
                last = tr(o[0:DCR, SKB + b * SK:SKB + (b + 1) * SK], xn[0:SK, b, P:DC], ident[0:SK, 0:SK])
            last.then_inc(s['prep_full'], 1)
            pe.wait_ge(s['prep_free'], unit[0])
            for b in range(B):
                o = bank()
                mm(o[0:SK, :], ctxT[:, 0, b * SK:(b + 1) * SK], wcT[:, 0, :], start=True, stop=False)
                mm(o[0:SK, :], ctxT[0:DCR, 1, b * SK:(b + 1) * SK], wcT[0:DCR, 1, :], start=False, stop=True)\
                    .then_inc(s['prep_full'], 1)
            pe.wait_ge(s['prep_free'], unit[0])

            G = 4
            with pe.Fori(0, B) as b:
                with pe.Fori(0, TB // G) as j:
                    it = b * (TB // G) + j
                    pe.wait_ge(s['g_xn'], it + 1)
                    for kc in range(KC):
                        for u in range(G):
                            last = tr(pb[kc][:, u * P:(u + 1) * P], xn[:, u, kc * P:(kc + 1) * P], ident[:])
                    last.then_inc(s['g_xnT_full'], 1)
                    pe.wait_ge(s['g_xnT'], it + 1)
                    for u in range(G):
                        so = pb[2][:, u * SK:(u + 1) * SK]
                        for kc in range(KC):
                            mm(so, xnT[:, kc, u * P:(u + 1) * P], m0[:, kc, bass.ds(b * SK, SK)], start=kc == 0, stop=False)
                        last = mm(so, ones[0:1, :], c0[0:1, bass.ds(b * SK, SK)], start=False, stop=True)
                    last.then_inc(s['g_sc'], 1)
                    pe.wait_ge(s['g_p'], it + 1)
                    for u in range(G):
                        last = tr(pb[3][0:SK, u * P:(u + 1) * P], p0[:, u, :], ident[:])
                    last.then_inc(s['g_pT_full'], 1)
                    pe.wait_ge(s['g_pT'], it + 1)
                    for u in range(G):
                        last = mm(pb[4 + u // 2][:, (u % 2) * D:(u % 2 + 1) * D], p0T[0:SK, u * P:(u + 1) * P],
                                  vv0[0:SK, bass.ds(b, 1), :].rearrange("p a d -> p (a d)"), start=True, stop=True)
                    last.then_inc(s['g_av'], 1)

            def ffn_in(t, u, first):
                pe.wait_ge(s['f_xq'], t + 1)
                o = pb[7][:].bitcast(bf16)
                for kc in range(KC):
                    last = tr(o[:, kc * P:(kc + 1) * P], xq[u][:, kc * P:(kc + 1) * P], ident_b[:])
                last.then_inc(s['f_xqT_full'], 1)
                pe.wait_ge(s['f_xqT'], t + 1)
                if not first:
                    pe.wait_ge(s['f_acc'], t - 1)
                for half in range(2):
                    for kc in range(KC):
                        last = mm(pb[2 * u + half][:], xqT[u][:, kc, :], w1T[:, kc, half * 512:(half + 1) * 512],
                                  start=kc == 0, stop=kc == KC - 1)
                last.then_inc(s['f_h'], 1)

            def ffn_out(t, u):
                pe.wait_ge(s['f_hq'], t + 1)
                o = pb[4 + u][:].bitcast(bf16)
                for hc in range(HC):
                    last = tr(o[:, hc * P:(hc + 1) * P], h_q[u][:, hc * P:(hc + 1) * P], ident_b[:])
                last.then_inc(s['f_hqT_full'], 1)
                pe.wait_ge(s['f_hqT'], t + 1)
                pe.wait_ge(s['f_yout'], t)
                for hc in range(HC):
                    last = mm(pb[6][:, 0:D], h_qT[u][:, hc, :], w2T[:, hc, :], start=hc == 0, stop=hc == HC - 1)
                last.then_inc(s['f_y'], 1)

            ffn_in(0, 0, True)
            ffn_in(1, 1, True)
            ffn_out(0, 0)
            with pe.Fori(0, (T - 2) // 2) as i:
                for u in range(2):
                    ffn_in(i * 2 + (2 + u), u, False)
                    ffn_out(i * 2 + (1 + u), 1 - u)
            ffn_out(T - 1, 1)

            def proj_in(t, u):
                pe.wait_ge(s['l_xh'], t + 1)
                pe.wait_ge(s['l_xT'], t)
                for kc in range(KC):
                    last = tr(pb[0][:, kc * P:(kc + 1) * P], xn[:, u, kc * P:(kc + 1) * P], ident[:])
                last.then_inc(s['l_xT_full'], 1)

            def proj(t, u, first):
                pe.wait_ge(s['l_xT'], t + 1)
                if not first:
                    pe.wait_ge(s['l_qk'], t - 1)
                    pe.wait_ge(s['l_v'], t - 1)
                for o, a, n in ((pb[1 + 2 * u], 0, 2 * D), (pb[2 + 2 * u], 2 * D, D)):
                    for kc in range(KC):
                        last = mm(o[:, 0:n], xnT[:, kc, u * P:(u + 1) * P], wT[:, kc, a:a + n], start=kc == 0, stop=kc == KC - 1)
                last.then_inc(s['l_qkv'], 1)

            proj_in(0, 0)
            proj_in(1, 1)
            proj(0, 0, True)
            proj_in(2, 0)
            proj(1, 1, True)
            with pe.Fori(0, (T - 4) // 2) as i:
                for u in range(2):
                    proj_in(i * 2 + (3 + u), 1 - u)
                    proj(i * 2 + (2 + u), u, False)
            proj_in(T - 1, 1)
            proj(T - 2, 0, False)
            proj(T - 1, 1, False)

            USES = 15
            TP = pb[7]
            KTILES = [(c * P, P) for c in range(TB)] + [(S, SK)]

            with pe.Fori(0, B) as b:
                with pe.Fori(0, NH // 2) as hp:
                    it = b * (NH // 2) + hp
                    for u in range(2):
                        n = it * 2 + u
                        use = [0]

                        def claim():
                            pe.wait_ge(s['t_free'], n * USES + use[0])
                            use[0] += 1

                        pe.wait_ge(s['a_qk'], n + 1)
                        for half in range(2):
                            claim()
                            for j in range(4):
                                last = mm(TP[0:DH, j * P:(j + 1) * P], qs[u][:, half * 4 + j, :], ident[:], start=True, stop=True)
                            last.then_inc(s['t_full'], 1)
                        for half in range(2):
                            claim()
                            for j in range(4):
                                last = mm(TP[0:DH, j * P:(j + 1) * P], ks[u][:, half * 4 + j, :], ident[:], start=True, stop=True)
                            last.then_inc(s['t_full'], 1)
                        claim()
                        mm(TP[0:DH, 0:SK], ks[u][0:SK, TB, :], ident[0:SK, 0:SK], start=True, stop=True).then_inc(s['t_full'], 1)
                        pe.wait_ge(s['t_free'], n * USES + 5)
                        for t in range(TB):
                            for k, (a, w) in enumerate(((0, 512), (512, 512), (S, SK))):
                                if t == 0:
                                    pe.wait_ge(s['a_mx_free'], n * (3 * TB))
                                else:
                                    pe.wait_ge(s['a_mx_free'], n * (3 * TB) + (3 * t - 2 + k))
                                mm(pb[k][:, 0:w], QT[u][0:DH, t * P:(t + 1) * P], KT[u][0:DH, a:a + w], start=True, stop=True)\
                                    .then_inc(s['a_mx_full'], 1)
                        pe.wait_ge(s['a_negm'], n + 1)
                        for half in range(2):
                            claim()
                            for j in range(4):
                                t = half * 4 + j
                                last = mm(TP[DH:DA, j * P:(j + 1) * P], negm[:, t:t + 1], ident[:], start=True, stop=True)
                            last.then_inc(s['t_full'], 1)
                        pe.wait_ge(s['t_free'], n * USES + 7)
                        pe.wait_ge(s['a_v'], n + 1)
                        NU = 2 * len(KTILES)

                        def scores(q):
                            c, half = divmod(q, 2)
                            a, w = KTILES[c]
                            if q >= 2:
                                pe.wait_ge(s['a_p'], n * NU + (q - 1))
                            mm(pb[3 + q % 2][0:w, :], KT[u][0:DA, a:a + w], QT[u][0:DA, half * 512:(half + 1) * 512],
                               start=True, stop=True).then_inc(s['a_s_full'], 1)

                        def values(q):
                            c, half = divmod(q, 2)
                            a, w = KTILES[c]
                            pe.wait_ge(s['a_p'], n * NU + (q + 1))
                            mm(pb[5 + half][0:DA, :], vh[u][0:w, c, :], pT[q % 3][0:w, :], start=c == 0,
                               stop=c == len(KTILES) - 1).then_inc(s['a_pv'], 1)

                        scores(0)
                        for q in range(NU):
                            if q + 1 < NU:
                                scores(q + 1)
                            if q == 0:
                                pe.wait_ge(s['a_o'], n)
                            values(q)
                        pe.wait_ge(s['a_o'], n + 1)
                        for t in range(TB):
                            claim()
                            mm(TP[:, 0:D + 1], oT[u][0:DA, t * P:(t + 1) * P],
                               woT[0:DA, bass.ds(hp * 2 + u, 1), :].rearrange("p a d -> p (a d)"), start=True, stop=True)\
                                .then_inc(s['t_full'], 1)
                        assert use[0] == USES

            with pe.Fori(0, T // 2) as i:
                for u in range(2):
                    t = i * 2 + u
                    pe.wait_ge(s['r_x'], t + 1)
                    for kc in range(KC):
                        last = tr(pb[u][:, kc * P:(kc + 1) * P], xn[:, u, kc * P:(kc + 1) * P], ident[:])
                    last.then_inc(s['r_xT_full'], 1)
                    pe.wait_ge(s['r_xT'], t + 1)
                    for kc in range(KC):
                        last = mm(pb[2][:, bass.ds(t * E, E)], xnT[:, kc, u * P:(u + 1) * P], gateT[:, kc, :],
                                  start=kc == 0, stop=kc == KC - 1)
                    last.then_inc(s['r_logit'], 1)
            pe.wait_ge(s['r_sel'], 1)
            flat = lambda v: v.rearrange("p a b -> p (a b)")
            mm(pb[0][:, 0:T * E], before[:], flat(sel_b), start=True, stop=False)
            mm(pb[0][:, 0:T * E], ones_b[:], flat(cum_b), start=False, stop=True)
            mm(pb[1][:, 0:E], ones_b[:], inc_b[:, T - 1, :], start=True, stop=True).then_inc(s['r_pos'], 1)

            def mixture(k, n, where, hot_of):
                def bring(t, u, turn):
                    pe.wait_ge(m_x[k][u], turn * 16 + 16)
                    pe.wait_ge(m[k]['xinT'], t)
                    for kc in range(KC):
                        last = tr(pb[4][:, kc * P:(kc + 1) * P], x_in[u][:, kc * P:(kc + 1) * P], ident[:])
                    last.then_inc(m[k]['xinT_full'], 1)

                def product(t, u, side, at):
                    for j, off in enumerate((OFF1, OFF3)):
                        o = pb[2 * side + j]
                        for kc in range(KC):
                            mm(o[:], x_inT[u][:, kc, :], halves(at, off, kc)[:, :, side], start=kc == 0, stop=False)
                        bb = bias_b[:, j * I2:(j + 1) * I2].rearrange("p (n two) -> p n two", two=2)
                        last = mm(o[:], hot_of(u), bb[:, :, side], start=False, stop=True)
                    last.then_inc(m[k]['prod'], 1)

                def hidden_T(t):
                    pe.wait_ge(m[k]['hid'], t + 1)
                    for c in range(IC):
                        last = tr(pb[5][:, c * P:(c + 1) * P], h_moe[:, c * P:(c + 1) * P], ident[:])
                    last.then_inc(m[k]['hT_full'], 1)

                def second(t, u, at):
                    pe.wait_ge(m[k]['hT'], t + 1)
                    pe.wait_ge(m[k]['ysb'], t)
                    for c in range(IC):
                        mm(pb[6][:, 0:D], h_moeT[:, c, :], wexp[:, bass.ds(at + (OFF2 + c * D), D)], start=c == 0, stop=False)
                    mm(pb[6][:, 0:D], hot_of(u), bias_b[:, 2 * I2:NB], start=False, stop=True).then_inc(m[k]['y'], 1)

                def step(t, u, turn, first, more):
                    at = where(t)
                    at_before = None if first else where(t, True)
                    pe.wait_ge(m[k]['xinT'], t + 1)
                    if k == 1:
                        pe.wait_ge(m[k]['hot'], t + 1)
                    pe.wait_ge(m[k]['gated'], t)
                    product(t, u, 0, at)
                    if not first:
                        hidden_T(t - 1)
                    pe.wait_ge(m[k]['lined'], t)
                    product(t, u, 1, at)
                    if not first:
                        second(t - 1, 1 - u, at_before)
                    if more:
                        bring(t + 1, 1 - u, turn)

                bring(0, 0, 0)
                step(0, 0, 0, True, True)
                pairs = (n - 2) // 2
                with pe.Fori(0, pairs) as i:
                    for u in range(2):
                        step(i * 2 + (1 + u), 1 - u, i + 1 if u == 0 else i + 1, False, True)
                for t in range(2 * pairs + 1, n):
                    step(t, t % 2, (t + 1) // 2, False, t + 1 < n)
                hidden_T(n - 1)
                second(n - 1, (n - 1) % 2, where(n - 1))

            pe.wait_ge(s['ld_shared'], NLD['ld_shared'])
            pe.wait_ge(s['r_hot'], 3)
            mixture(0, T, lambda t, before=False: SHARED_AT * WEXP, lambda u: hot_sh[:])
            pe.wait_ge(s['ld_e0'], NLD['ld_e0'])
            pe.wait_ge(s['ld_mid'], NLD['ld_mid'])
            pe.wait_ge(s['ld_last'], NLD['ld_last'])

            def slot_at(t, before=False):
                t = t - 1 if before else t
                return pe.value_load(slot_i[0:1, bass.ds(t, 1)], min_val=0, max_val=E - 1) * WEXP

            mixture(1, SLOTS, slot_at, lambda u: hot_t[u][0:96, :])

        @block.scalar
        def _(act):
            a = nc.scalar.activation
            roots = [0]

            def root(n):
                act.wait_ge(s['root_in'], roots[0] + 1)
                a(root_s[:, 0:n], root_a[:, 0:n], ACT.Sqrt).then_inc(s['root_out'], 1)
                roots[0] += 1

            root(T + B)
            with act.Fori(0, T // 4) as it:
                act.wait_ge(s['g_xnT_full'], it + 1)
                a(xnT[:, 0, :], pb[0][:], ACT.Copy)
                a(xnT[:, 1, :], pb[1][:], ACT.Copy).then_inc(s['g_xnT'], 1)
                act.wait_ge(s['g_sh'], it + 1)
                a(p0[:].rearrange("p a b -> p (a b)"), p0[:].rearrange("p a b -> p (a b)"), ACT.Exp, scale=SCALE0)\
                    .then_inc(s['g_p'], 1)
            root(T)

            def ffn_T(t, u):
                act.wait_ge(s['f_xqT_full'], t + 1)
                a(xqT[u][:].rearrange("p a b -> p (a b)"), pb[7][:].bitcast(bf16)[:, 0:D], ACT.Copy).then_inc(s['f_xqT'], 1)

            def ffn_act(t, u):
                act.wait_ge(s['f_acc'], t + 1)
                a(h_f[u], h_f[u], ACT.Gelu).then_inc(s['f_amax'], 1)

            def ffn_quant(t, u):
                act.wait_ge(s['f_hqT_full'], t + 1)
                a(h_qT[u][:].rearrange("p a b -> p (a b)"), pb[4 + u][:].bitcast(bf16), ACT.Copy).then_inc(s['f_hqT'], 1)

            ffn_T(0, 0)
            with act.Fori(0, (T - 2) // 2) as i:
                for u in range(2):
                    ffn_act(i * 2 + u, u)
                    ffn_T(i * 2 + (1 + u), 1 - u)
                    ffn_quant(i * 2 + u, u)
            ffn_act(T - 2, 0)
            ffn_T(T - 1, 1)
            ffn_quant(T - 2, 0)
            ffn_act(T - 1, 1)
            ffn_quant(T - 1, 1)
            root(T)
            root(T)

            def proj_T(t, u, first):
                act.wait_ge(s['l_xT_full'], t + 1)
                if not first:
                    act.wait_ge(s['l_qkv'], t - 1)
                for kc in range(KC):
                    last = a(xnT[:, kc, u * P:(u + 1) * P], pb[0][:, kc * P:(kc + 1) * P], ACT.Identity,
                             scale=lg[:, kc:kc + 1], bias=lb[:, kc:kc + 1])
                last.then_inc(s['l_xT'], 1)

            def proj_qk(t, u):
                act.wait_ge(s['l_qkv'], t + 1)
                act.wait_ge(s['const'], 2)
                a(qkv[:, bass.ds(t, 1), 0:2 * D].rearrange("p a d -> p (a d)"), pb[1 + 2 * u][:], ACT.Copy)\
                    .then_inc(s['l_qk'], 1)

            proj_T(0, 0, True)
            proj_T(1, 1, True)
            with act.Fori(0, (T - 2) // 2) as i:
                for u in range(2):
                    proj_qk(i * 2 + u, u)
                    proj_T(i * 2 + (2 + u), u, False)
            proj_qk(T - 2, 0)
            proj_qk(T - 1, 1)
            root(T * 2 * NH + 2 * NH)

            USES, NU = 15, 2 * (TB + 1)
            with act.Fori(0, B) as b:
                with act.Fori(0, NH // 2) as hp:
                    it = b * (NH // 2) + hp
                    for u in range(2):
                        n = it * 2 + u
                        dsts = [(QT[u][0:DH, 0:512], qg), (QT[u][0:DH, 512:S], qg), (KT[u][0:DH, 0:512], kg),
                                (KT[u][0:DH, 512:S], kg), (KT[u][0:DH, S:S + SK], kg)]
                        for k, (dst, gam) in enumerate(dsts):
                            act.wait_ge(s['t_full'], n * USES + (k + 1))
                            a(dst, pb[7][0:DH, 0:dst.shape[-1]], ACT.Copy, scale=gam[0:DH, :]).then_inc(s['t_free'], 1)
                        for half in range(2):
                            act.wait_ge(s['t_full'], n * USES + (6 + half))
                            a(QT[u][DH:DA, half * 512:(half + 1) * 512], pb[7][DH:DA, :], ACT.Copy).then_inc(s['t_free'], 1)
                        for q in range(NU):
                            act.wait_ge(s['a_s_full'], n * NU + (q + 1))
                            if q >= 3:
                                act.wait_ge(s['a_pv'], n * NU + (q - 2))
                            else:
                                act.wait_ge(s['a_pv'], n * NU)
                            if q < 2 * TB:
                                a(pT[q % 3], pb[3 + q % 2][:], ACT.Exp).then_inc(s['a_p'], 1)
                            else:
                                a(pT[q % 3][0:SK, :], pb[3 + q % 2][0:SK, :], ACT.Exp, bias=mask_now[:])\
                                    .then_inc(s['a_p'], 1)
                        act.wait_ge(s['a_pv'], n * NU + NU)
                        a(oT[u][0:DA, 0:512], pb[5][0:DA, :], ACT.Copy)
                        a(oT[u][0:DA, 512:S], pb[6][0:DA, :], ACT.Copy).then_inc(s['a_o'], 1)

            root(T)
            with act.Fori(0, T // 2) as i:
                for u in range(2):
                    t = i * 2 + u
                    act.wait_ge(s['r_xT_full'], t + 1)
                    for kc in range(KC):
                        last = a(xnT[:, kc, u * P:(u + 1) * P], pb[u][:, kc * P:(kc + 1) * P], ACT.Copy)
                    last.then_inc(s['r_xT'], 1)
            act.wait_ge(s['r_e'], 1)
            a(score[:], score[:], ACT.Exp).then_inc(s['r_exp'], 1)

            def mixture(k, n):
                def tokens(t, u):
                    act.wait_ge(m[k]['xinT_full'], t + 1)
                    a(x_inT[u][:].rearrange("p a b -> p (a b)"), pb[4][:, 0:D], ACT.Copy).then_inc(m[k]['xinT'], 1)

                def lifted(t, side):
                    act.wait_ge(m[k]['prod'], t * 2 + (1 + side))
                    act.wait_ge(m[k]['lined' if side else 'gated'], t)
                    a(lift[side], pb[2 * side + 1][:], ACT.Copy).then_inc(m[k]['lifted'], 1)

                def hidden(t):
                    act.wait_ge(m[k]['hT_full'], t + 1)
                    a(h_moeT[:].rearrange("p a b -> p (a b)"), pb[5][:], ACT.Copy).then_inc(m[k]['hT'], 1)

                def result(t, u, turn):
                    act.wait_ge(m_st[k][u], turn * 16)
                    act.wait_ge(m[k]['y'], t + 1)
                    a(y_sb[u], pb[6][:, 0:D], ACT.Copy).then_inc(m[k]['ysb'], 1)

                def step(t, u, turn, first, more):
                    lifted(t, 0)
                    if not first:
                        hidden(t - 1)
                    act.wait_ge(m[k]['gated'], t + 1)
                    a(sig, gate, ACT.Sigmoid, scale=ALPHA).then_inc(m[k]['sigd'], 1)
                    lifted(t, 1)
                    if not first:
                        result(t - 1, 1 - u, turn)
                    if more:
                        tokens(t + 1, 1 - u)

                tokens(0, 0)
                step(0, 0, 0, True, True)
                pairs = (n - 2) // 2
                with act.Fori(0, pairs) as i:
                    for u in range(2):
                        step(i * 2 + (1 + u), 1 - u, i, False, True)
                for t in range(2 * pairs + 1, n):
                    step(t, t % 2, (t - 1) // 2, False, t + 1 < n)
                hidden(n - 1)
                result(n - 1, (n - 1) % 2, (n - 1) // 2)

            mixture(0, T)
            mixture(1, SLOTS)

        @block.vector
        def _(ve):
            v = nc.vector
            link = Chain(ve, s['chain'])
            roots = [0]
            units = [0]

            def norm(n, guard):
                ve.wait_ge(s['root_out'], roots[0] + 1)
                roots[0] += 1
                r, q, t_, d = root_a[:, 0:n], root_s[:, 0:n], root_t[:, 0:n], rstd[:, 0:n]
                link(v.tensor_scalar(t_, q, 1e-30, None, ALU.max))
                link(v.reciprocal(d, t_))
                link(v.tensor_tensor(t_, r, d, ALU.mult))
                link(v.tensor_tensor(t_, t_, q, ALU.add))
                link(v.tensor_scalar(t_, t_, 0.5, guard, ALU.mult, ALU.max))
                link(v.reciprocal(d, t_))

            def filled():
                units[0] += 1
                ve.wait_ge(s['prep_full'], units[0])
                return pb[(units[0] - 1) % 2]

            ve.wait_ge(s['const'], 2)
            ve.wait_ge(s['ld_x'], NLD['ld_x'])
            with ve.Fori(0, T) as t:
                last = v.bn_stats(stats[:, bass.ds(t, 1), :].rearrange("p a d -> p (a d)"),
                                  x_sb[:, bass.ds(t, 1), :].rearrange("p a d -> p (a d)"))
                link.loop(t, 1)
                link(last)
            link.done(T)

            def aggregate():
                for t in range(T):
                    last = v.bn_aggr(mv[:, t, :], stats[:, t, :])
                link(last)

            aggregate()
            ve.wait_ge(s['ld_l0'], NLD['ld_l0'])
            for b in range(B):
                link(v.bn_stats(root_t[0:SK, 8 * b:8 * b + 6], ctx_sb[0:SK, b, :]))
                link(v.bn_aggr(mv[0:SK, T + b, :], root_t[0:SK, 8 * b:8 * b + 6]))
            v.tensor_scalar(root_a[:, 0:T + B], mv[:, :, 1], LN_EPS, None, ALU.add).then_inc(s['root_in'], 1)
            norm(T + B, 0.0)
            for b in range(B):
                last = v.tensor_scalar(xn[0:SK, b, 0:DC], ctx_sb[0:SK, b, :], mv[0:SK, T + b, 0:1], rstd[0:SK, T + b:T + b + 1],
                                       ALU.subtract, ALU.mult)
            link(last)
            free = lambda ins: ins.then_inc(s['prep_free'], 1)
            flat = lambda ap: ap.rearrange("p a b -> p (a b)")
            o = filled()
            free(v.tensor_copy(flat(l0_wqT[:]), o[:]))
            o = filled()
            v.tensor_copy(ctxT[:, 0, :], o[:, 0:SKB])
            free(v.tensor_copy(ctxT[0:DCR, 1, :], o[0:DCR, SKB:2 * SKB]))
            for dst, bias in ((kT0, bk0), (vT0, bv0)):
                o = filled()
                for ec in range(KC):
                    last = v.tensor_scalar(dst[:, ec, :], o[:, ec * SKB:(ec + 1) * SKB], bias[:, ec:ec + 1], None, ALU.add)
                free(last)
            o = filled()
            v.tensor_copy(flat(m0[:]), o[:, 0:KC * SKB])
            free(v.tensor_copy(c0[0:1, :], o[0:1, KC * SKB:(KC + 1) * SKB]))
            o = filled()
            free(v.tensor_copy(vv0[0:SK].rearrange("p a b -> p (a b)"), o[0:SK, 0:B * D]))
            ve.wait_ge(s['ld_ffn'], NLD['ld_ffn'])
            v.tensor_reduce(wsum[:, 0:1], w1_raw[:], AX.XY, ALU.add, apply_absolute_value=True)
            v.tensor_reduce(wsum[:, 1:2], w2_raw[:], AX.XY, ALU.add, apply_absolute_value=True).then_inc(s['f_pre'], 1)
            o = filled()
            v.tensor_scalar(wsc, o[:, 0:2], 1.0 / (HID * D), QEPS, ALU.mult, ALU.max).then_inc(s['prep_free'], 1)
            ve.wait_ge(s['prep_free'], units[0])
            link(v.reciprocal(winv, wsc))
            for k, (raw, q) in enumerate(((w1_raw, w1_t), (w2_raw, w2_t))):
                link(v.tensor_scalar(raw[:], raw[:], winv[:, k:k + 1], MAGIC, ALU.mult, ALU.add))
                link(v.tensor_scalar(raw[:], raw[:], MAGIC, 1.0, ALU.subtract, ALU.min))
                v.tensor_scalar(q, raw[:], -1.0, None, ALU.max).then_inc(s['f_pre'], 1)
            for kc in range(KC):
                o = filled()
                free(v.tensor_copy(w1T[:, kc, :], o[:].bitcast(bf16)))
            for half in range(2):
                o = filled()
                n = HC // 2
                free(v.tensor_copy(flat(w2T[:, half * n:(half + 1) * n, :]), o[:].bitcast(bf16)))
            o = filled()
            free(v.tensor_copy(wT[:, :, 0:D], o[:].rearrange("p (a b) -> p a b", a=KC)))
            for kc in range(KC):
                o = filled()
                free(v.tensor_copy(wT[:, kc, D:QKV], o[:]))
            for kc, n in ((0, P), (1, DCR)):
                o = filled()
                free(v.tensor_copy(wcT[0:n, kc, :], o[0:n, :]))
            for hp in range(NH // 2):
                o = filled()
                free(v.tensor_copy(woT[0:DH, 2 * hp:2 * hp + 2, 0:D], o[0:DH, :].rearrange("p (a b) -> p a b", a=2)))
            o = filled()
            free(v.tensor_copy(flat(gateT[:]), o[:, 0:KC * E]))
            v.tensor_scalar(flat(mask_row[:]), mask_u, BIG, -BIG, ALU.mult, ALU.add)
            v.tensor_scalar(mask_col[:], maskc_u[:], BIG, -BIG, ALU.mult, ALU.add).then_inc(s['f_pre'], 1)
            o = filled()
            v.tensor_scalar(ctxT[:, 0, :], o[:, 0:SKB], xg[:, 0:1], xb[:, 0:1], ALU.mult, ALU.add)
            free(v.tensor_scalar(ctxT[0:DCR, 1, :], o[0:DCR, SKB:2 * SKB], xg[0:DCR, 1:2], xb[0:DCR, 1:2], ALU.mult, ALU.add))
            for b in range(B):
                o = filled()
                free(v.tensor_copy(ckv[0:SK, b, :], o[0:SK, :]))
            ve.wait_ge(s['prep_free'], units[0])

            def tile(t):
                return x_sb[:, bass.ds(t, 1), :].rearrange("p a d -> p (a d)")

            def col(ap, t):
                return ap[:, bass.ds(t, 1)]

            def statistics(t):
                return v.bn_stats(stats[:, bass.ds(t, 1), :].rearrange("p a d -> p (a d)"), tile(t))

            def normalise(dst, t):
                return v.tensor_scalar(dst, tile(t), mv[:, bass.ds(t, 1), 0:1].rearrange("p a d -> p (a d)"), col(rstd, t),
                                       ALU.subtract, ALU.mult)

            with ve.Fori(0, T // 4) as it:
                link.loop(it, 5)
                for u in range(4):
                    last = normalise(xn[:, u, :], it * 4 + u)
                last.then_inc(s['g_xn'], 1)
                ve.wait_ge(s['g_sc'], it + 1)
                sc = pb[2][:, 0:4 * SK].rearrange("p (a b) -> p a b", a=4)
                link(v.tensor_reduce(mx4, sc, AX.X, ALU.max))
                v.tensor_tensor(p0[:], sc, mx4.unsqueeze(2).to_broadcast([P, 4, SK]), ALU.subtract).then_inc(s['g_sh'], 1)
                ve.wait_ge(s['g_p'], it + 1)
                link(v.tensor_reduce(sums4, p0[:], AX.X, ALU.add))
                link(v.reciprocal(sums4, sums4))
                ve.wait_ge(s['g_pT_full'], it + 1)
                v.tensor_copy(p0T[0:SK, :], pb[3][0:SK, :]).then_inc(s['g_pT'], 1)
                ve.wait_ge(s['g_av'], it + 1)
                for u in range(4):
                    last = v.scalar_tensor_tensor(tile(it * 4 + u), pb[4 + u // 2][:, (u % 2) * D:(u % 2 + 1) * D],
                                                  sums4[:, u:u + 1], tile(it * 4 + u), ALU.mult, ALU.add)
                link(last)
                for u in range(4):
                    last = statistics(it * 4 + u)
                link(last)
            link.done(T // 4)
            aggregate()
            v.tensor_scalar(root_a[:, 0:T], mv[:, 0:T, 1], LN_EPS, None, ALU.add).then_inc(s['root_in'], 1)
            norm(T, 0.0)

            def ffn_quantise(t, u):
                link(normalise(xn[:, u, :], t))
                link(v.tensor_reduce(amax[:, u:u + 1], xn[:, u, :], AX.X, ALU.max, apply_absolute_value=True))
                link(v.tensor_scalar(aden[:, u:u + 1], amax[:, u:u + 1], QEPS, None, ALU.max))
                link(v.reciprocal(arow[:, u:u + 1], aden[:, u:u + 1]))
                link(v.tensor_scalar(arow[:, u:u + 1], arow[:, u:u + 1], QB, None, ALU.mult))
                link(v.tensor_scalar(xn[:, u, :], xn[:, u, :], arow[:, u:u + 1], MAGIC, ALU.mult, ALU.add))
                v.tensor_scalar(aden[:, u:u + 1], aden[:, u:u + 1], wsc[:, 0:1], 1.0 / QB, ALU.mult, ALU.mult)
                v.tensor_scalar(xq[u][:], xn[:, u, :], MAGIC, QB, ALU.subtract, ALU.min).then_inc(s['f_xq'], 1)

            def ffn_hidden(t, u):
                ve.wait_ge(s['f_h'], t + 1)
                for half in range(2):
                    c = slice(half * 512, (half + 1) * 512)
                    last = v.scalar_tensor_tensor(h_f[u][:, c], pb[2 * u + half][:], aden[:, u:u + 1], b1_all[:, c], ALU.mult, ALU.add)
                last.then_inc(s['f_acc'], 1)

            def ffn_requantise(t, u):
                ve.wait_ge(s['f_amax'], t + 1)
                link(v.tensor_reduce(hmax[:, u:u + 1], h_f[u], AX.X, ALU.max, apply_absolute_value=True))
                link(v.tensor_scalar(hden[:, u:u + 1], hmax[:, u:u + 1], QEPS, None, ALU.max))
                link(v.reciprocal(hrow[:, u:u + 1], hden[:, u:u + 1]))
                link(v.tensor_scalar(hrow[:, u:u + 1], hrow[:, u:u + 1], QB, None, ALU.mult))
                link(v.tensor_scalar(h_f[u], h_f[u], hrow[:, u:u + 1], MAGIC, ALU.mult, ALU.add))
                v.tensor_scalar(hden[:, u:u + 1], hden[:, u:u + 1], wsc[:, 1:2], 1.0 / QB, ALU.mult, ALU.mult)
                v.tensor_scalar(h_q[u], h_f[u], MAGIC, QB, ALU.subtract, ALU.min).then_inc(s['f_hq'], 1)

            def ffn_finish(t, u):
                ve.wait_ge(s['f_y'], t + 1)
                ve.wait_ge(s['f_b2'], t + 1)
                v.scalar_tensor_tensor(tile(t), pb[6][:, 0:D], hden[:, u:u + 1], tile(t), ALU.mult, ALU.add)\
                    .then_inc(s['f_yout'], 1)
                ve.wait_ge(s['f_yout'], t + 1)
                link(statistics(t))

            ffn_quantise(0, 0)
            ffn_quantise(1, 1)
            ffn_hidden(0, 0)
            ffn_requantise(0, 0)
            with ve.Fori(0, (T - 2) // 2) as i:
                link.loop(i, 24)
                for u in range(2):
                    ffn_quantise(i * 2 + (2 + u), u)
                    ffn_hidden(i * 2 + (1 + u), 1 - u)
                    ffn_finish(i * 2 + u, u)
                    ffn_requantise(i * 2 + (1 + u), 1 - u)
            link.done((T - 2) // 2)
            ffn_hidden(T - 1, 1)
            ffn_finish(T - 2, 0)
            ffn_requantise(T - 1, 1)
            ffn_finish(T - 1, 1)
            aggregate()

            link(v.tensor_scalar(root_a[:, 0:T], mv[:, 0:T, 1], LN_EPS, None, ALU.add))
            v.tensor_copy(root_t[:, 0:1], root_a[:, 0:1]).then_inc(s['root_in'], 1)
            norm(T, 0.0)
            r1 = stats.rearrange("p a b -> p (a b)")[:, 0:T]
            link(v.tensor_copy(r1, rstd[:, 0:T]))
            link(v.tensor_tensor(root_t[:, 0:T], r1, r1, ALU.mult))
            link(v.tensor_tensor(root_t[:, 0:T], root_t[:, 0:T], mv[:, 0:T, 1], ALU.mult))
            v.tensor_scalar(root_a[:, 0:T], root_t[:, 0:T], LN_EPS, None, ALU.add).then_inc(s['root_in'], 1)
            norm(T, 0.0)
            link(v.tensor_tensor(rstd[:, 0:T], rstd[:, 0:T], r1, ALU.mult))
            sq = [oT[0][:, 0:512], oT[1][:, 0:512]]

            def proj_tokens(t, u):
                normalise(xn[:, u, :], t).then_inc(s['l_xh'], 1)

            def proj_kept(t, u):
                ve.wait_ge(s['l_qkv'], t + 1)
                v.tensor_copy(qkv[:, bass.ds(t, 1), 2 * D:QKV].rearrange("p a d -> p (a d)"), pb[2 + 2 * u][:, 0:D]).then_inc(s['l_v'], 1)
                ve.wait_ge(s['l_qk'], t + 1)
                qk = qkv[:, bass.ds(t, 1), 0:2 * D].rearrange("p a d -> p (a d)")
                link(v.tensor_tensor(sq[u], qk, qk, ALU.mult))
                v.tensor_reduce(ss_l[:, bass.ds(t * (2 * NH), 2 * NH)], sq[u].rearrange("p (a b) -> p a b", a=2 * NH), AX.X, ALU.add)

            ss_l = p0[:].rearrange("p a b -> p (a b)")
            NSS = T * 2 * NH + 2 * NH
            link(v.memset(ss_l[:, 0:NSS], 1.0))
            ve.wait_ge(s['prep_free'], units[0])
            for b in range(B):
                link(v.tensor_tensor(sq[b][0:SK, 0:D], ckv[0:SK, b, 0:D], ckv[0:SK, b, 0:D], ALU.mult))
                v.tensor_reduce(ss_l[0:SK, T * 2 * NH + b * NH:T * 2 * NH + (b + 1) * NH],
                                sq[b][0:SK, 0:D].rearrange("p (a b) -> p a b", a=NH), AX.X, ALU.add)
            proj_tokens(0, 0)
            proj_tokens(1, 1)
            with ve.Fori(0, (T - 2) // 2) as i:
                link.loop(i, 2)
                for u in range(2):
                    ve.wait_ge(s['l_xT'], i * 2 + (u + 1))
                    proj_tokens(i * 2 + (2 + u), u)
                    proj_kept(i * 2 + u, u)
            link.done((T - 2) // 2)
            proj_kept(T - 2, 0)
            proj_kept(T - 1, 1)
            link(v.tensor_copy(mx4[:, 0:1], hden[:, 0:1]))
            v.tensor_scalar(root_a[:, 0:NSS], ss_l[:, 0:NSS], 1.0 / DH, None, ALU.mult).then_inc(s['root_in'], 1)
            norm(NSS, RMS_EPS)
            rq = rstd[:, 0:T * 2 * NH].rearrange("p (a b) -> p a b", a=T)
            link(v.tensor_scalar(rq[:, :, 0:NH], rq[:, :, 0:NH], float(DH) ** -0.5, None, ALU.mult))

            USES = 15
            ve.wait_ge(s['l_bo'], T)
            with ve.Fori(0, B) as b:
                with ve.Fori(0, NH // 2) as hp:
                    it = b * (NH // 2) + hp
                    link.loop(it, 2 * (TB + 1 + TB))
                    for u in range(2):
                        n = it * 2 + u
                        h = hp * 2 + u
                        for dst, a0, r0 in ((qs[u][:], 0, 0), (ks[u][:, 0:TB, :], D, NH)):
                            src = qkv[:, bass.ds(b * TB, TB), bass.ds(hp * (2 * DH) + (a0 + u * DH), DH)]
                            r = rq[:, bass.ds(b * TB, TB), bass.ds(hp * 2 + (r0 + u), 1)]
                            v.tensor_tensor(dst, src, r.to_broadcast([P, TB, DH]), ALU.mult)
                        v.tensor_copy(mask_now[:], mask_col[:, bass.ds(b, 1)])
                        rc = rstd[0:SK, bass.ds(b * NH + hp * 2 + (T * 2 * NH + u), 1)]
                        csrc = ckv[0:SK, bass.ds(b, 1), bass.ds(hp * (2 * DH) + u * DH, DH)].rearrange("p a d -> p (a d)")
                        v.tensor_scalar(ks[u][0:SK, TB, :], csrc, rc, None, ALU.mult).then_inc(s['a_qk'], 1)
                        for t in range(TB):
                            for k in range(2):
                                ve.wait_ge(s['a_mx_full'], n * (3 * TB) + (3 * t + k + 1))
                                v.tensor_reduce(mx3[:, t, k:k + 1], pb[k][:], AX.X, ALU.max).then_inc(s['a_mx_free'], 1)
                            ve.wait_ge(s['a_mx_full'], n * (3 * TB) + (3 * t + 3))
                            v.tensor_tensor(cmask, pb[2][:, 0:SK], mask_row[:, bass.ds(b, 1), :].rearrange("p a d -> p (a d)"), ALU.add)\
                                .then_inc(s['a_mx_free'], 1)
                            ve.wait_ge(s['a_mx_free'], n * (3 * TB) + (3 * t + 3))
                            link(v.tensor_reduce(mx3[:, t, 2:3], cmask, AX.X, ALU.max))
                        v.tensor_reduce(negm, mx3[:], AX.X, ALU.max, negate=True).then_inc(s['a_negm'], 1)
                        for t in range(TB):
                            ve.wait_ge(s['t_full'], n * USES + (8 + t))
                            link(v.reciprocal(yden[:, 0:1], pb[7][:, D:D + 1]))
                            row_t = b * TB + t
                            v.scalar_tensor_tensor(tile(row_t), pb[7][:, 0:D], yden[:, 0:1], tile(row_t), ALU.mult, ALU.add)\
                                .then_inc(s['t_free'], 1)
                        ve.wait_ge(s['t_free'], n * USES + USES)
                        link(v.tensor_copy(yden[:, 1:2], yden[:, 0:1]))
            link.done(B * NH // 2)
            v.tensor_copy(mx4[:, 0:1], yden[:, 0:1]).then_inc(s['a_oT'], 1)

            ve.wait_ge(s['a_oT'], 1)
            with ve.Fori(0, T) as t:
                link.loop(t, 1)
                link(statistics(t))
            link.done(T)
            aggregate()
            v.tensor_scalar(root_a[:, 0:T], mv[:, 0:T, 1], LN_EPS, None, ALU.add).then_inc(s['root_in'], 1)
            norm(T, 0.0)
            ve.wait_ge(s['zero'], 16 * SLOTS)
            with ve.Fori(0, T) as t:
                normalise(xm[:, bass.ds(t, 1), :].rearrange("p a d -> p (a d)"), t).then_inc(s['r_norm'], 1)

            ve.wait_ge(s['r_logit'], T)
            lg3 = pb[2][:, 0:T * E].rearrange("p (a b) -> p a b", a=T)
            wide = lambda ap: ap.unsqueeze(2).to_broadcast([P, T, E])
            link(v.tensor_reduce(den16, lg3, AX.X, ALU.max))
            v.tensor_tensor(score[:], lg3, wide(den16), ALU.subtract).then_inc(s['r_e'], 1)
            ve.wait_ge(s['r_exp'], 1)
            link(v.tensor_reduce(den16, score[:], AX.X, ALU.add))
            link(v.reciprocal(den16, den16))
            link(v.tensor_tensor(score[:], score[:], wide(den16), ALU.mult))
            link(v.tensor_tensor(biased[:], score[:], gateb[:].unsqueeze(1).to_broadcast([P, T, E]), ALU.add))
            ve.wait_ge(s['r_bias'], 1)
            bg1 = big1.rearrange("p (t e) f -> p t e f", t=T)
            bg2 = big2.rearrange("p (t e) f -> p t e f", t=T)
            theirs = biased[:].unsqueeze(2).to_broadcast([P, T, E, E])
            mine = biased[:].unsqueeze(3).to_broadcast([P, T, E, E])
            v.tensor_tensor(bg1, theirs, mine, ALU.is_gt)
            link(v.tensor_tensor(bg2, theirs, mine, ALU.is_equal))
            link(v.tensor_tensor(bg2, bg2, lower[:].unsqueeze(1).to_broadcast([P, T, E, E]), ALU.mult))
            link(v.tensor_tensor(bg1, bg1, bg2, ALU.add))
            rank = tmp8
            link(v.tensor_reduce(rank[:], bg1, AX.X, ALU.add))
            link(v.tensor_scalar(sel[:], rank[:], float(TOPK), None, ALU.is_lt))
            link(v.tensor_copy(sel_b[:], sel[:]))
            for e in range(E):
                last = v.tensor_tensor_scan(cum[:, :, e], ones[:, 0:T], sel[:, :, e], 0.0, ALU.mult, ALU.add)
            link(last)
            link(v.tensor_copy(inc_b[:], cum[:]))
            v.tensor_tensor(cum_b[:], cum[:], sel[:], ALU.subtract).then_inc(s['r_sel'], 1)
            ve.wait_ge(s['r_pos'], 1)
            link(v.tensor_copy(flat(pos[:]), pb[0][:, 0:T * E]))
            ci = cnt_i.bitcast(i32)
            link(v.tensor_scalar(ci, pb[1][:, 0:E], float(P - 1), None, ALU.add))
            link(v.tensor_scalar(ci, ci, 7, None, ALU.arith_shift_right))
            link(v.tensor_copy(ntile, ci))
            link(v.tensor_tensor_scan(tend, ones[:, 0:E], ntile, 0.0, ALU.mult, ALU.add))
            link(v.tensor_tensor(tstart, tend, ntile, ALU.subtract))
            link(v.tensor_scalar(tstart, tstart, float(P), None, ALU.mult))
            link(v.tensor_tensor(row[:], pos[:], tstart.unsqueeze(1).to_broadcast([P, T, E]), ALU.add))
            for c in range(TOPK):
                link(v.tensor_scalar(sel[:], rank[:], float(c), None, ALU.is_equal))
                for k, val in ((c, row), (2 + c, score)):
                    link(v.tensor_tensor(cum[:], sel[:], val[:], ALU.mult))
                    link(v.tensor_reduce(route[:, k, :], cum[:], AX.X, ALU.add))
            v.tensor_copy(route_i[:], route[:, 0:2, :]).then_inc(s['r_done'], 1)
            link(v.tensor_tensor(slot_cmp[:], tend.unsqueeze(1).to_broadcast([P, SLOTS, E]),
                                 slot_no.unsqueeze(2).to_broadcast([P, SLOTS, E]), ALU.is_le))
            link(v.tensor_reduce(slot_e[:], slot_cmp[:], AX.X, ALU.add))
            link(v.tensor_scalar(slot_e[:], slot_e[:], float(E - 1), None, ALU.min))
            v.tensor_copy(slot_i[:], slot_e[0:1, :]).then_inc(s['r_slot'], 1)
            link(v.tensor_scalar(eno_i[:], eno_i[:], 31, None, ALU.bitwise_and))
            link(v.tensor_copy(eno[:], eno_i[:]))
            v.tensor_scalar(hot[:], slot_e[0:96, :], eno[0:96, 0:1], None, ALU.is_equal).then_inc(s['r_hot'], 1)
            ve.wait_ge(s['r_hot'], 1)
            link(v.tensor_scalar(eno[:], eno[:], float(SHARED), None, ALU.is_equal))
            v.tensor_copy(hot_sh[:], eno[0:96, 0:1].to_broadcast([96, P])).then_inc(s['r_hot'], 1)
            ve.wait_ge(s['ld_route'], NLD['ld_route'])
            part = bias_part[0:96, :]
            for k in range(3):
                link(v.tensor_copy(part, bias_f[0:96, :]))
                last = v.tensor_copy(bias_b[32 * k:32 * k + 32, :], part[32 * k:32 * k + 32, :])
                if k < 2:
                    link(v.tensor_tensor(bias_f[0:96, :], bias_f[0:96, :], part, ALU.subtract))
            last.then_inc(s['r_hot'], 1)

            def mixture(k, n):
                def step(t):
                    ve.wait_ge(m[k]['lifted'], t * 2 + 1)
                    ve.wait_ge(m[k]['hid'], t)
                    link(v.tensor_tensor(gate, pb[0][:], lift[0], ALU.mult))
                    v.tensor_scalar(gate, gate, LIMIT, None, ALU.min).then_inc(m[k]['gated'], 1)
                    ve.wait_ge(m[k]['lifted'], t * 2 + 2)
                    link(v.tensor_tensor(line, pb[2][:], lift[1], ALU.mult))
                    v.tensor_scalar(line, line, LIMIT, -LIMIT, ALU.min, ALU.max).then_inc(m[k]['lined'], 1)
                    ve.wait_ge(m[k]['sigd'], t + 1)
                    link(v.tensor_tensor(sig, sig, gate, ALU.mult))
                    ve.wait_ge(m[k]['hT_full'], t)
                    v.scalar_tensor_tensor(h_moe, line, 1.0, sig, ALU.add, ALU.mult).then_inc(m[k]['hid'], 1)

                with ve.Fori(0, n) as t:
                    link.loop(t, 3)
                    step(t)
                link.done(n)

            mixture(0, T)
            mixture(1, SLOTS)
            for t in range(T):
                u = t % 2
                ve.wait_ge(c_y[u], 32 * (t // 2 + 1))
                ve.wait_ge(c_s[u], 16 * (t // 2 + 1))
                link(v.scalar_tensor_tensor(ya[u], ya[u], route[:, 2, t:t + 1], x_sb[:, t, :], ALU.mult, ALU.add))
                link(v.scalar_tensor_tensor(ya[u], yb[u], route[:, 3, t:t + 1], ya[u], ALU.mult, ALU.add))
                v.tensor_tensor(x_sb[:, t, :], ya[u], ys[u], ALU.add).then_inc(c_used, 1)


def kernel(**inputs):
    import concourse.bacc as _bacc
    from concourse.bass_utils import run_bass_kernel_spmd as _run

    nc = _bacc.Bacc("TRN2", target_bir_lowering=False, num_devices=1)
    arrays, args = {}, {}
    for name in _INS:
        a = np.ascontiguousarray(inputs[name])
        if a.dtype == np.bool_:
            a = a.astype(np.int32)
        arrays[f"in_{name}"] = a
        args[name] = nc.dram_tensor(f"in_{name}", a.shape, mybir.dt.from_np(a.dtype), kind="ExternalInput").ap()
    out = nc.dram_tensor("out", inputs['x'].shape, mybir.dt.float32, kind="ExternalOutput").ap()
    program(nc, args, out)
    r = _run(nc, [arrays], core_ids=[0])
    return r.results[0]["out"]
```

```python
import concourse.bass as bass
from concourse import mybir
from contextlib import ExitStack
import numpy as np

_INS = ['x', 'ctx_768', 'mask_BxS2_bk0', 'L0_xattn_Wq', 'L0_xattn_bq', 'L0_xattn_Wk', 'L0_xattn_bk', 'L0_xattn_Wv',
        'L0_xattn_bv', 'L0_xattn_Wo', 'L0_xattn_bo', 'L0_ffn_W1', 'L0_ffn_b1', 'L0_ffn_W2', 'L0_ffn_b2',
        'L1_xattn_ln_x_g', 'L1_xattn_ln_x_b', 'L1_xattn_ln_l_g', 'L1_xattn_ln_l_b', 'L1_xattn_qn_g', 'L1_xattn_kn_g',
        'L1_xattn_Wq', 'L1_xattn_Wkv', 'L1_xattn_Wlkv', 'L1_xattn_Wo', 'L1_xattn_bo', 'L1_ffn_gate_w', 'L1_ffn_gate_b',
        'L1_ffn_w1', 'L1_ffn_b1', 'L1_ffn_w3', 'L1_ffn_b3', 'L1_ffn_w2', 'L1_ffn_b2', 'L1_ffn_sw1', 'L1_ffn_sb1',
        'L1_ffn_sw3', 'L1_ffn_sb3', 'L1_ffn_sw2', 'L1_ffn_sb2']


class Chain:

    def __init__(self, eng, sem):
        self.eng, self.sem, self.base, self.n, self.at, self.per = eng, sem, 0, 0, None, 0

    def loop(self, at, per):
        self.at, self.per, self.n = at, per, 0

    def done(self, turns):
        assert self.n == self.per, (self.n, self.per)
        self.base += turns * self.per
        self.at, self.n = None, 0

    def __call__(self, instruction):
        instruction.then_inc(self.sem, 1)
        self.n += 1
        if self.at is None:
            self.base, self.n = self.base + 1, 0
            self.eng.wait_ge(self.sem, self.base)
        else:
            self.eng.wait_ge(self.sem, self.at * self.per + (self.base + self.n))


def program(nc, ins, out):
    f32, bf16, i32, f32r = mybir.dt.float32, mybir.dt.bfloat16, mybir.dt.int32, mybir.dt.float32r
    ALU, ACT, AX = mybir.AluOpType, mybir.ActivationFunctionType, mybir.AxisListType
    P = 128
    B, S, D = ins['x'].shape
    SK, DC = ins['ctx_768'].shape[1:]
    T = B * S // P
    TB = S // P
    KC = D // P
    SKB = B * SK
    HID = ins['L0_ffn_W1'].shape[0]
    HC = HID // P
    DH = ins['L1_xattn_qn_g'].shape[0]
    NH = D // DH
    QKV = 3 * D
    E = ins['L1_ffn_gate_w'].shape[0]
    I2 = ins['L1_ffn_w1'].shape[2]
    I = I2 // 2
    IC = I // P
    TOPK = 2
    SLOTS = (B * S * TOPK - E) // P + E
    DCR = DC - P
    DA = DH + 1
    SCALE0 = 1.0 / float(np.sqrt(D // 8))
    LN_EPS, RMS_EPS, QB, QEPS = 1e-5, 1e-8, 127.0, 1e-5
    MAGIC = 12582912.0
    BIG = 1e30
    ALPHA, LIMIT = 1.702, 7.0
    WEXP = 2 * KC * I2 + IC * D
    OFF1, OFF3, OFF2 = 0, KC * I2, 2 * KC * I2
    PLACES_AT = 3
    SHARED = E
    SHARED_AT = E - 1
    NB = 2 * I2 + D

    ctx = ExitStack()
    with ctx:
        ctx.enter_context(nc.allow_non_contiguous_dma(reason="short bias columns"))

        def sb(name, shape, dt=f32):
            return ctx.enter_context(nc.sbuf_tensor(name, shape, dt))

        def sem(name):
            return ctx.enter_context(nc.semaphore(name))

        moe_in = nc.dram_tensor("moe_in", (SLOTS * P, D), f32, kind="Internal").ap()
        moe_x = nc.dram_tensor("moe_x", (T * P, D), f32, kind="Internal").ap()
        moe_out = nc.dram_tensor("moe_out", (SLOTS * P, D), f32, kind="Internal").ap()

        x_sb = sb("x_sb", [P, T, D])
        KW = -(-(S + SK) // 8) * 8
        SPLIT = B * 4 * KW
        early = ExitStack()
        early.enter_context(nc.sbuf_tensor("early_rest", [P, SHARED_AT * WEXP - SPLIT], f32))
        split = lambda name: [early.enter_context(nc.sbuf_tensor(f"{name}{u}", [P, KW], f32r)) for u in range(B)]
        q_hi = split("q_hi")
        q_lo = split("q_lo")
        k_hl = split("k_hl")
        k_hi = split("k_hi")
        early.close()
        wexp = sb("wexp", [P, E * WEXP])
        aux = sb("aux", [P, 5376])
        small = sb("small", [P, 800])

        class Words:

            def __init__(self, buf, at, end):
                self.buf, self.at, self.end = buf, at, end

            def take(self, n, parts=None, dt=None):
                a, words = self.at, n if dt is None else (n + 1) // 2
                self.at += words
                assert self.at <= self.end, (self.at, self.end)
                v = self.buf[:, a:a + words]
                if dt is not None:
                    v = v.bitcast(dt)
                return v if parts is None else v.rearrange("p (a b) -> p a b", a=parts)

        scr = Words(wexp, WEXP, SHARED_AT * WEXP)
        qkv = scr.take(T * QKV, T)
        mark = scr.at
        scr.at = WEXP
        w1_raw = scr.take(HC * D, HC)
        w2_raw = scr.take(KC * HID, KC)
        w1T = scr.take(KC * HID, KC, bf16)
        w2T = scr.take(HC * D, HC, bf16)
        b1_all = scr.take(HID)
        h_f = [scr.take(HID) for _ in range(2)]
        h_q = [scr.take(HID, dt=bf16) for _ in range(2)]
        h_qT = [scr.take(HID, HC, bf16) for _ in range(2)]
        assert scr.at <= mark
        w1_t = h_f[0].bitcast(bf16).rearrange("p (a b) -> p a b", a=HC)
        w2_t = h_f[1].bitcast(bf16).rearrange("p (a b) -> p a b", a=KC)
        scr.at = mark
        woT = scr.take(NH * (D + 1), NH)
        zeros = scr.take(D)
        mask_u = scr.take(SKB).bitcast(i32)
        first = scr.at
        wT = scr.take(KC * QKV, KC)
        wcT = scr.take(KC * 2 * D, KC)
        l0_wq = scr.take(KC * D, KC)
        l0_wk = scr.take(2 * D, 2)
        l0_wv = scr.take(2 * D, 2)
        l0_wo = scr.take(KC * D, KC)
        l0_wqT = scr.take(KC * D, KC)
        ctx_sb = scr.take(B * DC, B)
        ctxT = scr.take(2 * SKB, 2)
        kT0 = scr.take(KC * SKB, KC)
        vT0 = scr.take(KC * SKB, KC)
        m0 = scr.take(KC * SKB, KC)
        c0 = scr.take(SKB)
        vv0 = scr.take(B * D, B)
        bo0 = scr.take(D)
        wq_raw = scr.take(KC * D, KC)
        wlkv_raw = scr.take(2 * KC * D, 2 * KC)
        wkv_raw = scr.take(2 * KC * DC, 2 * KC)
        wo_raw = scr.take(KC * D, KC)
        scr.at = first
        q_dup = scr.take(TB * P, TB)
        k_dup = scr.take((TB + 1) * P, TB + 1)
        vh = [scr.take((TB + 1) * DA, TB + 1) for _ in range(2)]
        pT = [scr.take(512) for _ in range(3)]
        oT = [scr.take(S) for _ in range(2)]
        bias_part = scr.take(NB, dt=bf16)
        assert scr.at <= SHARED_AT * WEXP - SPLIT

        ax = Words(aux, 0, 5376)
        xn = ax.take(4 * D, 4)
        xnT = ax.take(KC * 512, KC)
        xq = [ax.take(D, dt=bf16) for _ in range(2)]
        xqT = [ax.take(D, KC, bf16) for _ in range(2)]
        p0 = ax.take(4 * SK, 4)
        ckv = ax.take(B * 2 * D, B)
        b2_all, bo1_all, gate_raw = ax.take(D), ax.take(D), ax.take(D)[0:E]
        ax.at = 0
        x_in = [ax.take(D) for _ in range(2)]
        x_inT = [ax.take(D, KC) for _ in range(2)]
        lift = [ax.take(I) for _ in range(2)]
        gate = ax.take(I)
        line = ax.take(I)
        sig = ax.take(I)
        h_moe = ax.take(I)
        h_moeT = ax.take(I, IC)
        y_sb = [ax.take(D) for _ in range(2)]
        hot_t, hot_y = ([ax.take(P, dt=bf16) for _ in range(2)] for _ in range(2))
        DEEP = 4
        y_of = [[aux[:, (4 + u * TOPK + c) * D:(5 + u * TOPK + c) * D] for c in range(TOPK)] for u in range(DEEP)]
        bias_f = aux[:, 0:NB]

        ident = sb("ident", [P, P])
        ident_b = sb("ident_b", [P, P], bf16)
        ones = sb("ones", [P, P])
        ones_b = sb("ones_b", [P, P], bf16)
        before = sb("before", [P, P], bf16)
        bias_b = sb("bias_b", [96, NB], bf16)
        hot_sh = sb("hot_sh", [96, P], bf16)

        sm = Words(small, 0, 800)
        stats = sm.take(T * 6, T)
        mv = sm.take((T + B) * 2, T + B)
        root_a, root_s, root_t, rstd = (sm.take(T * 2 * NH + 2 * NH) for _ in range(4))
        ss = root_a
        rn = rstd
        gateT = sb("gateT", [P, KC, E])
        gateb = sb("gateb", [P, E])
        cols = sm.take(40)
        bk0, bv0, bq0 = cols[:, 0:2], cols[:, 2:4], cols[:, 4:6]
        lg, lb, xg, xb = cols[:, 6:8], cols[:, 8:10], cols[:, 10:12], cols[:, 12:14]
        qg, kg = cols[:, 14:15], cols[:, 15:16]
        wsum, wsc, winv = cols[:, 16:18], cols[:, 18:20], cols[:, 20:22]
        amax, aden, arow = cols[:, 22:24], cols[:, 24:26], cols[:, 26:28]
        hmax, hden, hrow = cols[:, 28:30], cols[:, 30:32], cols[:, 32:34]
        yden = cols[:, 34:36]
        maskc_u = sb("maskc_u", [SK, B], i32)
        mask_row = sb("mask_row", [1, SKB], bf16)
        mask_col = sb("mask_col", [SK, B])
        mx4, sums4 = sm.take(4), sm.take(4)
        mx8 = sm.take(TB)
        negm = sm.take(TB)
        p0T = xnT[:, 0, :]
        banks = ctx.enter_context(nc.psum_tensor("banks", [P, 8 * 512], f32))
        pb = [banks[:, n * 512:(n + 1) * 512] for n in range(8)]
        rt = Words(wexp, SHARED_AT * WEXP - 7200, SHARED_AT * WEXP)
        NORM_AT = 4
        xm = wexp[:, NORM_AT * WEXP:NORM_AT * WEXP + T * D].rearrange("p (a b) -> p a b", a=T)
        score, biased, val, row, rank, *chosen = (rt.take(T * E, T) for _ in range(5 + TOPK))
        pos = rt.take((T + 1) * E, T + 1)
        big1, big2 = rt.take(T * E * E, T * E), rt.take(T * E * E, T * E)
        sel_b = rt.take(T * E, T, bf16)
        lower = rt.take(E * E, E)
        ntile, tend, tstart, ntile_r = (rt.take(E) for _ in range(4))
        slot_no = rt.take(SLOTS)
        slot_cmp = rt.take(SLOTS * E, SLOTS)
        den16 = rt.take(T)
        route = sb("route", [P, 4, T])
        route_i = sb("route_i", [P, 2, T], i32)
        slot_e = rt.take(SLOTS)
        slot_i = sb("slot_i", [1, SLOTS], i32)
        hot = sb("hot", [96, SLOTS], bf16)
        eno_i = sb("eno_i", [P, 1], i32)
        eno, eno_sh = sb("eno", [P, 1]), sb("eno_sh", [P, 1])

        names = """ld_x ld_l0 ld_ffn ld_l1 ld_route ld_shared ld_e0 ld_mid ld_late ld_last const prep_full prep_free
            root_in root_out chain chain_pool
            g_xn g_xnT_full g_xnT g_sc g_sh g_p g_pT_full g_pT g_av
            f_xq f_xqT_full f_xqT f_acc f_pre f_h f_amax f_h127 f_hq f_hqT_full f_hqT f_y f_yout f_b2
            l_free l_xh l_xT_full l_xT l_qkv l_qk l_v l_sq l_ss l_bo
            a_qk a_v a_hi a_khi t_full t_free a_mx_full a_mx_free a_negm a_s_full a_p a_pv a_o a_oT
            r_x r_xm r_xT_full r_xT r_logit r_e r_exp r_sel r_pos_full r_pos r_slot r_zero r_bias r_hot_sh r_table r_start
            zero xdram scat
            """.split()
        s = {n: sem(n) for n in names}
        st_in = [sem(f"ym_in{u}") for u in range(2)]
        mnames = "xin xinT_full xinT prod lifted gated sigd lined hid hT_full hT y ysb hot hoty".split()
        m = [{n: sem(f"m{k}_{n}") for n in mnames} for k in range(2)]
        m_x = [[sem(f"m{k}_x{u}") for u in range(2)] for k in range(2)]
        m_st = [[sem(f"m{k}_st{u}") for u in range(2)] for k in range(2)]
        c_y = [sem(f"c_y{u}") for u in range(DEEP)]
        c_used, c_acc, c_out = sem("c_used"), sem("c_acc"), sem("c_out")

        W = ins
        NLD = {}

        block = ctx.enter_context(nc.Block())

        def halves(e, off, kc):
            v = wexp[:, bass.ds(e + (off + kc * I2), I2)]
            return v.rearrange("p (n two) -> p n two", two=2)

        @block.sync
        def _(sp):
            def load(dst, src, to):
                sp.dma_start(dst, src).then_inc(s[to], 16)
                NLD[to] = NLD.get(to, 0) + 16

            load(x_sb[:], W['x'].rearrange("b (t p) d -> p (b t) d", p=P), 'ld_x')
            load(l0_wq[:], W['L0_xattn_Wq'].rearrange("(c p) n -> p c n", p=P), 'ld_l0')
            load(ctx_sb[0:SK], W['ctx_768'].rearrange("b k c -> k b c"), 'ld_l0')
            for dst, w in ((l0_wk, 'L0_xattn_Wk'), (l0_wv, 'L0_xattn_Wv')):
                load(dst[:, 0, :], W[w][0:P, :], 'ld_l0')
                load(dst[0:DCR, 1, :], W[w][P:DC, :], 'ld_l0')
            load(l0_wo[:], W['L0_xattn_Wo'].rearrange("(c p) n -> p c n", p=P), 'ld_l0')
            for dst, w in ((bk0, 'L0_xattn_bk'), (bv0, 'L0_xattn_bv'), (bq0, 'L0_xattn_bq')):
                load(dst, W[w].rearrange("(c p) -> p c", p=P), 'ld_l0')
            load(bo0[0:1, :], W['L0_xattn_bo'].rearrange("(a n) -> a n", a=1), 'ld_l0')
            load(w1_raw[:], W['L0_ffn_W1'].rearrange("(t p) n -> p t n", p=P), 'ld_ffn')
            load(w2_raw[:], W['L0_ffn_W2'].rearrange("(t p) n -> p t n", p=P), 'ld_ffn')
            load(b1_all[:], W['L0_ffn_b1'].partition_broadcast(P), 'ld_ffn')
            load(b2_all[:], W['L0_ffn_b2'].partition_broadcast(P), 'ld_ffn')
            load(wq_raw[:], W['L1_xattn_Wq'].rearrange("(t p) n -> p t n", p=P), 'ld_l1')
            load(wlkv_raw[:], W['L1_xattn_Wlkv'].rearrange("(t p) n -> p t n", p=P), 'ld_l1')
            load(wkv_raw[:], W['L1_xattn_Wkv'].rearrange("(t p) n -> p t n", p=P), 'ld_l1')
            load(wo_raw[:], W['L1_xattn_Wo'].rearrange("(t p) n -> p t n", p=P), 'ld_l1')
            for dst, w in ((lg, 'L1_xattn_ln_l_g'), (lb, 'L1_xattn_ln_l_b')):
                load(dst, W[w].rearrange("(c p) -> p c", p=P), 'ld_l1')
            for dst, w in ((xg, 'L1_xattn_ln_x_g'), (xb, 'L1_xattn_ln_x_b')):
                load(dst[:, 0:1], W[w][0:P].rearrange("(p a) -> p a", a=1), 'ld_l1')
                load(dst[0:DCR, 1:2], W[w][P:DC].rearrange("(p a) -> p a", a=1), 'ld_l1')
            for dst, w in ((qg, 'L1_xattn_qn_g'), (kg, 'L1_xattn_kn_g')):
                for r in range(0, P, DH):
                    load(dst[r:r + DH], W[w].rearrange("(p a) -> p a", a=1), 'ld_l1')
            load(bo1_all[:], W['L1_xattn_bo'].partition_broadcast(P), 'ld_l1')
            load(mask_u[0:1, :], W['mask_BxS2_bk0'].rearrange("b k -> (b k)").rearrange("(a n) -> a n", a=1), 'ld_l1')
            load(maskc_u[:], W['mask_BxS2_bk0'].rearrange("b k -> k b"), 'ld_l1')
            load(gate_raw[:], W['L1_ffn_gate_w'], 'ld_l1')
            load(gateb[:], W['L1_ffn_gate_b'].partition_broadcast(P), 'ld_l1')

            def expert(at, w1, w3, w2, to):
                base = at * WEXP
                for off, w, c in ((OFF1, w1, KC), (OFF3, w3, KC), (OFF2, w2, IC)):
                    n = w.shape[-1]
                    load(wexp[:, base + off:base + off + c * n].rearrange("p (c n) -> p c n", c=c),
                         w.rearrange("(c p) n -> p c n", p=P), to)

            expert(SHARED_AT, W['L1_ffn_sw1'], W['L1_ffn_sw3'], W['L1_ffn_sw2'], 'ld_shared')
            expert(0, W['L1_ffn_w1'][0], W['L1_ffn_w3'][0], W['L1_ffn_w2'][0], 'ld_e0')
            sp.wait_ge(s['const'], 1)
            for n in range(SLOTS):
                sp.dma_start(moe_in[n * P:(n + 1) * P, :], zeros[:]).then_inc(s['zero'], 16)
            sp.wait_ge(s['zero'], 16 * SLOTS)
            sp.wait_ge(s['r_zero'], 1)
            for k in range(3):
                r = slice(32 * k, 32 * k + E)
                q = slice(32 * k + E, 32 * k + E + 1)
                for a, b, wn, sn in ((0, I2, 'L1_ffn_b1', 'L1_ffn_sb1'), (I2, 2 * I2, 'L1_ffn_b3', 'L1_ffn_sb3'),
                                     (2 * I2, NB, 'L1_ffn_b2', 'L1_ffn_sb2')):
                    load(bias_f[r, a:b], W[wn], 'ld_route')
                    load(bias_f[q, a:b], W[sn].rearrange("(a n) -> a n", a=1), 'ld_route')
            def routed(e, to):
                expert(e, W['L1_ffn_w1'][e], W['L1_ffn_w3'][e], W['L1_ffn_w2'][e], to)

            sp.wait_ge(s['a_oT'], 1)
            for e in range(1, NORM_AT):
                routed(e, 'ld_mid')
            sp.wait_ge(s['r_xm'], T)
            sp.dma_start(moe_x.rearrange("(t p) d -> p t d", p=P), xm[:]).then_inc(s['xdram'], 16)
            sp.wait_ge(s['xdram'], 16)
            sp.wait_ge(s['r_logit'], T)
            sp.wait_ge(s['r_bias'], 1)

            def tiles(k, n, src, dst):
                def turn(t, u, first):
                    if not first:
                        sp.wait_ge(m[k]['xinT_full'], t - 1)
                    sp.dma_start(x_in[u], src[bass.ds(t * P, P), :]).then_inc(m_x[k][u], 16)

                def store(t, u):
                    if dst is None:
                        return
                    sp.wait_ge(m[k]['ysb'], t + 1)
                    sp.dma_start(dst[bass.ds(t * P, P), :], y_sb[u]).then_inc(m_st[k][u], 16)

                turn(0, 0, True)
                turn(1, 1, True)
                with sp.Fori(0, (n - 2) // 2) as i:
                    for u in range(2):
                        turn(i * 2 + (u + 2), u, False)
                        store(i * 2 + u, u)
                done = (n - 2) // 2 * 2
                for t in range(done, n):
                    if t + 2 < n:
                        turn(t + 2, t % 2, False)
                    store(t, t % 2)

            tiles(0, T, moe_x, None)
            sp.wait_ge(m[0]['y'], T)
            routed(E - 1, 'ld_last')
            sp.wait_ge(s['scat'], 16 * 2 * T)
            tiles(1, SLOTS, moe_in, moe_out)
            for u in range(2):
                sp.wait_ge(m_st[1][u], 16 * ((SLOTS + 1 - u) // 2))
            outv = out.rearrange("b (t p) d -> p (b t) d", p=P)
            for t in range(T):
                sp.wait_ge(c_used, t + 1)
                sp.dma_start(outv[:, t, :], x_sb[:, t, :]).then_inc(c_out, 16)
            sp.wait_ge(c_out, 16 * T)

        @block.gpsimd
        def _(pool):
            g = nc.gpsimd
            link = Chain(pool, s['chain_pool'])
            g.memset(zeros[:], 0.0).then_inc(s['const'], 1)
            g.memset(ones[:], 1.0)
            g.memset(ones_b[:], 1.0)
            link(g.memset(ident[:], 0.0))
            link(g.affine_select(out=ident[:], in_=ident[:], compare_op=ALU.not_equal, fill=1.0, base=0,
                                 pattern=[[-1, P]], channel_multiplier=1))
            g.tensor_copy(ident_b[:], ident[:])
            link(g.affine_select(out=before[:], in_=ones_b[:], compare_op=ALU.is_gt, fill=0.0, base=0,
                                 pattern=[[1, P]], channel_multiplier=-1))
            link(g.memset(mv[:], 1.0))
            link(g.memset(ctxT[:], 0.0))
            link(g.memset(woT[:], 0.0))
            link(g.memset(woT[DH:DA, :, D:D + 1], 1.0))
            g.iota(eno_i[:], pattern=[[0, 1]], base=0, channel_multiplier=1).then_inc(s['const'], 1)
            flat = lambda v: v.rearrange("p a b -> p (a b)")

            with pool.Fori(0, T) as t:
                pool.wait_ge(s['f_xq'], t + 1)
                g.tensor_tensor(x_sb[:, bass.ds(t, 1), :].rearrange("p a d -> p (a d)"),
                                x_sb[:, bass.ds(t, 1), :].rearrange("p a d -> p (a d)"),
                                b2_all[:], ALU.add).then_inc(s['f_b2'], 1)

            with pool.Fori(0, T) as t:
                pool.wait_ge(s['l_xh'], t + 1)
                g.tensor_tensor(x_sb[:, bass.ds(t, 1), :].rearrange("p a d -> p (a d)"),
                                x_sb[:, bass.ds(t, 1), :].rearrange("p a d -> p (a d)"),
                                bo1_all[:], ALU.add).then_inc(s['l_bo'], 1)

            pool.wait_ge(s['l_bo'], T)
            pool.wait_ge(s['l_free'], 1)
            g.memset(bias_f, 0.0).then_inc(s['r_zero'], 1)
            for u in range(2):
                link(g.memset(k_hl[u][:, S + SK:KW].bitcast(f32), 0.0))
                link(g.memset(k_hi[u][DH:DA, 0:S + SK].bitcast(f32), 1.0))
                link(g.memset(vh[u][:, :, DH:DA], 1.0))

            def head(n, h, b):
                if n is not None:
                    pool.wait_ge(s['a_o'], n - 1)
                pool.wait_ge(s['a_hi'], 5 if n is None and b == 0 else 10 if n is None else n * 5 + 5)
                col = h * DH + 2 * D
                g.tensor_copy(vh[b][:, 0:TB, 0:DH], qkv[:, b * TB:(b + 1) * TB, bass.ds(col, DH)])
                g.tensor_copy(vh[b][0:SK, TB, 0:DH], ckv[0:SK, b, bass.ds(h * DH + D, DH)]).then_inc(s['a_v'], 1)
                g.tensor_copy(k_hi[b][0:DH, 0:S + SK], k_hl[b][0:DH, 0:S + SK]).then_inc(s['a_khi'], 1)

            head(None, 0, 0)
            head(None, 0, 1)
            pool.wait_ge(s['ld_route'], NLD['ld_route'])
            part = bias_part[0:96, :]
            for k in range(3):
                link(g.tensor_copy(part, bias_f[0:96, :]))
                link(g.tensor_copy(bias_b[32 * k:32 * k + 32, :], part[32 * k:32 * k + 32, :]))
                if k < 2:
                    link(g.tensor_tensor(bias_f[0:96, :], bias_f[0:96, :], part, ALU.subtract))
            pool.sem_inc(s['r_bias'], 1)
            with pool.Fori(0, NH - 1) as i:
                for b in range(B):
                    head(i * 2 + (2 + b), i + 1, b)

            pool.wait_ge(s['a_oT'], 1)
            link(g.memset(lower[:], 1.0))
            link(g.affine_select(out=lower[:], in_=lower[:], compare_op=ALU.is_gt, fill=0.0, base=0,
                                 pattern=[[1, E], [-1, E]], channel_multiplier=0))
            g.iota(slot_no[:], pattern=[[1, SLOTS]], base=0, channel_multiplier=0,
                   allow_small_or_imprecise_dtypes=True).then_inc(s['r_table'], 1)
            pool.wait_ge(s['zero'], 16 * SLOTS)
            for t in range(T):
                pool.wait_ge(s['r_x'], t + 1)
                g.tensor_copy(xm[:, t, :], xn[:, t % 4, :]).then_inc(s['r_xm'], 1)
            def folded(dst, src):
                n = E // 2
                while n > 1:
                    link(g.tensor_tensor(src[:, :, 0:n], src[:, :, 0:n], src[:, :, n:2 * n], ALU.add))
                    n //= 2
                link(g.tensor_tensor(dst.unsqueeze(2), src[:, :, 0:1], src[:, :, 1:2], ALU.add))

            pool.wait_ge(s['r_start'], 1)
            link(g.tensor_tensor(row[:], pos[:, 0:T, :], tstart.unsqueeze(1).to_broadcast([P, T, E]), ALU.add))
            for c in range(TOPK):
                for k, of in ((c, row), (2 + c, score)):
                    link(g.tensor_tensor(val[:], chosen[c][:], of[:], ALU.mult))
                    folded(route[:, k, :], val)
            link(g.tensor_copy(route_i[:], route[:, 0:2, :]))
            for t in range(T):
                for c in range(2):
                    g.indirect_dma_start(out=moe_in, out_offset=bass.IndirectOffsetOnAxis(ap=route_i[:, c, t:t + 1], axis=0),
                                         in_=xm[:, t, :], in_offset=None,
                                         bounds_check=SLOTS * P - 1, oob_is_err=False).then_inc(s['scat'], 16)
            def routed(e):
                at = e * WEXP
                for off, w, c in ((OFF1, W['L1_ffn_w1'], KC), (OFF3, W['L1_ffn_w3'], KC), (OFF2, W['L1_ffn_w2'], IC)):
                    n = w.shape[-1]
                    g.dma_start(wexp[:, at + off:at + off + c * n].rearrange("p (c n) -> p c n", c=c),
                                w[e].rearrange("(c p) n -> p c n", p=P)).then_inc(s['ld_late'], 16)

            pool.wait_ge(s['r_slot'], 1)
            for e in range(NORM_AT + 1, E - 1):
                routed(e)
            pool.wait_ge(s['scat'], 16 * 2 * T)
            routed(NORM_AT)

            def pick(dst, t, sem):
                g.tensor_copy(dst[0:96, :], hot[:, bass.ds(t, 1)].to_broadcast([96, P])).then_inc(m[1][sem], 1)

            pool.wait_ge(m[0]['y'], T)
            pick(hot_t[0], 0, 'hot')
            pick(hot_t[1], 1, 'hot')
            pick(hot_y[0], 0, 'hoty')

            def picks(t, u):
                pool.wait_ge(m[1]['prod'], t * 2 - 2)
                pool.wait_ge(m[1]['y'], t - 2)
                pick(hot_t[u], t, 'hot')
                pick(hot_y[1 - u], t - 1, 'hoty')

            with pool.Fori(0, (SLOTS - 3) // 2) as i:
                for u in range(2):
                    picks(i * 2 + (2 + u), u)
            picks(SLOTS - 1, 0)
            pool.wait_ge(m[1]['y'], SLOTS - 2)
            pick(hot_y[0], SLOTS - 1, 'hoty')

            for u in range(2):
                pool.wait_ge(m_st[1][u], 16 * ((SLOTS + 1 - u) // 2))
            for t in range(T):
                u = t % DEEP
                if t >= DEEP:
                    pool.wait_ge(c_used, t - DEEP + 1)
                for c in range(TOPK):
                    g.indirect_dma_start(out=y_of[u][c], out_offset=None, in_=moe_out,
                                         in_offset=bass.IndirectOffsetOnAxis(ap=route_i[:, c, t:t + 1], axis=0),
                                         bounds_check=SLOTS * P - 1, oob_is_err=False).then_inc(c_y[u], 16)

        @block.tensor
        def _(pe):
            mm = nc.tensor.matmul
            tr = nc.tensor.transpose
            unit = [0]

            def bank():
                if unit[0] >= 2:
                    pe.wait_ge(s['prep_free'], unit[0] - 1)
                unit[0] += 1
                return pb[(unit[0] - 1) % 2]

            pe.wait_ge(s['const'], 2)
            pe.wait_ge(s['ld_l0'], NLD['ld_l0'])
            o = bank()
            for ec in range(KC):
                for dc in range(KC):
                    a = (ec * KC + dc) * P
                    last = tr(o[:, a:a + P], l0_wq[:, dc, ec * P:(ec + 1) * P], ident[:])
            last.then_inc(s['prep_full'], 1)
            o = bank()
            for b in range(B):
                tr(o[:, b * SK:(b + 1) * SK], ctx_sb[0:SK, b, 0:P], ident[0:SK, 0:SK])
                last = tr(o[0:DCR, SKB + b * SK:SKB + (b + 1) * SK], ctx_sb[0:SK, b, P:DC], ident[0:SK, 0:SK])
            last.then_inc(s['prep_full'], 1)
            pe.wait_ge(s['prep_free'], 2)
            for w in (l0_wk, l0_wv):
                o = bank()
                for ec in range(KC):
                    mm(o[:, ec * SKB:(ec + 1) * SKB], w[:, 0, ec * P:(ec + 1) * P], ctxT[:, 0, :], start=True, stop=False)
                    last = mm(o[:, ec * SKB:(ec + 1) * SKB], w[0:DCR, 1, ec * P:(ec + 1) * P], ctxT[0:DCR, 1, :],
                              start=False, stop=True)
                last.then_inc(s['prep_full'], 1)
            pe.wait_ge(s['prep_free'], 3)
            o = bank()
            for dc in range(KC):
                for ec in range(KC):
                    mm(o[:, dc * SKB:(dc + 1) * SKB], l0_wqT[:, ec, dc * P:(dc + 1) * P], kT0[:, ec, :],
                       start=ec == 0, stop=ec == KC - 1)
            for ec in range(KC):
                last = mm(o[0:1, KC * SKB:(KC + 1) * SKB], bq0[:, ec:ec + 1], kT0[:, ec, :], start=ec == 0, stop=ec == KC - 1)
            last.then_inc(s['prep_full'], 1)
            pe.wait_ge(s['prep_free'], 4)
            o = bank()
            for b in range(B):
                for ec in range(KC):
                    mm(o[0:SK, b * D:(b + 1) * D], vT0[:, ec, b * SK:(b + 1) * SK], l0_wo[:, ec, :], start=ec == 0, stop=False)
                last = mm(o[0:SK, b * D:(b + 1) * D], ones[0:1, 0:SK], bo0[0:1, :], start=False, stop=True)
            last.then_inc(s['prep_full'], 1)
            pe.wait_ge(s['f_pre'], 1)
            o = bank()
            mm(o[:, 0:2], ones[:], wsum, start=True, stop=True).then_inc(s['prep_full'], 1)
            pe.wait_ge(s['f_pre'], 2)
            for kc in range(KC):
                o = bank()[:].bitcast(bf16)
                for hc in range(HC):
                    last = tr(o[:, hc * P:(hc + 1) * P], w1_t[:, hc, kc * P:(kc + 1) * P], ident_b[:])
                last.then_inc(s['prep_full'], 1)
            pe.wait_ge(s['f_pre'], 3)
            for half in range(2):
                o = bank()[:].bitcast(bf16)
                for j in range(HC // 2):
                    hc = half * (HC // 2) + j
                    for oc in range(KC):
                        last = tr(o[:, (j * KC + oc) * P:(j * KC + oc + 1) * P], w2_t[:, oc, hc * P:(hc + 1) * P], ident_b[:])
                last.then_inc(s['prep_full'], 1)
            pe.wait_ge(s['ld_l1'], NLD['ld_l1'])
            o = bank()
            for kc in range(KC):
                for oc in range(KC):
                    a = (kc * KC + oc) * P
                    last = tr(o[:, a:a + P], wq_raw[:, oc, kc * P:(kc + 1) * P], ident[:])
            last.then_inc(s['prep_full'], 1)
            for kc in range(KC):
                o = bank()
                for oc in range(2 * KC):
                    last = tr(o[:, oc * P:(oc + 1) * P], wlkv_raw[:, oc, kc * P:(kc + 1) * P], ident[:])
                last.then_inc(s['prep_full'], 1)
            for a, b in ((0, P), (P, DC)):
                o = bank()
                for oc in range(2 * KC):
                    last = tr(o[0:b - a, oc * P:(oc + 1) * P], wkv_raw[:, oc, a:b], ident[:])
                last.then_inc(s['prep_full'], 1)
            for hp in range(NH // 2):
                o = bank()
                for j in range(2):
                    h = hp * 2 + j
                    for lc in range(KC):
                        last = tr(o[0:DH, (j * KC + lc) * P:(j * KC + lc + 1) * P], wo_raw[:, lc, h * DH:(h + 1) * DH], ident[:])
                last.then_inc(s['prep_full'], 1)
            o = bank()
            for kc in range(KC):
                last = tr(o[:, kc * E:(kc + 1) * E], gate_raw[:, kc * P:(kc + 1) * P], ident[0:E, 0:E])
            last.then_inc(s['prep_full'], 1)
            pe.wait_ge(s['f_pre'], 4)
            o = bank()
            for b in range(B):
                tr(o[:, b * SK:(b + 1) * SK], xn[0:SK, b, 0:P], ident[0:SK, 0:SK])
                last = tr(o[0:DCR, SKB + b * SK:SKB + (b + 1) * SK], xn[0:SK, b, P:DC], ident[0:SK, 0:SK])
            last.then_inc(s['prep_full'], 1)
            pe.wait_ge(s['prep_free'], unit[0])
            for b in range(B):
                o = bank()
                mm(o[0:SK, :], ctxT[:, 0, b * SK:(b + 1) * SK], wcT[:, 0, :], start=True, stop=False)
                mm(o[0:SK, :], ctxT[0:DCR, 1, b * SK:(b + 1) * SK], wcT[0:DCR, 1, :], start=False, stop=True)\
                    .then_inc(s['prep_full'], 1)
            pe.wait_ge(s['prep_free'], unit[0])

            G = 4
            with pe.Fori(0, B) as b:
                with pe.Fori(0, TB // G) as j:
                    it = b * (TB // G) + j
                    pe.wait_ge(s['g_xn'], it + 1)
                    for kc in range(KC):
                        for u in range(G):
                            last = tr(pb[kc][:, u * P:(u + 1) * P], xn[:, u, kc * P:(kc + 1) * P], ident[:])
                    last.then_inc(s['g_xnT_full'], 1)
                    pe.wait_ge(s['g_xnT'], it + 1)
                    for u in range(G):
                        so = pb[2][:, u * SK:(u + 1) * SK]
                        for kc in range(KC):
                            mm(so, xnT[:, kc, u * P:(u + 1) * P], m0[:, kc, bass.ds(b * SK, SK)], start=kc == 0, stop=False)
                        last = mm(so, ones[0:1, :], c0[0:1, bass.ds(b * SK, SK)], start=False, stop=True)
                    last.then_inc(s['g_sc'], 1)
                    pe.wait_ge(s['g_p'], it + 1)
                    for u in range(G):
                        last = tr(pb[3][0:SK, u * P:(u + 1) * P], p0[:, u, :], ident[:])
                    last.then_inc(s['g_pT_full'], 1)
                    pe.wait_ge(s['g_pT'], it + 1)
                    for u in range(G):
                        last = mm(pb[4 + u // 2][:, (u % 2) * D:(u % 2 + 1) * D], p0T[0:SK, u * P:(u + 1) * P],
                                  vv0[0:SK, bass.ds(b, 1), :].rearrange("p a d -> p (a d)"), start=True, stop=True)
                    last.then_inc(s['g_av'], 1)

            def ffn_in(t, u, first):
                pe.wait_ge(s['f_xq'], t + 1)
                o = pb[7][:].bitcast(bf16)
                for kc in range(KC):
                    last = tr(o[:, kc * P:(kc + 1) * P], xq[u][:, kc * P:(kc + 1) * P], ident_b[:])
                last.then_inc(s['f_xqT_full'], 1)
                pe.wait_ge(s['f_xqT'], t + 1)
                if not first:
                    pe.wait_ge(s['f_acc'], t - 1)
                for half in range(2):
                    for kc in range(KC):
                        last = mm(pb[2 * u + half][:], xqT[u][:, kc, :], w1T[:, kc, half * 512:(half + 1) * 512],
                                  start=kc == 0, stop=kc == KC - 1)
                last.then_inc(s['f_h'], 1)

            def ffn_out(t, u):
                pe.wait_ge(s['f_hq'], t + 1)
                o = pb[4 + u][:].bitcast(bf16)
                for hc in range(HC):
                    last = tr(o[:, hc * P:(hc + 1) * P], h_q[u][:, hc * P:(hc + 1) * P], ident_b[:])
                last.then_inc(s['f_hqT_full'], 1)
                pe.wait_ge(s['f_hqT'], t + 1)
                pe.wait_ge(s['f_yout'], t)
                for hc in range(HC):
                    last = mm(pb[6][:, 0:D], h_qT[u][:, hc, :], w2T[:, hc, :], start=hc == 0, stop=hc == HC - 1)
                last.then_inc(s['f_y'], 1)

            ffn_in(0, 0, True)
            ffn_in(1, 1, True)
            ffn_out(0, 0)
            with pe.Fori(0, (T - 2) // 2) as i:
                for u in range(2):
                    ffn_in(i * 2 + (2 + u), u, False)
                    ffn_out(i * 2 + (1 + u), 1 - u)
            ffn_out(T - 1, 1)

            def proj_in(t, u):
                pe.wait_ge(s['l_xh'], t + 1)
                pe.wait_ge(s['l_xT'], t)
                for kc in range(KC):
                    last = tr(pb[0][:, kc * P:(kc + 1) * P], xn[:, u, kc * P:(kc + 1) * P], ident[:])
                last.then_inc(s['l_xT_full'], 1)

            def proj(t, u, first):
                pe.wait_ge(s['l_xT'], t + 1)
                if not first:
                    pe.wait_ge(s['l_qk'], t - 1)
                    pe.wait_ge(s['l_v'], t - 1)
                for o, a, n in ((pb[1 + 2 * u], 0, 2 * D), (pb[2 + 2 * u], 2 * D, D)):
                    for kc in range(KC):
                        last = mm(o[:, 0:n], xnT[:, kc, u * P:(u + 1) * P], wT[:, kc, a:a + n], start=kc == 0, stop=kc == KC - 1)
                last.then_inc(s['l_qkv'], 1)

            proj_in(0, 0)
            proj_in(1, 1)
            proj(0, 0, True)
            proj_in(2, 0)
            proj(1, 1, True)
            with pe.Fori(0, (T - 4) // 2) as i:
                for u in range(2):
                    proj_in(i * 2 + (3 + u), 1 - u)
                    proj(i * 2 + (2 + u), u, False)
            proj_in(T - 1, 1)
            proj(T - 2, 0, False)
            proj(T - 1, 1, False)

            TP = pb[7]
            KTILES = [(c * P, P) for c in range(TB)] + [(S, SK)]
            NU = 2 * len(KTILES)
            flat = lambda v: v.rearrange("p a b -> p (a b)")

            def claim(use):
                if not isinstance(use, int) or use > 0:
                    pe.wait_ge(s['t_free'], use)

            def turned(n, use, b, k):
                if k == 0:
                    pe.wait_ge(s['a_qk'], n + 1)
                claim(use + k)
                if k < 4:
                    src = q_dup if k < 2 else k_dup
                    for j in range(4):
                        last = tr(TP[:, j * P:(j + 1) * P], src[:, (k % 2) * 4 + j, :], ident[:])
                else:
                    last = tr(TP[:, 0:SK], k_dup[0:SK, TB, :], ident[0:SK, 0:SK])
                last.then_inc(s['t_full'], 1)

            def maxima(n, use, b, t):
                if t == 0:
                    pe.wait_ge(s['t_free'], use + 5)
                if t > 0 or not isinstance(n, int) or n > 0:
                    pe.wait_ge(s['a_mx_free'], n * TB + t)
                for a, w in ((0, 512), (512, 512), (S, SK + SK % 2)):
                    mm(banks[:, a:a + w], q_hi[b][:, t * P:(t + 1) * P], k_hl[b][:, a:a + w], start=True, stop=a < S)
                mm(banks[:, S:S + SK], ones_b[0:1, :], mask_row[0:1, b * SK:(b + 1) * SK], start=False, stop=True)\
                    .then_inc(s['a_mx_full'], 1)

            def minus(n, use, half):
                if half == 0:
                    pe.wait_ge(s['a_negm'], n + 1)
                claim(use + half)
                for j in range(4):
                    last = mm(TP[DH:DA, j * P:(j + 1) * P], negm[:, half * 4 + j:half * 4 + j + 1], ident[:], start=True, stop=True)
                last.then_inc(s['t_full'], 1)

            def scores(n, b, q):
                c, half = divmod(q, 2)
                a, w = KTILES[c]
                if q >= 2 or not isinstance(n, int) or n > 0:
                    pe.wait_ge(s['a_p'], n * NU + (q - 1))
                cols = slice(half * 512, (half + 1) * 512)
                mm(pb[3 + q % 2][0:w, :], k_hl[b][:, a:a + w], q_hi[b][:, cols], start=True, stop=False)
                mm(pb[3 + q % 2][0:w, :], k_hi[b][0:DA, a:a + w], q_lo[b][0:DA, cols], start=False, stop=True)\
                    .then_inc(s['a_s_full'], 1)

            def values(n, b, q):
                c, half = divmod(q, 2)
                a, w = KTILES[c]
                pe.wait_ge(s['a_p'], n * NU + (q + 1))
                mm(pb[5 + half][0:DA, :], vh[b][0:w, c, :], pT[q % 3][0:w, :], start=c == 0,
                   stop=c == len(KTILES) - 1).then_inc(s['a_pv'], 1)

            def joined(n, h, use, b, t):
                if t == 0:
                    pe.wait_ge(s['a_o'], n + 1)
                claim(use + t)
                mm(TP[:, 0:D + 1], oT[b][0:DA, t * P:(t + 1) * P], flat(woT[0:DA, bass.ds(h, 1), :]), start=True, stop=True)\
                    .then_inc(s['t_full'], 1)

            def step(n, b, h_last, use, first, last):
                pe.wait_ge(s['t_free'], use)
                pe.wait_ge(s['a_khi'], n + 1)
                pe.wait_ge(s['a_v'], n + 1)
                out_at = use if last else use + 5
                minus_at = use + 5 if first else use + 5 + TB
                scores(n, b, 0)
                for q in range(NU):
                    if q + 1 < NU:
                        scores(n, b, q + 1)
                    if q == 0 and not first:
                        pe.wait_ge(s['a_o'], n)
                    values(n, b, q)
                    if q < 5 and not last:
                        turned(n + 1, use, 1 - b, q)
                    if 5 <= q < 5 + TB:
                        if not last:
                            maxima(n + 1, use, 1 - b, q - 5)
                        if not first:
                            joined(n - 1, h_last, out_at, 1 - b, q - 5)
                    if q in (15, 16) and not last:
                        minus(n + 1, minus_at, q - 15)

            HEADS = B * NH
            USES = 5 + TB + 2
            for k in range(5):
                turned(0, 0, 0, k)
            pe.wait_ge(s['a_v'], 1)
            for t in range(TB):
                maxima(0, 0, 0, t)
            for half in range(2):
                minus(0, 5, half)
            step(0, 0, 0, 7, True, False)
            with pe.Fori(0, NH - 1) as i:
                step(i * 2 + 1, 1, i, i * (2 * USES) + (USES - 1), False, False)
                step(i * 2 + 2, 0, i, i * (2 * USES) + (2 * USES - 1), False, False)
            end = (HEADS - 1) * USES - 1
            step(HEADS - 1, 1, NH - 1, end, False, True)
            for t in range(TB):
                joined(HEADS - 1, NH - 1, end + TB, 1, t)

            GATES, PLACES = slice(0, T * E), T * E
            with pe.Fori(0, T // 4) as i:
                for u in range(4):
                    t = i * 4 + u
                    pe.wait_ge(s['r_x'], t + 1)
                    for kc in range(KC):
                        last = tr(pb[u][:, kc * P:(kc + 1) * P], xn[:, u, kc * P:(kc + 1) * P], ident[:])
                    last.then_inc(s['r_xT_full'], 1)
                for u in range(4):
                    t = i * 4 + u
                    pe.wait_ge(s['r_xT'], t + 1)
                    for kc in range(KC):
                        last = mm(pb[7][:, bass.ds(t * E, E)], xnT[:, kc, u * P:(u + 1) * P], gateT[:, kc, :],
                                  start=kc == 0, stop=kc == KC - 1)
                    last.then_inc(s['r_logit'], 1)

            def places():
                pe.wait_ge(s['r_sel'], 1)
                o = pb[7][:, PLACES:PLACES + (T + 1) * E]
                mm(o[:, 0:T * E], before[:], flat(sel_b), start=True, stop=False)
                mm(o[:, T * E:], ones_b[:], sel_b[:, 0, :], start=False, stop=False)
                for t in range(T):
                    n = T - max(t, 1)
                    later = o[:, (t + 1) * E:(t + 1 + n) * E].rearrange("p (a b) -> p a b", a=n)
                    last = mm(later, ones_b[:], sel_b[:, t:t + 1, :].to_broadcast([P, n, E]), start=False, stop=t == T - 1)
                last.then_inc(s['r_pos_full'], 1)

            def mixture(k, n, where, hot_of, split, between):
                def bring(t, u, turn):
                    pe.wait_ge(m_x[k][u], turn * 16 + 16)
                    pe.wait_ge(m[k]['xinT'], t)
                    for kc in range(KC):
                        last = tr(pb[4][:, kc * P:(kc + 1) * P], x_in[u][:, kc * P:(kc + 1) * P], ident[:])
                    last.then_inc(m[k]['xinT_full'], 1)

                def product(t, u, side, at):
                    for j, off in enumerate((OFF1, OFF3)):
                        o = pb[2 * side + j]
                        for kc in range(KC):
                            mm(o[:], x_inT[u][:, kc, :], halves(at, off, kc)[:, :, side], start=kc == 0, stop=False)
                        bb = bias_b[:, j * I2:(j + 1) * I2].rearrange("p (n two) -> p n two", two=2)
                        last = mm(o[:], hot_of(u)[0], bb[:, :, side], start=False, stop=True)
                    last.then_inc(m[k]['prod'], 1)

                def hidden_T(t):
                    pe.wait_ge(m[k]['hid'], t + 1)
                    for c in range(IC):
                        last = tr(pb[5][:, c * P:(c + 1) * P], h_moe[:, c * P:(c + 1) * P], ident[:])
                    last.then_inc(m[k]['hT_full'], 1)

                def second(t, u, at):
                    pe.wait_ge(m[k]['hT'], t + 1)
                    pe.wait_ge(m[k]['ysb'], t)
                    if k == 1:
                        pe.wait_ge(m[k]['hoty'], t + 1)
                    for c in range(IC):
                        mm(pb[6][:, 0:D], h_moeT[:, c, :], wexp[:, bass.ds(at + (OFF2 + c * D), D)], start=c == 0, stop=False)
                    mm(pb[6][:, 0:D], hot_of(u)[1], bias_b[:, 2 * I2:NB], start=False, stop=True).then_inc(m[k]['y'], 1)

                def step(t, u, turn, at_before, at, more):
                    first = at_before is None
                    pe.wait_ge(m[k]['xinT'], t + 1)
                    if k == 1:
                        pe.wait_ge(m[k]['hot'], t + 1)
                    pe.wait_ge(m[k]['gated'], t)
                    product(t, u, 0, at)
                    if not first:
                        hidden_T(t - 1)
                    pe.wait_ge(m[k]['lined'], t)
                    product(t, u, 1, at)
                    if more:
                        bring(t + 1, 1 - u, turn)
                    if not first:
                        second(t - 1, 1 - u, at_before)

                bring(0, 0, 0)
                step(0, 0, 0, None, where(0), True)
                pairs = (n - 2) // 2

                def pair(i):
                    at = [where(i * 2 + j) for j in range(3)]
                    for u in range(2):
                        step(i * 2 + (1 + u), 1 - u, i + 1, at[u], at[u + 1], True)

                with pe.Fori(0, split) as i:
                    pair(i)
                between()
                with pe.Fori(0, pairs - split) as i:
                    pair(i + split)
                for t in range(2 * pairs + 1, n):
                    step(t, t % 2, (t + 1) // 2, where(t - 1), where(t), t + 1 < n)
                hidden_T(n - 1)
                second(n - 1, (n - 1) % 2, where(n - 1))

            pe.wait_ge(s['ld_shared'], NLD['ld_shared'])
            pe.wait_ge(s['r_bias'], 1)
            pe.wait_ge(s['r_hot_sh'], 1)
            mixture(0, T, lambda t: SHARED_AT * WEXP, lambda u: (hot_sh[:], hot_sh[:]), PLACES_AT, places)
            pe.wait_ge(s['ld_e0'], NLD['ld_e0'])
            pe.wait_ge(s['ld_mid'], NLD['ld_mid'])
            pe.wait_ge(s['ld_late'], 3 * 16 * (E - 1 - NORM_AT))
            pe.wait_ge(s['r_slot'], 1)

            def slot_at(t):
                return pe.value_load(slot_i[0:1, bass.ds(t, 1)], min_val=0, max_val=E - 1) * WEXP

            OTHERS = T * (TOPK - 1)
            mixture(1, SLOTS, slot_at, lambda u: (hot_t[u][0:96, :], hot_y[u][0:96, :]), (OTHERS - 1) // 2,
                    lambda: pe.wait_ge(s['ld_last'], NLD['ld_last']))

        @block.scalar
        def _(act):
            a = nc.scalar.activation
            roots = [0]

            def root(n):
                act.wait_ge(s['root_in'], roots[0] + 1)
                a(root_s[:, 0:n], root_a[:, 0:n], ACT.Sqrt).then_inc(s['root_out'], 1)
                roots[0] += 1

            root(T + B)
            with act.Fori(0, T // 4) as it:
                act.wait_ge(s['g_xnT_full'], it + 1)
                a(xnT[:, 0, :], pb[0][:], ACT.Copy)
                a(xnT[:, 1, :], pb[1][:], ACT.Copy).then_inc(s['g_xnT'], 1)
                act.wait_ge(s['g_sh'], it + 1)
                a(p0[:].rearrange("p a b -> p (a b)"), p0[:].rearrange("p a b -> p (a b)"), ACT.Exp, scale=SCALE0)\
                    .then_inc(s['g_p'], 1)
            root(T)

            def ffn_T(t, u):
                act.wait_ge(s['f_xqT_full'], t + 1)
                a(xqT[u][:].rearrange("p a b -> p (a b)"), pb[7][:].bitcast(bf16)[:, 0:D], ACT.Copy).then_inc(s['f_xqT'], 1)

            def ffn_act(t, u):
                act.wait_ge(s['f_acc'], t + 1)
                a(h_f[u], h_f[u], ACT.Gelu).then_inc(s['f_amax'], 1)

            def ffn_quant(t, u):
                act.wait_ge(s['f_hqT_full'], t + 1)
                a(h_qT[u][:].rearrange("p a b -> p (a b)"), pb[4 + u][:].bitcast(bf16), ACT.Copy).then_inc(s['f_hqT'], 1)

            ffn_T(0, 0)
            with act.Fori(0, (T - 2) // 2) as i:
                for u in range(2):
                    ffn_act(i * 2 + u, u)
                    ffn_T(i * 2 + (1 + u), 1 - u)
                    ffn_quant(i * 2 + u, u)
            ffn_act(T - 2, 0)
            ffn_T(T - 1, 1)
            ffn_quant(T - 2, 0)
            ffn_act(T - 1, 1)
            ffn_quant(T - 1, 1)
            root(T)
            root(T)

            def proj_T(t, u, first):
                act.wait_ge(s['l_xT_full'], t + 1)
                if not first:
                    act.wait_ge(s['l_qkv'], t - 1)
                for kc in range(KC):
                    last = a(xnT[:, kc, u * P:(u + 1) * P], pb[0][:, kc * P:(kc + 1) * P], ACT.Identity,
                             scale=lg[:, kc:kc + 1], bias=lb[:, kc:kc + 1])
                last.then_inc(s['l_xT'], 1)

            def proj_qk(t, u):
                act.wait_ge(s['l_qkv'], t + 1)
                act.wait_ge(s['const'], 2)
                a(qkv[:, bass.ds(t, 1), 0:2 * D].rearrange("p a d -> p (a d)"), pb[1 + 2 * u][:], ACT.Copy)\
                    .then_inc(s['l_qk'], 1)

            proj_T(0, 0, True)
            proj_T(1, 1, True)
            with act.Fori(0, (T - 2) // 2) as i:
                for u in range(2):
                    proj_qk(i * 2 + u, u)
                    proj_T(i * 2 + (2 + u), u, False)
            proj_qk(T - 2, 0)
            proj_qk(T - 1, 1)
            root(T * 2 * NH + 2 * NH)

            NU = 2 * (TB + 1)
            HEADS, USES = B * NH, 5 + TB + 2

            def high(n, use, b, k):
                act.wait_ge(s['t_full'], use + (k + 1))
                act.wait_ge(s['const'], 2)
                dst, gam = ((q_hi[b][:, (k % 2) * 512:(k % 2 + 1) * 512], qg) if k < 2 else
                            (k_hl[b][:, (k - 2) * 512:min((k - 1) * 512, S + SK)], kg))
                a(dst, pb[7][:, 0:dst.shape[-1]], ACT.Copy, scale=gam[:, :]).then_inc(s['a_hi'], 1)

            def minus(use, b, half):
                act.wait_ge(s['t_full'], use + (half + 1))
                a(q_lo[b][DH:DA, half * 512:(half + 1) * 512], pb[7][DH:DA, :], ACT.Copy).then_inc(s['t_free'], 1)

            def step(n, b, use, first, last):
                minus_at = use + 5 if first else use + 5 + TB
                for q in range(NU):
                    act.wait_ge(s['a_s_full'], n * NU + (q + 1))
                    if q >= 3 or not first:
                        act.wait_ge(s['a_pv'], n * NU + (q - 2))
                    if q < 2 * TB:
                        a(pT[q % 3], pb[3 + q % 2][:], ACT.Exp).then_inc(s['a_p'], 1)
                    else:
                        a(pT[q % 3][0:SK, :], pb[3 + q % 2][0:SK, :], ACT.Exp, bias=mask_col[:, b:b + 1]).then_inc(s['a_p'], 1)
                    if 1 <= q <= 5 and not last:
                        high(n + 1, use, 1 - b, q - 1)
                    if q in (16, 17) and not last:
                        minus(minus_at, 1 - b, q - 16)
                act.wait_ge(s['a_pv'], n * NU + NU)
                a(oT[b][0:DA, 0:512], pb[5][0:DA, :], ACT.Copy)
                a(oT[b][0:DA, 512:S], pb[6][0:DA, :], ACT.Copy).then_inc(s['a_o'], 1)

            for k in range(5):
                high(0, 0, 0, k)
            for half in range(2):
                minus(5, 0, half)
            step(0, 0, 7, True, False)
            with act.Fori(0, NH - 1) as i:
                step(i * 2 + 1, 1, i * (2 * USES) + (USES - 1), False, False)
                step(i * 2 + 2, 0, i * (2 * USES) + (2 * USES - 1), False, False)
            step(HEADS - 1, 1, (HEADS - 1) * USES - 1, False, True)

            root(T)
            with act.Fori(0, T // 4) as i:
                for u in range(4):
                    t = i * 4 + u
                    act.wait_ge(s['r_xT_full'], t + 1)
                    act.wait_ge(s['r_logit'], i * 4)
                    a(xnT[:, :, u * P:(u + 1) * P], pb[u][:, 0:D].rearrange("p (a b) -> p a b", a=KC), ACT.Copy).then_inc(s['r_xT'], 1)
            act.wait_ge(s['r_e'], 1)
            a(score[:], score[:], ACT.Exp).then_inc(s['r_exp'], 1)

            def mixture(k, n):
                def tokens(t, u):
                    act.wait_ge(m[k]['xinT_full'], t + 1)
                    a(x_inT[u][:].rearrange("p a b -> p (a b)"), pb[4][:, 0:D], ACT.Copy).then_inc(m[k]['xinT'], 1)

                def lifted(t, side):
                    act.wait_ge(m[k]['prod'], t * 2 + (1 + side))
                    act.wait_ge(m[k]['lined' if side else 'gated'], t)
                    a(lift[side], pb[2 * side + 1][:], ACT.Copy).then_inc(m[k]['lifted'], 1)

                def hidden(t):
                    act.wait_ge(m[k]['hT_full'], t + 1)
                    a(h_moeT[:].rearrange("p a b -> p (a b)"), pb[5][:], ACT.Copy).then_inc(m[k]['hT'], 1)

                def result(t, u, turn):
                    act.wait_ge(m_st[k][u], turn * 16)
                    act.wait_ge(m[k]['y'], t + 1)
                    a(y_sb[u], pb[6][:, 0:D], ACT.Copy).then_inc(m[k]['ysb'], 1)

                def step(t, u, turn, first, more):
                    lifted(t, 0)
                    if not first:
                        hidden(t - 1)
                    act.wait_ge(m[k]['gated'], t + 1)
                    a(sig, gate, ACT.Sigmoid, scale=ALPHA).then_inc(m[k]['sigd'], 1)
                    lifted(t, 1)
                    if more:
                        tokens(t + 1, 1 - u)
                    if not first and k == 1:
                        result(t - 1, 1 - u, turn)

                tokens(0, 0)
                step(0, 0, 0, True, True)
                pairs = (n - 2) // 2
                with act.Fori(0, pairs) as i:
                    for u in range(2):
                        step(i * 2 + (1 + u), 1 - u, i, False, True)
                for t in range(2 * pairs + 1, n):
                    step(t, t % 2, (t - 1) // 2, False, t + 1 < n)
                hidden(n - 1)
                if k == 1:
                    result(n - 1, (n - 1) % 2, (n - 1) // 2)

            mixture(0, T)
            mixture(1, SLOTS)

        @block.vector
        def _(ve):
            v = nc.vector
            link = Chain(ve, s['chain'])
            roots = [0]
            units = [0]

            def norm(n, guard):
                ve.wait_ge(s['root_out'], roots[0] + 1)
                roots[0] += 1
                r, q, t_, d = root_a[:, 0:n], root_s[:, 0:n], root_t[:, 0:n], rstd[:, 0:n]
                link(v.tensor_scalar(t_, q, 1e-30, None, ALU.max))
                link(v.reciprocal(d, t_))
                link(v.tensor_tensor(t_, r, d, ALU.mult))
                link(v.tensor_tensor(t_, t_, q, ALU.add))
                link(v.tensor_scalar(t_, t_, 0.5, guard, ALU.mult, ALU.max))
                link(v.reciprocal(d, t_))

            def filled():
                units[0] += 1
                ve.wait_ge(s['prep_full'], units[0])
                return pb[(units[0] - 1) % 2]

            ve.wait_ge(s['const'], 2)
            link(v.tensor_scalar(eno_i[:], eno_i[:], 31, None, ALU.bitwise_and))
            link(v.tensor_copy(eno[:], eno_i[:]))
            link(v.tensor_scalar(eno_sh[:], eno[:], float(SHARED), None, ALU.is_equal))
            v.tensor_copy(hot_sh[:], eno_sh[0:96, 0:1].to_broadcast([96, P])).then_inc(s['r_hot_sh'], 1)
            ve.wait_ge(s['ld_x'], NLD['ld_x'])
            with ve.Fori(0, T) as t:
                last = v.bn_stats(stats[:, bass.ds(t, 1), :].rearrange("p a d -> p (a d)"),
                                  x_sb[:, bass.ds(t, 1), :].rearrange("p a d -> p (a d)"))
                link.loop(t, 1)
                link(last)
            link.done(T)

            def aggregate():
                for t in range(T):
                    last = v.bn_aggr(mv[:, t, :], stats[:, t, :])
                link(last)

            aggregate()
            ve.wait_ge(s['ld_l0'], NLD['ld_l0'])
            for b in range(B):
                link(v.bn_stats(root_t[0:SK, 8 * b:8 * b + 6], ctx_sb[0:SK, b, :]))
                link(v.bn_aggr(mv[0:SK, T + b, :], root_t[0:SK, 8 * b:8 * b + 6]))
            v.tensor_scalar(root_a[:, 0:T + B], mv[:, :, 1], LN_EPS, None, ALU.add).then_inc(s['root_in'], 1)
            norm(T + B, 0.0)
            for b in range(B):
                last = v.tensor_scalar(xn[0:SK, b, 0:DC], ctx_sb[0:SK, b, :], mv[0:SK, T + b, 0:1], rstd[0:SK, T + b:T + b + 1],
                                       ALU.subtract, ALU.mult)
            link(last)
            free = lambda ins: ins.then_inc(s['prep_free'], 1)
            flat = lambda ap: ap.rearrange("p a b -> p (a b)")
            o = filled()
            free(v.tensor_copy(flat(l0_wqT[:]), o[:]))
            o = filled()
            v.tensor_copy(ctxT[:, 0, :], o[:, 0:SKB])
            free(v.tensor_copy(ctxT[0:DCR, 1, :], o[0:DCR, SKB:2 * SKB]))
            for dst, bias in ((kT0, bk0), (vT0, bv0)):
                o = filled()
                for ec in range(KC):
                    last = v.tensor_scalar(dst[:, ec, :], o[:, ec * SKB:(ec + 1) * SKB], bias[:, ec:ec + 1], None, ALU.add)
                free(last)
            o = filled()
            v.tensor_copy(flat(m0[:]), o[:, 0:KC * SKB])
            free(v.tensor_copy(c0[0:1, :], o[0:1, KC * SKB:(KC + 1) * SKB]))
            o = filled()
            free(v.tensor_copy(vv0[0:SK].rearrange("p a b -> p (a b)"), o[0:SK, 0:B * D]))
            ve.wait_ge(s['ld_ffn'], NLD['ld_ffn'])
            v.tensor_reduce(wsum[:, 0:1], w1_raw[:], AX.XY, ALU.add, apply_absolute_value=True)
            v.tensor_reduce(wsum[:, 1:2], w2_raw[:], AX.XY, ALU.add, apply_absolute_value=True).then_inc(s['f_pre'], 1)
            o = filled()
            v.tensor_scalar(wsc, o[:, 0:2], 1.0 / (HID * D), QEPS, ALU.mult, ALU.max).then_inc(s['prep_free'], 1)
            ve.wait_ge(s['prep_free'], units[0])
            link(v.reciprocal(winv, wsc))
            for k, (raw, q) in enumerate(((w1_raw, w1_t), (w2_raw, w2_t))):
                link(v.tensor_scalar(raw[:], raw[:], winv[:, k:k + 1], MAGIC, ALU.mult, ALU.add))
                link(v.tensor_scalar(raw[:], raw[:], MAGIC, 1.0, ALU.subtract, ALU.min))
                v.tensor_scalar(q, raw[:], -1.0, None, ALU.max).then_inc(s['f_pre'], 1)
            for kc in range(KC):
                o = filled()
                free(v.tensor_copy(w1T[:, kc, :], o[:].bitcast(bf16)))
            for half in range(2):
                o = filled()
                n = HC // 2
                free(v.tensor_copy(flat(w2T[:, half * n:(half + 1) * n, :]), o[:].bitcast(bf16)))
            o = filled()
            free(v.tensor_copy(wT[:, :, 0:D], o[:].rearrange("p (a b) -> p a b", a=KC)))
            for kc in range(KC):
                o = filled()
                free(v.tensor_copy(wT[:, kc, D:QKV], o[:]))
            for kc, n in ((0, P), (1, DCR)):
                o = filled()
                free(v.tensor_copy(wcT[0:n, kc, :], o[0:n, :]))
            for hp in range(NH // 2):
                o = filled()
                free(v.tensor_copy(woT[0:DH, 2 * hp:2 * hp + 2, 0:D], o[0:DH, :].rearrange("p (a b) -> p a b", a=2)))
            o = filled()
            free(v.tensor_copy(flat(gateT[:]), o[:, 0:KC * E]))
            v.tensor_scalar(mask_row[:], mask_u[0:1, :], BIG, -BIG, ALU.mult, ALU.add)
            v.tensor_scalar(mask_col[:], maskc_u[:], BIG, -BIG, ALU.mult, ALU.add).then_inc(s['f_pre'], 1)
            o = filled()
            v.tensor_scalar(ctxT[:, 0, :], o[:, 0:SKB], xg[:, 0:1], xb[:, 0:1], ALU.mult, ALU.add)
            free(v.tensor_scalar(ctxT[0:DCR, 1, :], o[0:DCR, SKB:2 * SKB], xg[0:DCR, 1:2], xb[0:DCR, 1:2], ALU.mult, ALU.add))
            for b in range(B):
                o = filled()
                free(v.tensor_copy(ckv[0:SK, b, :], o[0:SK, :]))
            ve.wait_ge(s['prep_free'], units[0])

            def tile(t):
                return x_sb[:, bass.ds(t, 1), :].rearrange("p a d -> p (a d)")

            def col(ap, t):
                return ap[:, bass.ds(t, 1)]

            def statistics(t):
                return v.bn_stats(stats[:, bass.ds(t, 1), :].rearrange("p a d -> p (a d)"), tile(t))

            def normalise(dst, t):
                return v.tensor_scalar(dst, tile(t), mv[:, bass.ds(t, 1), 0:1].rearrange("p a d -> p (a d)"), col(rstd, t),
                                       ALU.subtract, ALU.mult)

            with ve.Fori(0, T // 4) as it:
                link.loop(it, 5)
                for u in range(4):
                    last = normalise(xn[:, u, :], it * 4 + u)
                last.then_inc(s['g_xn'], 1)
                ve.wait_ge(s['g_sc'], it + 1)
                sc = pb[2][:, 0:4 * SK].rearrange("p (a b) -> p a b", a=4)
                link(v.tensor_reduce(mx4, sc, AX.X, ALU.max))
                v.tensor_tensor(p0[:], sc, mx4.unsqueeze(2).to_broadcast([P, 4, SK]), ALU.subtract).then_inc(s['g_sh'], 1)
                ve.wait_ge(s['g_p'], it + 1)
                link(v.tensor_reduce(sums4, p0[:], AX.X, ALU.add))
                link(v.reciprocal(sums4, sums4))
                ve.wait_ge(s['g_pT_full'], it + 1)
                v.tensor_copy(p0T[0:SK, :], pb[3][0:SK, :]).then_inc(s['g_pT'], 1)
                ve.wait_ge(s['g_av'], it + 1)
                for u in range(4):
                    last = v.scalar_tensor_tensor(tile(it * 4 + u), pb[4 + u // 2][:, (u % 2) * D:(u % 2 + 1) * D],
                                                  sums4[:, u:u + 1], tile(it * 4 + u), ALU.mult, ALU.add)
                link(last)
                for u in range(4):
                    last = statistics(it * 4 + u)
                link(last)
            link.done(T // 4)
            aggregate()
            v.tensor_scalar(root_a[:, 0:T], mv[:, 0:T, 1], LN_EPS, None, ALU.add).then_inc(s['root_in'], 1)
            norm(T, 0.0)

            def ffn_quantise(t, u):
                link(normalise(xn[:, u, :], t))
                link(v.tensor_reduce(amax[:, u:u + 1], xn[:, u, :], AX.X, ALU.max, apply_absolute_value=True))
                link(v.tensor_scalar(aden[:, u:u + 1], amax[:, u:u + 1], QEPS, None, ALU.max))
                link(v.reciprocal(arow[:, u:u + 1], aden[:, u:u + 1]))
                link(v.tensor_scalar(arow[:, u:u + 1], arow[:, u:u + 1], QB, None, ALU.mult))
                link(v.tensor_scalar(xn[:, u, :], xn[:, u, :], arow[:, u:u + 1], MAGIC, ALU.mult, ALU.add))
                v.tensor_scalar(aden[:, u:u + 1], aden[:, u:u + 1], wsc[:, 0:1], 1.0 / QB, ALU.mult, ALU.mult)
                v.tensor_scalar(xq[u][:], xn[:, u, :], MAGIC, QB, ALU.subtract, ALU.min).then_inc(s['f_xq'], 1)

            def ffn_hidden(t, u):
                ve.wait_ge(s['f_h'], t + 1)
                for half in range(2):
                    c = slice(half * 512, (half + 1) * 512)
                    last = v.scalar_tensor_tensor(h_f[u][:, c], pb[2 * u + half][:], aden[:, u:u + 1], b1_all[:, c], ALU.mult, ALU.add)
                last.then_inc(s['f_acc'], 1)

            def ffn_requantise(t, u):
                ve.wait_ge(s['f_amax'], t + 1)
                link(v.tensor_reduce(hmax[:, u:u + 1], h_f[u], AX.X, ALU.max, apply_absolute_value=True))
                link(v.tensor_scalar(hden[:, u:u + 1], hmax[:, u:u + 1], QEPS, None, ALU.max))
                link(v.reciprocal(hrow[:, u:u + 1], hden[:, u:u + 1]))
                link(v.tensor_scalar(hrow[:, u:u + 1], hrow[:, u:u + 1], QB, None, ALU.mult))
                link(v.tensor_scalar(h_f[u], h_f[u], hrow[:, u:u + 1], MAGIC, ALU.mult, ALU.add))
                v.tensor_scalar(hden[:, u:u + 1], hden[:, u:u + 1], wsc[:, 1:2], 1.0 / QB, ALU.mult, ALU.mult)
                v.tensor_scalar(h_q[u], h_f[u], MAGIC, QB, ALU.subtract, ALU.min).then_inc(s['f_hq'], 1)

            def ffn_finish(t, u):
                ve.wait_ge(s['f_y'], t + 1)
                ve.wait_ge(s['f_b2'], t + 1)
                v.scalar_tensor_tensor(tile(t), pb[6][:, 0:D], hden[:, u:u + 1], tile(t), ALU.mult, ALU.add)\
                    .then_inc(s['f_yout'], 1)
                ve.wait_ge(s['f_yout'], t + 1)
                link(statistics(t))

            ffn_quantise(0, 0)
            ffn_quantise(1, 1)
            ffn_hidden(0, 0)
            ffn_requantise(0, 0)
            with ve.Fori(0, (T - 2) // 2) as i:
                link.loop(i, 24)
                for u in range(2):
                    ffn_quantise(i * 2 + (2 + u), u)
                    ffn_hidden(i * 2 + (1 + u), 1 - u)
                    ffn_finish(i * 2 + u, u)
                    ffn_requantise(i * 2 + (1 + u), 1 - u)
            link.done((T - 2) // 2)
            ffn_hidden(T - 1, 1)
            ffn_finish(T - 2, 0)
            ffn_requantise(T - 1, 1)
            ffn_finish(T - 1, 1)
            aggregate()

            link(v.tensor_scalar(root_a[:, 0:T], mv[:, 0:T, 1], LN_EPS, None, ALU.add))
            v.tensor_copy(root_t[:, 0:1], root_a[:, 0:1]).then_inc(s['root_in'], 1)
            norm(T, 0.0)
            r1 = stats.rearrange("p a b -> p (a b)")[:, 0:T]
            link(v.tensor_copy(r1, rstd[:, 0:T]))
            link(v.tensor_tensor(root_t[:, 0:T], r1, r1, ALU.mult))
            link(v.tensor_tensor(root_t[:, 0:T], root_t[:, 0:T], mv[:, 0:T, 1], ALU.mult))
            v.tensor_scalar(root_a[:, 0:T], root_t[:, 0:T], LN_EPS, None, ALU.add).then_inc(s['root_in'], 1)
            norm(T, 0.0)
            link(v.tensor_tensor(rstd[:, 0:T], rstd[:, 0:T], r1, ALU.mult))
            sq = [oT[0][:, 0:512], oT[1][:, 0:512]]

            def proj_tokens(t, u):
                normalise(xn[:, u, :], t).then_inc(s['l_xh'], 1)

            def proj_kept(t, u):
                ve.wait_ge(s['l_qkv'], t + 1)
                v.tensor_copy(qkv[:, bass.ds(t, 1), 2 * D:QKV].rearrange("p a d -> p (a d)"), pb[2 + 2 * u][:, 0:D]).then_inc(s['l_v'], 1)
                ve.wait_ge(s['l_qk'], t + 1)
                qk = qkv[:, bass.ds(t, 1), 0:2 * D].rearrange("p a d -> p (a d)")
                link(v.tensor_tensor(sq[u], qk, qk, ALU.mult))
                v.tensor_reduce(ss_l[:, bass.ds(t * (2 * NH), 2 * NH)], sq[u].rearrange("p (a b) -> p a b", a=2 * NH), AX.X, ALU.add)

            ss_l = p0[:].rearrange("p a b -> p (a b)")
            NSS = T * 2 * NH + 2 * NH
            link(v.memset(ss_l[:, 0:NSS], 1.0))
            ve.wait_ge(s['prep_free'], units[0])
            for b in range(B):
                link(v.tensor_tensor(sq[b][0:SK, 0:D], ckv[0:SK, b, 0:D], ckv[0:SK, b, 0:D], ALU.mult))
                v.tensor_reduce(ss_l[0:SK, T * 2 * NH + b * NH:T * 2 * NH + (b + 1) * NH],
                                sq[b][0:SK, 0:D].rearrange("p (a b) -> p a b", a=NH), AX.X, ALU.add)
            proj_tokens(0, 0)
            proj_tokens(1, 1)
            with ve.Fori(0, (T - 2) // 2) as i:
                link.loop(i, 2)
                for u in range(2):
                    ve.wait_ge(s['l_xT'], i * 2 + (u + 1))
                    proj_tokens(i * 2 + (2 + u), u)
                    proj_kept(i * 2 + u, u)
            link.done((T - 2) // 2)
            proj_kept(T - 2, 0)
            proj_kept(T - 1, 1)
            v.tensor_copy(mx4[:, 1:2], hden[:, 0:1]).then_inc(s['l_free'], 1)
            link(v.tensor_copy(mx4[:, 0:1], hden[:, 0:1]))
            v.tensor_scalar(root_a[:, 0:NSS], ss_l[:, 0:NSS], 1.0 / DH, None, ALU.mult).then_inc(s['root_in'], 1)
            norm(NSS, RMS_EPS)
            rq = rstd[:, 0:T * 2 * NH].rearrange("p (a b) -> p a b", a=T)
            link(v.tensor_scalar(rq[:, :, 0:NH], rq[:, :, 0:NH], float(DH) ** -0.5, None, ALU.mult))

            HEADS, USES = B * NH, 5 + TB + 2
            ve.wait_ge(s['l_bo'], T)

            def scaled(h, b):
                for dst, a0, r0 in ((q_dup, 0, 0), (k_dup[:, 0:TB, :], D, NH)):
                    src = qkv[:, b * TB:(b + 1) * TB, bass.ds(h * DH + a0, DH)].unsqueeze(2).to_broadcast([P, TB, 2, DH])
                    r = rq[:, b * TB:(b + 1) * TB, bass.ds(h + r0, 1)].unsqueeze(2).to_broadcast([P, TB, 2, DH])
                    v.tensor_tensor(dst.rearrange("p t (a d) -> p t a d", a=2), src, r, ALU.mult)
                rc = rstd[0:SK, bass.ds(h + (b * NH + T * 2 * NH), 1)]
                csrc = ckv[0:SK, b, bass.ds(h * DH, DH)].unsqueeze(1).to_broadcast([SK, 2, DH])
                v.tensor_scalar(k_dup[0:SK, TB, :].rearrange("p (a d) -> p a d", a=2), csrc, rc, None, ALU.mult)\
                    .then_inc(s['a_qk'], 1)

            def low(n, b, k):
                ve.wait_ge(s['a_hi'], n * 5 + (k + 1))
                if k < 2:
                    hi, dst, src, gam = q_hi[b][0:DH], q_lo[b][0:DH], pb[7][0:DH], qg[0:DH, :]
                else:
                    hi, dst, src, gam = k_hl[b][DH:P], k_hl[b][DH:P], pb[7][DH:P], kg[DH:P, :]
                at = slice((k % 2) * 512, (k % 2 + 1) * 512) if k < 4 else slice(S, S + SK)
                v.scalar_tensor_tensor(dst[:, at], src[:, 0:at.stop - at.start], gam, hi[:, at].bitcast(f32), ALU.mult, ALU.subtract)\
                    .then_inc(s['t_free'], 1)

            def maximum(n, t):
                ve.wait_ge(s['a_mx_full'], n * TB + (t + 1))
                v.tensor_reduce(mx8[:, t:t + 1], banks[:, 0:S + SK], AX.X, ALU.max).then_inc(s['a_mx_free'], 1)

            def minus(n):
                ve.wait_ge(s['a_mx_free'], n * TB + TB)
                v.tensor_scalar(negm, mx8, -1.0, None, ALU.mult).then_inc(s['a_negm'], 1)

            def joined(use, b, t):
                ve.wait_ge(s['t_full'], use + (t + 1))
                link(v.reciprocal(yden[:, 0:1], pb[7][:, D:D + 1]))
                x_t = x_sb[:, b * TB + t, :]
                v.scalar_tensor_tensor(x_t, pb[7][:, 0:D], yden[:, 0:1], x_t, ALU.mult, ALU.add).then_inc(s['t_free'], 1)

            def step(n, b, use, h_next, first, last, more):
                if not last:
                    for k in range(5):
                        low(n + 1, 1 - b, k)
                for t in range(TB):
                    if not last:
                        maximum(n + 1, t)
                    if not first:
                        joined(use if last else use + 5, 1 - b, t)
                if not last:
                    minus(n + 1)
                if more:
                    scaled(h_next, b)

            scaled(0, 0)
            for k in range(5):
                low(0, 0, k)
            ve.wait_ge(s['t_free'], 5)
            scaled(0, 1)
            for t in range(TB):
                maximum(0, t)
            minus(0)
            step(0, 0, 7, 1, True, False, True)
            with ve.Fori(0, NH - 2) as i:
                link.loop(i, 2 * TB)
                step(i * 2 + 1, 1, i * (2 * USES) + (USES - 1), i + 1, False, False, True)
                step(i * 2 + 2, 0, i * (2 * USES) + (2 * USES - 1), i + 2, False, False, True)
            link.done(NH - 2)
            end = (HEADS - 3) * USES - 1
            step(HEADS - 3, 1, end, NH - 1, False, False, True)
            step(HEADS - 2, 0, end + USES, None, False, False, False)
            end += 2 * USES
            step(HEADS - 1, 1, end, None, False, True, False)
            for t in range(TB):
                joined(end + TB, 1, t)
            ve.wait_ge(s['t_free'], end + 2 * TB)
            v.tensor_copy(mx4[:, 0:1], yden[:, 0:1]).then_inc(s['a_oT'], 1)

            ve.wait_ge(s['a_oT'], 1)
            with ve.Fori(0, T) as t:
                link.loop(t, 1)
                link(statistics(t))
            link.done(T)
            aggregate()
            v.tensor_scalar(root_a[:, 0:T], mv[:, 0:T, 1], LN_EPS, None, ALU.add).then_inc(s['root_in'], 1)
            norm(T, 0.0)
            with ve.Fori(0, T // 4) as i:
                for u in range(4):
                    ve.wait_ge(s['r_xm'], i * 4)
                    ve.wait_ge(s['r_xT_full'], i * 4)
                    normalise(xn[:, u, :], i * 4 + u).then_inc(s['r_x'], 1)

            wide = lambda ap: ap.unsqueeze(2).to_broadcast([P, T, E])
            ve.wait_ge(s['r_logit'], T)
            lg3 = pb[7][:, 0:T * E].rearrange("p (a b) -> p a b", a=T)
            link(v.tensor_reduce(den16, lg3, AX.X, ALU.max))
            v.tensor_tensor(score[:], lg3, wide(den16), ALU.subtract).then_inc(s['r_e'], 1)
            ve.wait_ge(s['r_exp'], 1)
            link(v.tensor_reduce(den16, score[:], AX.X, ALU.add))
            link(v.reciprocal(den16, den16))
            link(v.tensor_tensor(score[:], score[:], wide(den16), ALU.mult))
            link(v.tensor_tensor(biased[:], score[:], gateb[:].unsqueeze(1).to_broadcast([P, T, E]), ALU.add))
            ve.wait_ge(s['r_table'], 1)
            bg1 = big1.rearrange("p (t e) f -> p t e f", t=T)
            bg2 = big2.rearrange("p (t e) f -> p t e f", t=T)
            theirs = biased[:].unsqueeze(2).to_broadcast([P, T, E, E])
            mine = biased[:].unsqueeze(3).to_broadcast([P, T, E, E])
            v.tensor_tensor(bg1, theirs, mine, ALU.is_gt)
            link(v.tensor_tensor(bg2, theirs, mine, ALU.is_equal))
            link(v.tensor_tensor(bg2, bg2, lower[:].unsqueeze(1).to_broadcast([P, T, E, E]), ALU.mult))
            link(v.tensor_tensor(bg1, bg1, bg2, ALU.add))
            link(v.tensor_reduce(rank[:], bg1, AX.X, ALU.add))
            v.tensor_scalar(sel_b[:], rank[:], float(TOPK), None, ALU.is_lt).then_inc(s['r_sel'], 1)
            for c in range(TOPK):
                v.tensor_scalar(chosen[c][:], rank[:], float(c), None, ALU.is_equal)

            def places():
                ve.wait_ge(s['r_pos_full'], 1)
                link(v.tensor_copy(flat(pos[:]), pb[7][:, T * E:(2 * T + 1) * E]))
                link(v.tensor_scalar(ntile, pos[:, T, :], 1.0 / P, 0.5 - 0.5 / P, ALU.mult, ALU.add))
                link(v.tensor_scalar(ntile_r, ntile, MAGIC, None, ALU.add))
                link(v.tensor_scalar(ntile, ntile_r, MAGIC, None, ALU.subtract))
                link(v.tensor_tensor_scan(tend, ones[:, 0:E], ntile, 0.0, ALU.mult, ALU.add))
                link(v.tensor_tensor(tstart, tend, ntile, ALU.subtract))
                link(v.tensor_scalar(tstart, tstart, float(P), None, ALU.mult))
                v.tensor_copy(mx4[:, 0:1], tstart[:, 0:1]).then_inc(s['r_start'], 1)
                link(v.tensor_tensor(slot_cmp[:], tend.unsqueeze(1).to_broadcast([P, SLOTS, E]),
                                     slot_no.unsqueeze(2).to_broadcast([P, SLOTS, E]), ALU.is_le))
                link(v.tensor_reduce(slot_e[:], slot_cmp[:], AX.X, ALU.add))
                link(v.tensor_scalar(slot_e[:], slot_e[:], float(E - 1), None, ALU.min))
                link(v.tensor_copy(slot_i[:], slot_e[0:1, :]))
                v.tensor_scalar(hot[:], slot_e[0:96, :], eno[0:96, 0:1], None, ALU.is_equal).then_inc(s['r_slot'], 1)

            def mixture(k, n, split, between):
                def step(t):
                    ve.wait_ge(m[k]['lifted'], t * 2 + 1)
                    ve.wait_ge(m[k]['hid'], t)
                    link(v.tensor_tensor(gate, pb[0][:], lift[0], ALU.mult))
                    v.tensor_scalar(gate, gate, LIMIT, None, ALU.min).then_inc(m[k]['gated'], 1)
                    ve.wait_ge(m[k]['lifted'], t * 2 + 2)
                    link(v.tensor_tensor(line, pb[2][:], lift[1], ALU.mult))
                    v.tensor_scalar(line, line, LIMIT, -LIMIT, ALU.min, ALU.max).then_inc(m[k]['lined'], 1)
                    ve.wait_ge(m[k]['sigd'], t + 1)
                    link(v.tensor_tensor(sig, sig, gate, ALU.mult))
                    ve.wait_ge(m[k]['hT_full'], t)
                    v.scalar_tensor_tensor(h_moe, line, 1.0, sig, ALU.add, ALU.mult).then_inc(m[k]['hid'], 1)

                def result(t):
                    ve.wait_ge(m[k]['y'], t + 1)
                    v.tensor_tensor(tile(t), tile(t), pb[6][:, 0:D], ALU.add).then_inc(m[k]['ysb'], 1)

                step(0)
                for a0, a1 in ((0, split), (split, n - 1))[0:1 + (split < n - 1)]:
                    with ve.Fori(0, a1 - a0) as i:
                        link.loop(i, 3)
                        step(i + (a0 + 1))
                        if k == 0:
                            result(i + a0)
                    link.done(a1 - a0)
                    if a1 < n - 1:
                        between()
                if k == 0:
                    result(n - 1)

            mixture(0, T, 2 * PLACES_AT, places)
            mixture(1, SLOTS, SLOTS - 1, None)
            for t in range(T):
                u = t % DEEP
                ve.wait_ge(c_y[u], 16 * TOPK * (t // DEEP + 1))
                link(v.scalar_tensor_tensor(x_sb[:, t, :], y_of[u][0], route[:, 2, t:t + 1], x_sb[:, t, :], ALU.mult, ALU.add))
                v.scalar_tensor_tensor(x_sb[:, t, :], y_of[u][1], route[:, 3, t:t + 1], x_sb[:, t, :], ALU.mult, ALU.add)\
                    .then_inc(c_used, 1)


def kernel(**inputs):
    import concourse.bacc as _bacc
    from concourse.bass_utils import run_bass_kernel_spmd as _run

    nc = _bacc.Bacc("TRN2", target_bir_lowering=False, num_devices=1)
    arrays, args = {}, {}
    for name in _INS:
        a = np.ascontiguousarray(inputs[name])
        if a.dtype == np.bool_:
            a = a.astype(np.int32)
        arrays[f"in_{name}"] = a
        args[name] = nc.dram_tensor(f"in_{name}", a.shape, mybir.dt.from_np(a.dtype), kind="ExternalInput").ap()
    out = nc.dram_tensor("out", inputs['x'].shape, mybir.dt.float32, kind="ExternalOutput").ap()
    program(nc, args, out)
    r = _run(nc, [arrays], core_ids=[0])
    return r.results[0]["out"]
```

```python
import concourse.bass as bass
from concourse import mybir
from contextlib import ExitStack
import numpy as np

_INS = ['x', 'ctx_768', 'mask_BxS2_bk0', 'L0_xattn_Wq', 'L0_xattn_bq', 'L0_xattn_Wk', 'L0_xattn_bk', 'L0_xattn_Wv',
        'L0_xattn_bv', 'L0_xattn_Wo', 'L0_xattn_bo', 'L0_ffn_W1', 'L0_ffn_b1', 'L0_ffn_W2', 'L0_ffn_b2',
        'L1_xattn_ln_x_g', 'L1_xattn_ln_x_b', 'L1_xattn_ln_l_g', 'L1_xattn_ln_l_b', 'L1_xattn_qn_g', 'L1_xattn_kn_g',
        'L1_xattn_Wq', 'L1_xattn_Wkv', 'L1_xattn_Wlkv', 'L1_xattn_Wo', 'L1_xattn_bo', 'L1_ffn_gate_w', 'L1_ffn_gate_b',
        'L1_ffn_w1', 'L1_ffn_b1', 'L1_ffn_w3', 'L1_ffn_b3', 'L1_ffn_w2', 'L1_ffn_b2', 'L1_ffn_sw1', 'L1_ffn_sb1',
        'L1_ffn_sw3', 'L1_ffn_sb3', 'L1_ffn_sw2', 'L1_ffn_sb2']


class Chain:

    def __init__(self, eng, sem):
        self.eng, self.sem, self.base, self.n, self.at, self.per = eng, sem, 0, 0, None, 0

    def loop(self, at, per):
        self.at, self.per, self.n = at, per, 0

    def done(self, turns):
        assert self.n == self.per, (self.n, self.per)
        self.base += turns * self.per
        self.at, self.n = None, 0

    def __call__(self, instruction):
        instruction.then_inc(self.sem, 1)
        self.n += 1
        if self.at is None:
            self.base, self.n = self.base + 1, 0
            self.eng.wait_ge(self.sem, self.base)
        else:
            self.eng.wait_ge(self.sem, self.at * self.per + (self.base + self.n))


def program(nc, ins, out):
    f32, bf16, i32, f32r = mybir.dt.float32, mybir.dt.bfloat16, mybir.dt.int32, mybir.dt.float32r
    ALU, ACT, AX = mybir.AluOpType, mybir.ActivationFunctionType, mybir.AxisListType
    P = 128
    B, S, D = ins['x'].shape
    SK, DC = ins['ctx_768'].shape[1:]
    T = B * S // P
    TB = S // P
    KC = D // P
    SKB = B * SK
    HID = ins['L0_ffn_W1'].shape[0]
    HC = HID // P
    DH = ins['L1_xattn_qn_g'].shape[0]
    NH = D // DH
    QKV = 3 * D
    E = ins['L1_ffn_gate_w'].shape[0]
    I2 = ins['L1_ffn_w1'].shape[2]
    I = I2 // 2
    IC = I // P
    TOPK = 2
    SLOTS = (B * S * TOPK - E) // P + E
    DCR = DC - P
    DA = DH + 1
    SCALE0 = 1.0 / float(np.sqrt(D // 8))
    LN_EPS, RMS_EPS, QB, QEPS = 1e-5, 1e-8, 127.0, 1e-5
    MAGIC = 12582912.0
    BIG = 1e30
    ALPHA, LIMIT = 1.702, 7.0
    WEXP = 2 * KC * I2 + IC * D
    OFF1, OFF3, OFF2 = 0, KC * I2, 2 * KC * I2
    PLACES_AT = 3
    SHARED = E
    SHARED_AT = E - 1
    NB = 2 * I2 + D
    XW = D + 2

    ctx = ExitStack()
    with ctx:
        ctx.enter_context(nc.allow_non_contiguous_dma(reason="short bias columns"))

        def sb(name, shape, dt=f32):
            return ctx.enter_context(nc.sbuf_tensor(name, shape, dt))

        def sem(name):
            return ctx.enter_context(nc.semaphore(name))

        moe_in = nc.dram_tensor("moe_in", (SLOTS * P, XW), f32, kind="Internal").ap()
        moe_x = nc.dram_tensor("moe_x", (T * P, D), f32, kind="Internal").ap()
        rows_out = out.rearrange("b s d -> (b s) d")

        x_sb = sb("x_sb", [P, T, D])
        KW = -(-(S + SK) // 8) * 8
        SPLIT = B * 4 * KW
        early = ExitStack()
        early.enter_context(nc.sbuf_tensor("early_rest", [P, SHARED_AT * WEXP - SPLIT], f32))
        split = lambda name: [early.enter_context(nc.sbuf_tensor(f"{name}{u}", [P, KW], f32r)) for u in range(B)]
        q_hi = split("q_hi")
        q_lo = split("q_lo")
        k_hl = split("k_hl")
        k_hi = split("k_hi")
        early.close()
        wexp = sb("wexp", [P, E * WEXP])
        aux = sb("aux", [P, 5376])
        small = sb("small", [P, 800])

        class Words:

            def __init__(self, buf, at, end):
                self.buf, self.at, self.end = buf, at, end

            def take(self, n, parts=None, dt=None):
                a, words = self.at, n if dt is None else (n + 1) // 2
                self.at += words
                assert self.at <= self.end, (self.at, self.end)
                v = self.buf[:, a:a + words]
                if dt is not None:
                    v = v.bitcast(dt)
                return v if parts is None else v.rearrange("p (a b) -> p a b", a=parts)

        scr = Words(wexp, WEXP, SHARED_AT * WEXP)
        qkv = scr.take(T * QKV, T)
        mark = scr.at
        scr.at = WEXP
        w1_raw = scr.take(HC * D, HC)
        w2_raw = scr.take(KC * HID, KC)
        w1T = scr.take(KC * HID, KC, bf16)
        w2T = scr.take(HC * D, HC, bf16)
        b1_all = scr.take(HID)
        h_f = [scr.take(HID) for _ in range(2)]
        h_q = [scr.take(HID, dt=bf16) for _ in range(2)]
        h_qT = [scr.take(HID, HC, bf16) for _ in range(2)]
        assert scr.at <= mark
        w1_t = h_f[0].bitcast(bf16).rearrange("p (a b) -> p a b", a=HC)
        w2_t = h_f[1].bitcast(bf16).rearrange("p (a b) -> p a b", a=KC)
        scr.at = mark
        woT = scr.take(NH * (D + 1), NH)
        zeros = scr.take(XW)
        mask_u = scr.take(SKB).bitcast(i32)
        first = scr.at
        wT = scr.take(KC * QKV, KC)
        wcT = scr.take(KC * 2 * D, KC)
        l0_wq = scr.take(KC * D, KC)
        l0_wk = scr.take(2 * D, 2)
        l0_wv = scr.take(2 * D, 2)
        l0_wo = scr.take(KC * D, KC)
        l0_wqT = scr.take(KC * D, KC)
        ctx_sb = scr.take(B * DC, B)
        ctxT = scr.take(2 * SKB, 2)
        kT0 = scr.take(KC * SKB, KC)
        vT0 = scr.take(KC * SKB, KC)
        m0 = scr.take(KC * SKB, KC)
        c0 = scr.take(SKB)
        vv0 = scr.take(B * D, B)
        bo0 = scr.take(D)
        wq_raw = scr.take(KC * D, KC)
        wlkv_raw = scr.take(2 * KC * D, 2 * KC)
        wkv_raw = scr.take(2 * KC * DC, 2 * KC)
        wo_raw = scr.take(KC * D, KC)
        scr.at = first
        q_dup = scr.take(TB * P, TB)
        k_dup = scr.take((TB + 1) * P, TB + 1)
        vh = [scr.take((TB + 1) * DA, TB + 1) for _ in range(2)]
        pT = [scr.take(512) for _ in range(3)]
        oT = [scr.take(S) for _ in range(2)]
        bias_part = scr.take(NB, dt=bf16)
        assert scr.at <= SHARED_AT * WEXP - SPLIT

        ax = Words(aux, 0, 5376)
        xn = ax.take(4 * D, 4)
        xnT = ax.take(KC * 512, KC)
        xq = [ax.take(D, dt=bf16) for _ in range(2)]
        xqT = [ax.take(D, KC, bf16) for _ in range(2)]
        p0 = ax.take(4 * SK, 4)
        ckv = ax.take(B * 2 * D, B)
        b2_all, bo1_all, gate_raw = ax.take(D), ax.take(D), ax.take(D)[0:E]
        ax.at = 0
        lift = [ax.take(I) for _ in range(2)]
        gate = ax.take(I)
        line = ax.take(I)
        assert ax.at >= (4 + 2 * KC) * D
        x_in = [ax.take(D) for _ in range(2)]
        x_inT = [ax.take(D, KC) for _ in range(2)]
        sig = ax.take(I)
        h_moe = ax.take(I)
        h_moeT = ax.take(I, IC)
        y_sb = ax.take(D)
        hot_t, hot_y = ([ax.take(P, dt=bf16) for _ in range(2)] for _ in range(2))
        bias_f = aux[:, 0:NB]

        ident = sb("ident", [P, P])
        ident_b = sb("ident_b", [P, P], bf16)
        ones = sb("ones", [P, P])
        ones_b = sb("ones_b", [P, P], bf16)
        before = sb("before", [P, P], bf16)
        bias_b = sb("bias_b", [96, NB], bf16)
        hot_sh = sb("hot_sh", [96, P], bf16)

        sm = Words(small, 0, 800)
        stats = sm.take(T * 6, T)
        mv = sm.take((T + B) * 2, T + B)
        root_a, root_s, root_t, rstd = (sm.take(T * 2 * NH + 2 * NH) for _ in range(4))
        ss = root_a
        rn = rstd
        gateT = sb("gateT", [P, KC, E])
        gateb = sb("gateb", [P, E])
        cols = sm.take(40)
        bk0, bv0, bq0 = cols[:, 0:2], cols[:, 2:4], cols[:, 4:6]
        lg, lb, xg, xb = cols[:, 6:8], cols[:, 8:10], cols[:, 10:12], cols[:, 12:14]
        qg, kg = cols[:, 14:15], cols[:, 15:16]
        wsum, wsc, winv = cols[:, 16:18], cols[:, 18:20], cols[:, 20:22]
        f_max = cols[:, 22:24]
        f_by, f_step = (cols[:, k:k + 4].rearrange("p (u c) -> p u c", u=2) for k in (24, 28))
        yden = cols[:, 34:36]
        maskc_u = sb("maskc_u", [SK, B], i32)
        mask_row = sb("mask_row", [1, SKB], bf16)
        mask_col = sb("mask_col", [SK, B])
        mx4, sums4 = sm.take(4), sm.take(4)
        mx8 = sm.take(TB)
        negm = sm.take(TB)
        p0T = xnT[:, 0, :]
        banks = ctx.enter_context(nc.psum_tensor("banks", [P, 8 * 512], f32))
        pb = [banks[:, n * 512:(n + 1) * 512] for n in range(8)]
        rt = Words(wexp, SHARED_AT * WEXP - 7200, SHARED_AT * WEXP)
        NORM_AT = 4
        xm = wexp[:, NORM_AT * WEXP:NORM_AT * WEXP + T * XW].rearrange("p (a b) -> p a b", a=T)
        prior = x_sb[:, 0, :]
        meta = x_sb[:, 1, 0:SLOTS * 2].rearrange("p (a b) -> p a b", a=SLOTS)
        slot_rows = x_sb[:, 2, 0:1].bitcast(i32)
        score, biased, val, row, rank, *chosen = (rt.take(T * E, T) for _ in range(5 + TOPK))
        pos = rt.take((T + 1) * E, T + 1)
        big1, big2 = rt.take(T * E * E, T * E), rt.take(T * E * E, T * E)
        sel_b = rt.take(T * E, T, bf16)
        lower = rt.take(E * E, E)
        ntile, tend, tstart, ntile_r = (rt.take(E) for _ in range(4))
        slot_no = rt.take(SLOTS)
        slot_cmp = rt.take(SLOTS * E, SLOTS)
        den16 = rt.take(T)
        route = sb("route", [P, 4, T])
        route_i = sb("route_i", [P, 2, T], i32)
        slot_e = rt.take(SLOTS)
        slot_i = sb("slot_i", [1, SLOTS], i32)
        hot = sb("hot", [96, SLOTS], bf16)
        eno_i = sb("eno_i", [P, 1], i32)
        eno, eno_sh = sb("eno", [P, 1]), sb("eno_sh", [P, 1])

        names = """ld_x ld_l0 ld_ffn ld_l1 ld_route ld_shared ld_e0 ld_mid ld_late ld_last const prep_full prep_free ctx_n w_abs
            w_sum
            root_in root_out chain chain_pool
            g_xn g_xnT_full g_xnT g_sc g_sh g_p g_pT_full g_pT g_av
            f_by f_hm f_xm f_xq f_xqT_full f_xqT f_acc f_pre f_h f_amax f_h127 f_hq f_hqT_full f_hqT f_y f_yout f_b2 a_const a_q
            l_free l_xh l_xT_full l_xT l_qkv l_qk l_v l_sq l_ss l_bo
            a_qk a_v a_hi a_khi t_full t_free a_mx_full a_mx_free a_negm a_s_full a_p a_pv a_o a_oT
            r_x r_xm r_xT_full r_xT r_logit r_e r_exp r_sel r_pos_full r_pos r_slot r_zero r_bias r_hot_sh r_table r_start
            zero xfirst xdram scat
            """.split()
        s = {n: sem(n) for n in names}
        st_in = [sem(f"ym_in{u}") for u in range(2)]
        mnames = "xin xinT_full xinT prod lifted gated sigd lined hid hT_full hT y ysb hot hoty".split()
        m = [{n: sem(f"m{k}_{n}") for n in mnames} for k in range(2)]
        m_x = [[sem(f"m{k}_x{u}") for u in range(2)] for k in range(2)]
        c_out, c_meta, c_rows, c_prior, c_sum, c_go = sem("c_out"), sem("c_meta"), sem("c_rows"), sem("c_prior"), sem("c_sum"), sem("c_go")

        W = ins
        NLD = {}

        block = ctx.enter_context(nc.Block())

        def ffn_turns(eng, turn, link=None, steps=0):
            for i in range(-4, 2):
                turn(i, i % 2)
            with eng.Fori(0, (T - 6) // 2) as j:
                if link is not None:
                    link.loop(j, 2 * steps)
                for u in range(2):
                    turn(j * 2 + (u + 2), u)
            if link is not None:
                link.done((T - 6) // 2)
            for i in range(T - 4, T + 1):
                turn(i, i % 2)

        def there(t):
            return not isinstance(t, int) or 0 <= t < T

        def halves(e, off, kc):
            v = wexp[:, bass.ds(e + (off + kc * I2), I2)]
            return v.rearrange("p (n two) -> p n two", two=2)

        @block.sync
        def _(sp):
            def load(dst, src, to):
                sp.dma_start(dst, src).then_inc(s[to], 16)
                NLD[to] = NLD.get(to, 0) + 16

            load(l0_wq[:], W['L0_xattn_Wq'].rearrange("(c p) n -> p c n", p=P), 'ld_l0')
            load(ctx_sb[0:SK], W['ctx_768'].rearrange("b k c -> k b c"), 'ld_l0')
            for dst, w in ((l0_wk, 'L0_xattn_Wk'), (l0_wv, 'L0_xattn_Wv')):
                load(dst[:, 0, :], W[w][0:P, :], 'ld_l0')
                load(dst[0:DCR, 1, :], W[w][P:DC, :], 'ld_l0')
            load(l0_wo[:], W['L0_xattn_Wo'].rearrange("(c p) n -> p c n", p=P), 'ld_l0')
            for dst, w in ((bk0, 'L0_xattn_bk'), (bv0, 'L0_xattn_bv'), (bq0, 'L0_xattn_bq')):
                load(dst, W[w].rearrange("(c p) -> p c", p=P), 'ld_l0')
            load(bo0[0:1, :], W['L0_xattn_bo'].rearrange("(a n) -> a n", a=1), 'ld_l0')
            load(x_sb[:], W['x'].rearrange("b (t p) d -> p (b t) d", p=P), 'ld_x')
            load(wq_raw[:], W['L1_xattn_Wq'].rearrange("(t p) n -> p t n", p=P), 'ld_l1')
            load(wlkv_raw[:], W['L1_xattn_Wlkv'].rearrange("(t p) n -> p t n", p=P), 'ld_l1')
            load(wkv_raw[:], W['L1_xattn_Wkv'].rearrange("(t p) n -> p t n", p=P), 'ld_l1')
            load(wo_raw[:], W['L1_xattn_Wo'].rearrange("(t p) n -> p t n", p=P), 'ld_l1')
            for dst, w in ((lg, 'L1_xattn_ln_l_g'), (lb, 'L1_xattn_ln_l_b')):
                load(dst, W[w].rearrange("(c p) -> p c", p=P), 'ld_l1')
            for dst, w in ((xg, 'L1_xattn_ln_x_g'), (xb, 'L1_xattn_ln_x_b')):
                load(dst[:, 0:1], W[w][0:P].rearrange("(p a) -> p a", a=1), 'ld_l1')
                load(dst[0:DCR, 1:2], W[w][P:DC].rearrange("(p a) -> p a", a=1), 'ld_l1')
            for dst, w in ((qg, 'L1_xattn_qn_g'), (kg, 'L1_xattn_kn_g')):
                for r in range(0, P, DH):
                    load(dst[r:r + DH], W[w].rearrange("(p a) -> p a", a=1), 'ld_l1')
            load(bo1_all[:], W['L1_xattn_bo'].partition_broadcast(P), 'ld_l1')
            load(mask_u[0:1, :], W['mask_BxS2_bk0'].rearrange("b k -> (b k)").rearrange("(a n) -> a n", a=1), 'ld_l1')
            load(maskc_u[:], W['mask_BxS2_bk0'].rearrange("b k -> k b"), 'ld_l1')
            load(gate_raw[:], W['L1_ffn_gate_w'], 'ld_l1')
            load(gateb[:], W['L1_ffn_gate_b'].partition_broadcast(P), 'ld_l1')

            load(w1_raw[:], W['L0_ffn_W1'].rearrange("(t p) n -> p t n", p=P), 'ld_ffn')
            load(w2_raw[:], W['L0_ffn_W2'].rearrange("(t p) n -> p t n", p=P), 'ld_ffn')
            load(b1_all[:], W['L0_ffn_b1'].partition_broadcast(P), 'ld_ffn')
            load(b2_all[:], W['L0_ffn_b2'].partition_broadcast(P), 'ld_ffn')

            def expert(at, w1, w3, w2, to):
                base = at * WEXP
                for off, w, c in ((OFF1, w1, KC), (OFF3, w3, KC), (OFF2, w2, IC)):
                    n = w.shape[-1]
                    load(wexp[:, base + off:base + off + c * n].rearrange("p (c n) -> p c n", c=c),
                         w.rearrange("(c p) n -> p c n", p=P), to)

            expert(SHARED_AT, W['L1_ffn_sw1'], W['L1_ffn_sw3'], W['L1_ffn_sw2'], 'ld_shared')
            expert(0, W['L1_ffn_w1'][0], W['L1_ffn_w3'][0], W['L1_ffn_w2'][0], 'ld_e0')
            sp.wait_ge(s['const'], 1)
            for n in range(SLOTS):
                sp.dma_start(moe_in[n * P:(n + 1) * P, :], zeros[:]).then_inc(s['zero'], 16)
            sp.wait_ge(s['zero'], 16 * SLOTS)
            sp.wait_ge(s['r_zero'], 1)
            for k in range(3):
                r = slice(32 * k, 32 * k + E)
                q = slice(32 * k + E, 32 * k + E + 1)
                for a, b, wn, sn in ((0, I2, 'L1_ffn_b1', 'L1_ffn_sb1'), (I2, 2 * I2, 'L1_ffn_b3', 'L1_ffn_sb3'),
                                     (2 * I2, NB, 'L1_ffn_b2', 'L1_ffn_sb2')):
                    load(bias_f[r, a:b], W[wn], 'ld_route')
                    load(bias_f[q, a:b], W[sn].rearrange("(a n) -> a n", a=1), 'ld_route')
            def routed(e, to):
                expert(e, W['L1_ffn_w1'][e], W['L1_ffn_w3'][e], W['L1_ffn_w2'][e], to)

            sp.wait_ge(s['r_bias'], 1)
            XG = 4
            for t in range(0, T, XG):
                sp.wait_ge(s['r_xm'], t + XG)
                sp.dma_start(moe_x[t * P:(t + XG) * P, :].rearrange("(t p) d -> p t d", p=P), xm[:, t:t + XG, 0:D])\
                    .then_inc(s['xdram' if t else 'xfirst'], 16)

            def tiles(k, n, src, store, begun):
                def turn(t, u, first):
                    if not first:
                        sp.wait_ge(m[k]['xinT_full'], t - 1)
                    sp.dma_start(x_in[u], src[bass.ds(t * P, P), 0:D]).then_inc(m_x[k][u], 16)

                for u in range(2):
                    turn(u, u, True)
                begun()
                for u in range(2):
                    turn(u + 2, u, False)
                with sp.Fori(0, (n - 4) // 2) as i:
                    for u in range(2):
                        turn(i * 2 + (u + 4), u, False)
                        if store is not None:
                            store(i * 2 + u)
                for t in range((n - 2) // 2 * 2, n - 2):
                    turn(t + 2, t % 2, False)

            def store(t):
                sp.wait_ge(m[0]['ysb'], t + 1)
                sp.dma_start(rows_out[bass.ds(t * P, P), :], x_sb[:, bass.ds(t, 1), :].rearrange("p a d -> p (a d)")).then_inc(c_out, 16)

            def shared_begun():
                sp.wait_ge(s['xdram'], 16 * (T // XG - 1))
                for e in range(1, NORM_AT):
                    routed(e, 'ld_mid')

            def slots_begun():
                for t in range(T - 4, T):
                    store(t)
                sp.wait_ge(c_out, 16 * T)
                sp.dma_start(meta, moe_in[:, D:D + 2].rearrange("(n p) m -> p n m", p=P)).then_inc(c_meta, 16)
                sp.wait_ge(m[0]['y'], T)
                routed(E - 1, 'ld_last')

            sp.wait_ge(s['xfirst'], 16)
            tiles(0, T, moe_x, store, shared_begun)
            sp.wait_ge(m[0]['xinT_full'], T)
            sp.wait_ge(s['scat'], 16 * 2 * T)
            tiles(1, SLOTS, moe_in, None, slots_begun)

        @block.gpsimd
        def _(pool):
            g = nc.gpsimd
            link = Chain(pool, s['chain_pool'])
            link(g.memset(zeros[:], 0.0))
            g.iota(zeros[:, D:D + 1].bitcast(i32), pattern=[[0, 1]], base=T * P, channel_multiplier=0).then_inc(s['const'], 1)
            g.memset(ones[:], 1.0)
            g.memset(ones_b[:], 1.0)
            link(g.memset(ident[:], 0.0))
            link(g.affine_select(out=ident[:], in_=ident[:], compare_op=ALU.not_equal, fill=1.0, base=0,
                                 pattern=[[-1, P]], channel_multiplier=1))
            g.tensor_copy(ident_b[:], ident[:])
            link(g.affine_select(out=before[:], in_=ones_b[:], compare_op=ALU.is_gt, fill=0.0, base=0,
                                 pattern=[[1, P]], channel_multiplier=-1))
            link(g.memset(mv[:], 1.0))
            link(g.memset(ctxT[:], 0.0))
            link(g.memset(woT[:], 0.0))
            link(g.memset(woT[DH:DA, :, D:D + 1], 1.0))
            g.iota(eno_i[:], pattern=[[0, 1]], base=0, channel_multiplier=1).then_inc(s['const'], 1)
            flat = lambda v: v.rearrange("p a b -> p (a b)")

            with pool.Fori(0, T) as t:
                pool.wait_ge(s['f_xq'], t + 1)
                g.tensor_tensor(x_sb[:, bass.ds(t, 1), :].rearrange("p a d -> p (a d)"),
                                x_sb[:, bass.ds(t, 1), :].rearrange("p a d -> p (a d)"),
                                b2_all[:], ALU.add).then_inc(s['f_b2'], 1)

            with pool.Fori(0, T) as t:
                pool.wait_ge(s['l_xh'], t + 1)
                g.tensor_tensor(x_sb[:, bass.ds(t, 1), :].rearrange("p a d -> p (a d)"),
                                x_sb[:, bass.ds(t, 1), :].rearrange("p a d -> p (a d)"),
                                bo1_all[:], ALU.add).then_inc(s['l_bo'], 1)

            pool.wait_ge(s['l_bo'], T)
            pool.wait_ge(s['l_free'], 1)
            g.memset(bias_f, 0.0).then_inc(s['r_zero'], 1)
            for u in range(2):
                link(g.memset(k_hl[u][:, S + SK:KW].bitcast(f32), 0.0))
                link(g.memset(k_hi[u][DH:DA, 0:S + SK].bitcast(f32), 1.0))
                link(g.memset(vh[u][:, :, DH:DA], 1.0))
            pool.sem_inc(s['a_const'], 1)

            def head(n, h, b):
                if n is not None:
                    pool.wait_ge(s['a_o'], n - 1)
                col = h * DH + 2 * D
                g.tensor_copy(vh[b][:, 0:TB, 0:DH], qkv[:, b * TB:(b + 1) * TB, bass.ds(col, DH)])
                g.tensor_copy(vh[b][0:SK, TB, 0:DH], ckv[0:SK, b, bass.ds(h * DH + D, DH)]).then_inc(s['a_v'], 1)
                pool.wait_ge(s['a_hi'], 5 if n is None and b == 0 else 10 if n is None else n * 5 + 5)
                g.tensor_copy(k_hi[b][0:DH, 0:S + SK], k_hl[b][0:DH, 0:S + SK]).then_inc(s['a_khi'], 1)

            head(None, 0, 0)
            head(None, 0, 1)
            PARTS = 3
            part = bias_part[0:96, :]
            for i in range(NH - 1):
                for b in range(B):
                    head(i * 2 + (2 + b), i + 1, b)
                for k in range(PARTS)[i::NH - 1]:
                    if k == 0:
                        pool.wait_ge(s['ld_route'], NLD['ld_route'])
                    link(g.tensor_copy(part, bias_f[0:96, :]))
                    link(g.tensor_copy(bias_b[32 * k:32 * k + 32, :], part[32 * k:32 * k + 32, :]))
                    if k < PARTS - 1:
                        link(g.tensor_tensor(bias_f[0:96, :], bias_f[0:96, :], part, ALU.subtract))
            pool.sem_inc(s['r_bias'], 1)

            pool.wait_ge(s['a_oT'], 1)
            link(g.memset(lower[:], 1.0))
            link(g.affine_select(out=lower[:], in_=lower[:], compare_op=ALU.is_gt, fill=0.0, base=0,
                                 pattern=[[1, E], [-1, E]], channel_multiplier=0))
            g.iota(slot_no[:], pattern=[[1, SLOTS]], base=0, channel_multiplier=0,
                   allow_small_or_imprecise_dtypes=True).then_inc(s['r_table'], 1)
            pool.wait_ge(s['zero'], 16 * SLOTS)
            g.iota(xm.bitcast(i32)[:, :, D:D + 1], pattern=[[P, T], [0, 1]], base=0, channel_multiplier=1)
            for t in range(T):
                pool.wait_ge(s['r_x'], t + 1)
                g.tensor_copy(xm[:, t, 0:D], xn[:, t % 4, :]).then_inc(s['r_xm'], 1)
            def folded(dst, src):
                n = E // 2
                while n > 1:
                    link(g.tensor_tensor(src[:, :, 0:n], src[:, :, 0:n], src[:, :, n:2 * n], ALU.add))
                    n //= 2
                link(g.tensor_tensor(dst.unsqueeze(2), src[:, :, 0:1], src[:, :, 1:2], ALU.add))

            pool.wait_ge(s['r_start'], 1)
            link(g.tensor_tensor(row[:], pos[:, 0:T, :], tstart.unsqueeze(1).to_broadcast([P, T, E]), ALU.add))
            for c in range(TOPK):
                for k, of in ((c, row), (2 + c, score)):
                    link(g.tensor_tensor(val[:], chosen[c][:], of[:], ALU.mult))
                    folded(route[:, k, :], val)
            link(g.tensor_copy(route_i[:], route[:, 0:2, :]))
            for c in range(TOPK):
                if c > 0:
                    pool.wait_ge(s['scat'], 16 * c * T)
                link(g.tensor_copy(xm[:, :, D + 1:D + 2], route[:, 2 + c, :].unsqueeze(2)))
                for t in range(T):
                    g.indirect_dma_start(out=moe_in, out_offset=bass.IndirectOffsetOnAxis(ap=route_i[:, c, t:t + 1], axis=0),
                                         in_=xm[:, t, :], in_offset=None,
                                         bounds_check=SLOTS * P - 1, oob_is_err=False).then_inc(s['scat'], 16)
            def routed(e):
                at = e * WEXP
                for off, w, c in ((OFF1, W['L1_ffn_w1'], KC), (OFF3, W['L1_ffn_w3'], KC), (OFF2, W['L1_ffn_w2'], IC)):
                    n = w.shape[-1]
                    g.dma_start(wexp[:, at + off:at + off + c * n].rearrange("p (c n) -> p c n", c=c),
                                w[e].rearrange("(c p) n -> p c n", p=P)).then_inc(s['ld_late'], 16)

            pool.wait_ge(s['r_slot'], 1)
            for e in range(NORM_AT + 1, E - 1):
                routed(e)
            pool.wait_ge(s['scat'], 16 * 2 * T)
            routed(NORM_AT)

            def pick(dst, t, sem):
                g.tensor_copy(dst[0:96, :], hot[:, bass.ds(t, 1)].to_broadcast([96, P])).then_inc(m[1][sem], 1)

            pool.wait_ge(m[0]['y'], T)
            pick(hot_t[0], 0, 'hot')
            pick(hot_t[1], 1, 'hot')
            pick(hot_y[0], 0, 'hoty')

            def gather_sums(t):
                if not isinstance(t, int) or t > 0:
                    pool.wait_ge(c_sum, t * 16)
                    pool.wait_ge(c_rows, t)
                g.tensor_copy(slot_rows, meta.bitcast(i32)[:, bass.ds(t, 1), 0:1].rearrange("p a b -> p (a b)")).then_inc(c_rows, 1)
                pool.wait_ge(c_rows, t + 1)
                pool.sem_inc(c_go, 1)
                g.indirect_dma_start(out=prior, out_offset=None, in_=rows_out,
                                     in_offset=bass.IndirectOffsetOnAxis(ap=slot_rows, axis=0),
                                     bounds_check=T * P - 1, oob_is_err=False).then_inc(c_prior, 16)

            def scatter_sums(t):
                pool.wait_ge(c_prior, t * 16 + 16)
                pool.wait_ge(m[1]['ysb'], t + 1)
                pool.sem_inc(c_go, 1)
                g.indirect_dma_start(out=rows_out, out_offset=bass.IndirectOffsetOnAxis(ap=slot_rows, axis=0),
                                     in_=y_sb, in_offset=None,
                                     bounds_check=T * P - 1, oob_is_err=False).then_inc(c_sum, 16)

            pool.wait_ge(c_out, 16 * T)
            pool.wait_ge(c_meta, 16)
            gather_sums(0)

            def picks(t, u):
                pool.wait_ge(m[1]['prod'], t * 2 - 2)
                pool.wait_ge(m[1]['y'], t - 2)
                pick(hot_t[u], t, 'hot')
                pick(hot_y[1 - u], t - 1, 'hoty')
                scatter_sums(t - 2)
                gather_sums(t - 1)

            with pool.Fori(0, (SLOTS - 3) // 2) as i:
                for u in range(2):
                    picks(i * 2 + (2 + u), u)
            picks(SLOTS - 1, 0)
            pool.wait_ge(m[1]['y'], SLOTS - 2)
            pick(hot_y[0], SLOTS - 1, 'hoty')

            for t in (SLOTS - 2, SLOTS - 1):
                scatter_sums(t)
                if t + 1 < SLOTS:
                    gather_sums(t + 1)
            pool.wait_ge(c_sum, 16 * SLOTS)

        @block.tensor
        def _(pe):
            mm = nc.tensor.matmul
            tr = nc.tensor.transpose
            unit = [0]

            def bank():
                if unit[0] >= 2:
                    pe.wait_ge(s['prep_free'], unit[0] - 1)
                unit[0] += 1
                return pb[6 + (unit[0] - 1) % 2]

            def full(last):
                last.then_inc(s['prep_full'], 1)

            pe.wait_ge(s['const'], 2)
            pe.wait_ge(s['ld_l0'], NLD['ld_l0'])
            o = bank()
            for b in range(B):
                tr(o[:, b * SK:(b + 1) * SK], ctx_sb[0:SK, b, 0:P], ident[0:SK, 0:SK])
                last = tr(o[0:DCR, SKB + b * SK:SKB + (b + 1) * SK], ctx_sb[0:SK, b, P:DC], ident[0:SK, 0:SK])
            full(last)
            o = bank()
            for ec in range(KC):
                for dc in range(KC):
                    a = (ec * KC + dc) * P
                    last = tr(o[:, a:a + P], l0_wq[:, dc, ec * P:(ec + 1) * P], ident[:])
            full(last)
            for w in (l0_wk, l0_wv):
                o = bank()
                for ec in range(KC):
                    mm(o[:, ec * SKB:(ec + 1) * SKB], w[:, 0, ec * P:(ec + 1) * P], ctxT[:, 0, :], start=True, stop=False)
                    last = mm(o[:, ec * SKB:(ec + 1) * SKB], w[0:DCR, 1, ec * P:(ec + 1) * P], ctxT[0:DCR, 1, :],
                              start=False, stop=True)
                full(last)
            o = bank()
            for dc in range(KC):
                for ec in range(KC):
                    mm(o[:, dc * SKB:(dc + 1) * SKB], l0_wqT[:, ec, dc * P:(dc + 1) * P], kT0[:, ec, :],
                       start=ec == 0, stop=ec == KC - 1)
            for ec in range(KC):
                last = mm(o[0:1, KC * SKB:(KC + 1) * SKB], bq0[:, ec:ec + 1], kT0[:, ec, :], start=ec == 0, stop=ec == KC - 1)
            full(last)
            o = bank()
            for b in range(B):
                for ec in range(KC):
                    mm(o[0:SK, b * D:(b + 1) * D], vT0[:, ec, b * SK:(b + 1) * SK], l0_wo[:, ec, :], start=ec == 0, stop=False)
                last = mm(o[0:SK, b * D:(b + 1) * D], ones[0:1, 0:SK], bo0[0:1, :], start=False, stop=True)
            full(last)
            pe.wait_ge(s['prep_free'], unit[0])

            def turn_w1(kc):
                pe.wait_ge(s['f_pre'], 1)
                o = bank().bitcast(bf16)
                for hc in range(HC):
                    last = tr(o[:, hc * P:(hc + 1) * P], w1_t[:, hc, kc * P:(kc + 1) * P], ident_b[:])
                full(last)

            def turn_w2(half):
                pe.wait_ge(s['f_pre'], 2)
                o = bank().bitcast(bf16)
                for j in range(HC // 2):
                    hc = half * (HC // 2) + j
                    for oc in range(KC):
                        last = tr(o[:, (j * KC + oc) * P:(j * KC + oc + 1) * P], w2_t[:, oc, hc * P:(hc + 1) * P], ident_b[:])
                full(last)

            def turn_wq():
                pe.wait_ge(s['ld_l1'], NLD['ld_l1'])
                o = bank()
                for kc in range(KC):
                    for oc in range(KC):
                        a = (kc * KC + oc) * P
                        last = tr(o[:, a:a + P], wq_raw[:, oc, kc * P:(kc + 1) * P], ident[:])
                full(last)

            def turn_wlkv(kc):
                o = bank()
                for oc in range(2 * KC):
                    last = tr(o[:, oc * P:(oc + 1) * P], wlkv_raw[:, oc, kc * P:(kc + 1) * P], ident[:])
                full(last)

            def turn_wkv(a, b):
                o = bank()
                for oc in range(2 * KC):
                    last = tr(o[0:b - a, oc * P:(oc + 1) * P], wkv_raw[:, oc, a:b], ident[:])
                full(last)

            def turn_wo(hp):
                o = bank()
                for j in range(2):
                    h = hp * 2 + j
                    for lc in range(KC):
                        last = tr(o[0:DH, (j * KC + lc) * P:(j * KC + lc + 1) * P], wo_raw[:, lc, h * DH:(h + 1) * DH], ident[:])
                full(last)

            def turn_gate():
                o = bank()
                for kc in range(KC):
                    last = tr(o[:, kc * E:(kc + 1) * E], gate_raw[:, kc * P:(kc + 1) * P], ident[0:E, 0:E])
                full(last)

            def turn_ctx():
                pe.wait_ge(s['ctx_n'], 1)
                o = bank()
                for b in range(B):
                    tr(o[:, b * SK:(b + 1) * SK], ctx_sb[0:SK, b, 0:P], ident[0:SK, 0:SK])
                    last = tr(o[0:DCR, SKB + b * SK:SKB + (b + 1) * SK], ctx_sb[0:SK, b, P:DC], ident[0:SK, 0:SK])
                full(last)

            def context(b):
                if b == 0:
                    pe.wait_ge(s['prep_free'], unit[0])
                o = bank()
                mm(o[0:SK, :], ctxT[:, 0, b * SK:(b + 1) * SK], wcT[:, 0, :], start=True, stop=False)
                full(mm(o[0:SK, :], ctxT[0:DCR, 1, b * SK:(b + 1) * SK], wcT[0:DCR, 1, :], start=False, stop=True))

            def weights_sums():
                pe.wait_ge(s['w_abs'], 1)
                mm(pb[2][:, 510:512], ones[:], wsum, start=True, stop=True).then_inc(s['w_sum'], 1)

            pieces = [[turn_wq, lambda: turn_wlkv(0), lambda: turn_wlkv(1), lambda: turn_wkv(0, P)],
                      [weights_sums, lambda: turn_wkv(P, DC), lambda: turn_wo(0), lambda: turn_wo(1), turn_gate],
                      [turn_ctx, lambda: turn_w1(0), lambda: turn_w1(1)],
                      [lambda: turn_w2(0), lambda: turn_w2(1), lambda: context(0), lambda: context(1)]]

            G = 4

            def scores0(it):
                b = it * G // TB
                pe.wait_ge(s['g_xn'], it + 1)
                for kc in range(KC):
                    for u in range(G):
                        last = tr(pb[kc][:, u * P:(u + 1) * P], xn[:, u, kc * P:(kc + 1) * P], ident[:])
                last.then_inc(s['g_xnT_full'], 1)
                pe.wait_ge(s['g_xnT'], it + 1)
                if it > 0:
                    pe.wait_ge(s['g_sh'], it)
                for u in range(G):
                    so = pb[2][:, u * SK:(u + 1) * SK]
                    for kc in range(KC):
                        mm(so, xnT[:, kc, u * P:(u + 1) * P], m0[:, kc, b * SK:(b + 1) * SK], start=kc == 0, stop=False)
                    last = mm(so, ones[0:1, :], c0[0:1, b * SK:(b + 1) * SK], start=False, stop=True)
                last.then_inc(s['g_sc'], 1)

            scores0(0)
            for it in range(T // G):
                b = it * G // TB
                if it + 1 < T // G:
                    scores0(it + 1)
                for piece in pieces[it][:2]:
                    piece()
                pe.wait_ge(s['g_p'], it + 1)
                for u in range(G):
                    last = tr(pb[3][0:SK, u * P:(u + 1) * P], p0[:, u, :], ident[:])
                last.then_inc(s['g_pT_full'], 1)
                for piece in pieces[it][2:]:
                    piece()
                pe.wait_ge(s['g_pT'], it + 1)
                for u in range(G):
                    last = mm(pb[4 + u // 2][:, (u % 2) * D:(u % 2 + 1) * D], p0T[0:SK, u * P:(u + 1) * P],
                              vv0[0:SK, b, :], start=True, stop=True)
                last.then_inc(s['g_av'], 1)
            pe.wait_ge(s['prep_free'], unit[0])
            NLD['prep'] = unit[0]

            def ffn_in(t, u):
                pe.wait_ge(s['f_xq'], t + 1)
                o = pb[7][:].bitcast(bf16)
                for kc in range(KC):
                    last = tr(o[:, kc * P:(kc + 1) * P], xq[u][:, kc * P:(kc + 1) * P], ident_b[:])
                last.then_inc(s['f_xqT_full'], 1)
                pe.wait_ge(s['f_xqT'], t + 1)
                if not isinstance(t, int) or t >= 2:
                    pe.wait_ge(s['f_acc'], t - 1)
                for half in range(2):
                    for kc in range(KC):
                        last = mm(pb[2 * u + half][:], xqT[u][:, kc, :], w1T[:, kc, half * 512:(half + 1) * 512],
                                  start=kc == 0, stop=kc == KC - 1)
                last.then_inc(s['f_h'], 1)

            def ffn_hidden_T(t, u):
                pe.wait_ge(s['f_hq'], t + 1)
                o = pb[4 + u][:].bitcast(bf16)
                for hc in range(HC):
                    last = tr(o[:, hc * P:(hc + 1) * P], h_q[u][:, hc * P:(hc + 1) * P], ident_b[:])
                last.then_inc(s['f_hqT_full'], 1)

            def ffn_out(t, u):
                pe.wait_ge(s['f_hqT'], t + 1)
                if not isinstance(t, int) or t > 0:
                    pe.wait_ge(s['f_yout'], t)
                for hc in range(HC):
                    last = mm(pb[6][:, 0:D], h_qT[u][:, hc, :], w2T[:, hc, :], start=hc == 0, stop=hc == HC - 1)
                last.then_inc(s['f_y'], 1)

            def ffn_turn(i, u):
                if there(i + 3):
                    ffn_in(i + 3, 1 - u)
                if there(i):
                    ffn_out(i, u)
                if there(i + 1):
                    ffn_hidden_T(i + 1, 1 - u)

            ffn_turns(pe, ffn_turn)

            def proj_in(t, u):
                pe.wait_ge(s['l_xh'], t + 1)
                pe.wait_ge(s['l_xT'], t)
                for kc in range(KC):
                    last = tr(pb[0][:, kc * P:(kc + 1) * P], xn[:, u, kc * P:(kc + 1) * P], ident[:])
                last.then_inc(s['l_xT_full'], 1)

            def proj(t, u, first):
                pe.wait_ge(s['l_xT'], t + 1)
                if not first:
                    pe.wait_ge(s['l_qk'], t - 1)
                    pe.wait_ge(s['l_v'], t - 1)
                for o, a, n in ((pb[1 + 2 * u], 0, 2 * D), (pb[2 + 2 * u], 2 * D, D)):
                    for kc in range(KC):
                        last = mm(o[:, 0:n], xnT[:, kc, u * P:(u + 1) * P], wT[:, kc, a:a + n], start=kc == 0, stop=kc == KC - 1)
                last.then_inc(s['l_qkv'], 1)

            proj_in(0, 0)
            proj_in(1, 1)
            proj(0, 0, True)
            proj_in(2, 0)
            proj(1, 1, True)
            with pe.Fori(0, (T - 4) // 2) as i:
                for u in range(2):
                    proj_in(i * 2 + (3 + u), 1 - u)
                    proj(i * 2 + (2 + u), u, False)
            proj_in(T - 1, 1)
            proj(T - 2, 0, False)
            proj(T - 1, 1, False)

            TP = pb[7]
            TURNED = (0, 1, 2, 7, 0)
            KTILES = [(c * P, P) for c in range(TB)] + [(S, SK)]
            NU = 2 * len(KTILES)
            flat = lambda v: v.rearrange("p a b -> p (a b)")

            def claim(use):
                if not isinstance(use, int) or use > 0:
                    pe.wait_ge(s['t_free'], use)

            def turned(n, use, b, k, TP=None):
                if k in (0, 2):
                    pe.wait_ge(s['a_qk' if k else 'a_q'], n + 1)
                if TP is None:
                    TP = pb[TURNED[k]]
                    if k == 4:
                        claim(use + 1)
                if k < 4:
                    src = q_dup if k < 2 else k_dup
                    for j in range(4):
                        last = tr(TP[:, j * P:(j + 1) * P], src[:, (k % 2) * 4 + j, :], ident[:])
                else:
                    last = tr(TP[:, 0:SK], k_dup[0:SK, TB, :], ident[0:SK, 0:SK])
                last.then_inc(s['t_full'], 1)

            def maxima(n, use, b, t, o=0, ahead=0):
                if t == 0:
                    pe.wait_ge(s['t_free'], use + 5)
                if t > ahead or not isinstance(n, int) or n > 0:
                    pe.wait_ge(s['a_mx_free'], n * TB + (t - ahead))
                for a, w in ((0, 512), (512, 512), (S, SK + SK % 2)):
                    mm(banks[:, o + a:o + a + w], q_hi[b][:, t * P:(t + 1) * P], k_hl[b][:, a:a + w], start=True, stop=a < S)
                mm(banks[:, o + S:o + S + SK], ones_b[0:1, :], mask_row[0:1, b * SK:(b + 1) * SK], start=False, stop=True)\
                    .then_inc(s['a_mx_full'], 1)

            def minus(n, use, half):
                if half == 0:
                    pe.wait_ge(s['a_negm'], n + 1)
                claim(use + half)
                for j in range(4):
                    last = mm(TP[DH:DA, j * P:(j + 1) * P], negm[:, half * 4 + j:half * 4 + j + 1], ident[:], start=True, stop=True)
                last.then_inc(s['t_full'], 1)

            def scores(n, b, q):
                c, half = divmod(q, 2)
                a, w = KTILES[c]
                if q >= 2 or not isinstance(n, int) or n > 0:
                    pe.wait_ge(s['a_p'], n * NU + (q - 1))
                cols = slice(half * 512, (half + 1) * 512)
                mm(pb[3 + q % 2][0:w, :], k_hl[b][:, a:a + w], q_hi[b][:, cols], start=True, stop=False)
                mm(pb[3 + q % 2][0:w, :], k_hi[b][0:DA, a:a + w], q_lo[b][0:DA, cols], start=False, stop=True)\
                    .then_inc(s['a_s_full'], 1)

            def values(n, b, q):
                c, half = divmod(q, 2)
                a, w = KTILES[c]
                pe.wait_ge(s['a_p'], n * NU + (q + 1))
                mm(pb[5 + half][0:DA, :], vh[b][0:w, c, :], pT[q % 3][0:w, :], start=c == 0,
                   stop=c == len(KTILES) - 1).then_inc(s['a_pv'], 1)

            def joined(n, h, use, b, t, TP=None):
                if t == 0:
                    pe.wait_ge(s['a_o'], n + 1)
                    claim(use)
                elif TP is None:
                    claim(use + t)
                TP = pb[7] if TP is None else TP
                mm(TP[:, 0:D + 1], oT[b][0:DA, t * P:(t + 1) * P], flat(woT[0:DA, bass.ds(h, 1), :]), start=True, stop=True)\
                    .then_inc(s['t_full'], 1)

            def step(n, b, h_last, use, first, last):
                pe.wait_ge(s['t_free'], use)
                pe.wait_ge(s['a_khi'], n + 1)
                pe.wait_ge(s['a_v'], n + 1)
                out_at = use if last else use + 5
                minus_at = use + 5 if first else use + 5 + TB
                scores(n, b, 0)
                for q in range(NU):
                    if q + 1 < NU:
                        scores(n, b, q + 1)
                    if q == 0 and not last:
                        for k in range(2):
                            turned(n + 1, use, 1 - b, k)
                    if q == 0 and not first:
                        pe.wait_ge(s['a_o'], n)
                    values(n, b, q)
                    if q in (1, 2, 3) and not last:
                        turned(n + 1, use, 1 - b, q + 1)
                    if 5 <= q < 5 + TB:
                        if not last:
                            maxima(n + 1, use, 1 - b, q - 5)
                        if not first:
                            joined(n - 1, h_last, out_at, 1 - b, q - 5)
                    if q in (15, 16) and not last:
                        minus(n + 1, minus_at, q - 15)

            HEADS = B * NH
            USES = 5 + TB + 2
            for k in range(5):
                turned(0, 0, 0, k, pb[3 + k])
            pe.wait_ge(s['a_const'], 1)
            for t in range(TB):
                maxima(0, 0, 0, t, t % 2 * 3 * 512, 1)
            for half in range(2):
                minus(0, 5, half)
            step(0, 0, 0, 7, True, False)
            with pe.Fori(0, NH - 1) as i:
                step(i * 2 + 1, 1, i, i * (2 * USES) + (USES - 1), False, False)
                step(i * 2 + 2, 0, i, i * (2 * USES) + (2 * USES - 1), False, False)
            end = (HEADS - 1) * USES - 1
            step(HEADS - 1, 1, NH - 1, end, False, True)
            for t in range(TB):
                joined(HEADS - 1, NH - 1, end + TB, 1, t, pb[t])

            GATES, PLACES = slice(0, T * E), T * E
            with pe.Fori(0, T // 4) as i:
                for u in range(4):
                    t = i * 4 + u
                    pe.wait_ge(s['r_x'], t + 1)
                    for kc in range(KC):
                        last = tr(pb[u][:, kc * P:(kc + 1) * P], xn[:, u, kc * P:(kc + 1) * P], ident[:])
                    last.then_inc(s['r_xT_full'], 1)
                for u in range(4):
                    t = i * 4 + u
                    pe.wait_ge(s['r_xT'], t + 1)
                    for kc in range(KC):
                        last = mm(pb[7][:, bass.ds(t * E, E)], xnT[:, kc, u * P:(u + 1) * P], gateT[:, kc, :],
                                  start=kc == 0, stop=kc == KC - 1)
                    last.then_inc(s['r_logit'], 1)

            def places():
                pe.wait_ge(s['r_sel'], 1)
                o = pb[7][:, PLACES:PLACES + (T + 1) * E]
                mm(o[:, 0:T * E], before[:], flat(sel_b), start=True, stop=False)
                mm(o[:, T * E:], ones_b[:], sel_b[:, 0, :], start=False, stop=False)
                for t in range(T):
                    n = T - max(t, 1)
                    later = o[:, (t + 1) * E:(t + 1 + n) * E].rearrange("p (a b) -> p a b", a=n)
                    last = mm(later, ones_b[:], sel_b[:, t:t + 1, :].to_broadcast([P, n, E]), start=False, stop=t == T - 1)
                last.then_inc(s['r_pos_full'], 1)

            def mixture(k, n, where, hot_of, split, between):
                def bring(t, u, turn):
                    pe.wait_ge(m_x[k][u], turn * 16 + 16)
                    pe.wait_ge(m[k]['xinT'], t)
                    for kc in range(KC):
                        last = tr(pb[4][:, kc * P:(kc + 1) * P], x_in[u][:, kc * P:(kc + 1) * P], ident[:])
                    last.then_inc(m[k]['xinT_full'], 1)

                def product(t, u, side, at):
                    for j, off in enumerate((OFF1, OFF3)):
                        o = pb[2 * side + j]
                        for kc in range(KC):
                            mm(o[:], x_inT[u][:, kc, :], halves(at, off, kc)[:, :, side], start=kc == 0, stop=False)
                        bb = bias_b[:, j * I2:(j + 1) * I2].rearrange("p (n two) -> p n two", two=2)
                        last = mm(o[:], hot_of(u)[0], bb[:, :, side], start=False, stop=True)
                    last.then_inc(m[k]['prod'], 1)

                def hidden_T(t):
                    pe.wait_ge(m[k]['hid'], t + 1)
                    for c in range(IC):
                        last = tr(pb[5][:, c * P:(c + 1) * P], h_moe[:, c * P:(c + 1) * P], ident[:])
                    last.then_inc(m[k]['hT_full'], 1)

                def second(t, u, at):
                    pe.wait_ge(m[k]['hT'], t + 1)
                    pe.wait_ge(m[k]['ysb'], t)
                    if k == 1:
                        pe.wait_ge(m[k]['hoty'], t + 1)
                    for c in range(IC):
                        mm(pb[6][:, 0:D], h_moeT[:, c, :], wexp[:, bass.ds(at + (OFF2 + c * D), D)], start=c == 0, stop=False)
                    mm(pb[6][:, 0:D], hot_of(u)[1], bias_b[:, 2 * I2:NB], start=False, stop=True).then_inc(m[k]['y'], 1)

                def step(t, u, turn, at_before, at, more):
                    first = at_before is None
                    pe.wait_ge(m[k]['xinT'], t + 1)
                    if k == 1:
                        pe.wait_ge(m[k]['hot'], t + 1)
                    pe.wait_ge(m[k]['gated'], t)
                    product(t, u, 0, at)
                    if not first:
                        hidden_T(t - 1)
                    pe.wait_ge(m[k]['lined'], t)
                    product(t, u, 1, at)
                    if more:
                        bring(t + 1, 1 - u, turn)
                    if not first:
                        second(t - 1, 1 - u, at_before)

                bring(0, 0, 0)
                step(0, 0, 0, None, where(0), True)
                pairs = (n - 2) // 2

                def pair(i):
                    at = [where(i * 2 + j) for j in range(3)]
                    for u in range(2):
                        step(i * 2 + (1 + u), 1 - u, i + 1, at[u], at[u + 1], True)

                with pe.Fori(0, split) as i:
                    pair(i)
                between()
                with pe.Fori(0, pairs - split) as i:
                    pair(i + split)
                for t in range(2 * pairs + 1, n):
                    step(t, t % 2, (t + 1) // 2, where(t - 1), where(t), t + 1 < n)
                hidden_T(n - 1)
                second(n - 1, (n - 1) % 2, where(n - 1))

            pe.wait_ge(s['ld_shared'], NLD['ld_shared'])
            pe.wait_ge(s['r_bias'], 1)
            pe.wait_ge(s['r_hot_sh'], 1)
            mixture(0, T, lambda t: SHARED_AT * WEXP, lambda u: (hot_sh[:], hot_sh[:]), PLACES_AT, places)
            pe.wait_ge(s['ld_e0'], NLD['ld_e0'])
            pe.wait_ge(s['ld_mid'], NLD['ld_mid'])
            pe.wait_ge(s['ld_late'], 3 * 16 * (E - 1 - NORM_AT))
            pe.wait_ge(s['r_slot'], 1)

            def slot_at(t):
                return pe.value_load(slot_i[0:1, bass.ds(t, 1)], min_val=0, max_val=E - 1) * WEXP

            OTHERS = T * (TOPK - 1)
            mixture(1, SLOTS, slot_at, lambda u: (hot_t[u][0:96, :], hot_y[u][0:96, :]), (OTHERS - 1) // 2,
                    lambda: pe.wait_ge(s['ld_last'], NLD['ld_last']))

        @block.scalar
        def _(act):
            a = nc.scalar.activation
            roots = [0]

            def ready(function):
                a(cols[:, 36:37], ones[:, 0:1], function)

            def root(n):
                act.wait_ge(s['root_in'], roots[0] + 1)
                a(root_s[:, 0:n], root_a[:, 0:n], ACT.Sqrt).then_inc(s['root_out'], 1)
                roots[0] += 1

            units = [0]
            flat = lambda ap: ap.rearrange("p a b -> p (a b)")

            def filled():
                units[0] += 1
                act.wait_ge(s['prep_full'], units[0])
                return pb[6 + (units[0] - 1) % 2]

            def kept(*pairs):
                o = filled()
                for dst, of in pairs:
                    last = a(dst, of(o), ACT.Copy)
                last.then_inc(s['prep_free'], 1)

            act.wait_ge(s['const'], 2)
            kept((ctxT[:, 0, :], lambda o: o[:, 0:SKB]), (ctxT[0:DCR, 1, :], lambda o: o[0:DCR, SKB:2 * SKB]))
            kept((flat(l0_wqT), lambda o: o))
            for dst, bias in ((kT0, bk0), (vT0, bv0)):
                o = filled()
                for ec in range(KC):
                    last = a(dst[:, ec, :], o[:, ec * SKB:(ec + 1) * SKB], ACT.Identity, bias=bias[:, ec:ec + 1])
                last.then_inc(s['prep_free'], 1)
            kept((flat(m0), lambda o: o[:, 0:KC * SKB]), (c0[0:1, :], lambda o: o[0:1, KC * SKB:(KC + 1) * SKB]))
            kept((flat(vv0[0:SK]), lambda o: o[0:SK, 0:B * D]))

            def keep_ctx():
                o = filled()
                a(ctxT[:, 0, :], o[:, 0:SKB], ACT.Identity, scale=xg[:, 0:1], bias=xb[:, 0:1])
                a(ctxT[0:DCR, 1, :], o[0:DCR, SKB:2 * SKB], ACT.Identity, scale=xg[0:DCR, 1:2], bias=xb[0:DCR, 1:2])\
                    .then_inc(s['prep_free'], 1)

            keep_wq = lambda: kept((wT[:, :, 0:D], lambda o: o.rearrange("p (a b) -> p a b", a=KC)))
            keep_wlkv = lambda kc: kept((wT[:, kc, D:QKV], lambda o: o))
            keep_wkv = lambda kc, n: kept((wcT[0:n, kc, :], lambda o: o[0:n, :]))
            keep_wo = lambda hp: kept((woT[0:DH, 2 * hp:2 * hp + 2, 0:D], lambda o: o[0:DH, :].rearrange("p (a b) -> p a b", a=2)))
            keep_gate = lambda: kept((flat(gateT[:]), lambda o: o[:, 0:KC * E]))
            keep_w1 = lambda kc: kept((w1T[:, kc, :], lambda o: o.bitcast(bf16)))
            keep_w2 = lambda half: kept((flat(w2T[:, half * (HC // 2):(half + 1) * (HC // 2), :]), lambda o: o.bitcast(bf16)))
            keep_context = lambda b: kept((ckv[0:SK, b, :], lambda o: o[0:SK, :]))
            pieces = [[keep_wq, lambda: keep_wlkv(0), lambda: keep_wlkv(1), lambda: keep_wkv(0, P)],
                      [lambda: keep_wkv(1, DCR), lambda: keep_wo(0), lambda: keep_wo(1), keep_gate],
                      [keep_ctx, lambda: keep_w1(0), lambda: keep_w1(1)],
                      [lambda: keep_w2(0), lambda: keep_w2(1), lambda: keep_context(0), lambda: keep_context(1)]]
            root(T + B)

            def tokens0(it):
                act.wait_ge(s['g_xnT_full'], it + 1)
                a(xnT[:, 0, :], pb[0][:], ACT.Copy)
                a(xnT[:, 1, :], pb[1][:], ACT.Copy).then_inc(s['g_xnT'], 1)

            tokens0(0)
            for it in range(T // 4):
                if it + 1 < T // 4:
                    tokens0(it + 1)
                act.wait_ge(s['g_sh'], it + 1)
                a(flat(p0), flat(p0), ACT.Exp, scale=SCALE0).then_inc(s['g_p'], 1)
                for piece in pieces[it]:
                    piece()
            root(T)
            ready(ACT.Gelu)

            def ffn_T(t, u):
                act.wait_ge(s['f_xqT_full'], t + 1)
                a(xqT[u][:].rearrange("p a b -> p (a b)"), pb[7][:].bitcast(bf16)[:, 0:D], ACT.Copy).then_inc(s['f_xqT'], 1)

            def ffn_act(t, u):
                act.wait_ge(s['f_acc'], t + 1)
                a(h_f[u], h_f[u], ACT.Gelu).then_inc(s['f_amax'], 1)

            def ffn_hidden_T(t, u):
                act.wait_ge(s['f_hqT_full'], t + 1)
                a(h_qT[u][:].rearrange("p a b -> p (a b)"), pb[4 + u][:].bitcast(bf16), ACT.Copy).then_inc(s['f_hqT'], 1)

            def ffn_quantise(tokens, hidden, i, u):
                act.wait_ge(s['f_by'], i + 5)
                if there(tokens):
                    a(xn[:, u, :], xn[:, u, :], ACT.Copy, scale=f_by[:, u, 0:1], bias=MAGIC).then_inc(s['f_xm'], 1)
                if there(hidden):
                    a(h_f[1 - u], h_f[1 - u], ACT.Copy, scale=f_by[:, u, 1:2], bias=MAGIC).then_inc(s['f_hm'], 1)
                if there(tokens):
                    act.wait_ge(s['f_xm'], tokens + 1)
                    a(xq[u][:], xn[:, u, :], ACT.Copy, bias=-MAGIC).then_inc(s['f_xq'], 1)
                if there(hidden):
                    act.wait_ge(s['f_hm'], hidden + 1)
                    a(h_q[1 - u], h_f[1 - u], ACT.Copy, bias=-MAGIC).then_inc(s['f_hq'], 1)

            def ffn_turn(i, u):
                if there(i + 3):
                    ffn_T(i + 3, 1 - u)
                if there(i):
                    ffn_hidden_T(i, u)
                if there(i + 4) or there(i + 1):
                    ffn_quantise(i + 4, i + 1, i, u)
                if there(i + 2):
                    ffn_act(i + 2, u)

            ffn_turns(act, ffn_turn)
            root(T)

            def proj_T(t, u, first):
                act.wait_ge(s['l_xT_full'], t + 1)
                if not first:
                    act.wait_ge(s['l_qkv'], t - 1)
                for kc in range(KC):
                    last = a(xnT[:, kc, u * P:(u + 1) * P], pb[0][:, kc * P:(kc + 1) * P], ACT.Identity,
                             scale=lg[:, kc:kc + 1], bias=lb[:, kc:kc + 1])
                last.then_inc(s['l_xT'], 1)

            def proj_qk(t, u):
                act.wait_ge(s['l_qkv'], t + 1)
                act.wait_ge(s['const'], 2)
                a(qkv[:, bass.ds(t, 1), 0:2 * D].rearrange("p a d -> p (a d)"), pb[1 + 2 * u][:], ACT.Copy)\
                    .then_inc(s['l_qk'], 1)

            proj_T(0, 0, True)
            proj_T(1, 1, True)
            with act.Fori(0, (T - 2) // 2) as i:
                for u in range(2):
                    proj_qk(i * 2 + u, u)
                    proj_T(i * 2 + (2 + u), u, False)
            proj_qk(T - 2, 0)
            proj_qk(T - 1, 1)
            root(T * 2 * NH + 2 * NH)
            ready(ACT.Exp)

            NU = 2 * (TB + 1)
            HEADS, USES = B * NH, 5 + TB + 2

            TURNED = (0, 1, 2, 7, 0)

            def high(n, use, b, k, o=None):
                o = pb[TURNED[k]] if o is None else o
                act.wait_ge(s['t_full'], use + (k + 1))
                act.wait_ge(s['const'], 2)
                dst, gam = ((q_hi[b][:, (k % 2) * 512:(k % 2 + 1) * 512], qg) if k < 2 else
                            (k_hl[b][:, (k - 2) * 512:min((k - 1) * 512, S + SK)], kg))
                a(dst, o[:, 0:dst.shape[-1]], ACT.Copy, scale=gam[:, :]).then_inc(s['a_hi'], 1)

            def minus(use, b, half):
                act.wait_ge(s['t_full'], use + (half + 1))
                a(q_lo[b][DH:DA, half * 512:(half + 1) * 512], pb[7][DH:DA, :], ACT.Copy).then_inc(s['t_free'], 1)

            def step(n, b, use, first, last):
                minus_at = use + 5 if first else use + 5 + TB
                for q in range(NU):
                    act.wait_ge(s['a_s_full'], n * NU + (q + 1))
                    if q >= 3 or not first:
                        act.wait_ge(s['a_pv'], n * NU + (q - 2))
                    if q < 2 * TB:
                        a(pT[q % 3], pb[3 + q % 2][:], ACT.Exp).then_inc(s['a_p'], 1)
                    else:
                        a(pT[q % 3][0:SK, :], pb[3 + q % 2][0:SK, :], ACT.Exp, bias=mask_col[:, b:b + 1]).then_inc(s['a_p'], 1)
                    if 1 <= q <= 5 and not last:
                        high(n + 1, use, 1 - b, q - 1)
                    if q in (16, 17) and not last:
                        minus(minus_at, 1 - b, q - 16)
                act.wait_ge(s['a_pv'], n * NU + NU)
                a(oT[b][0:DA, 0:512], pb[5][0:DA, :], ACT.Copy)
                a(oT[b][0:DA, 512:S], pb[6][0:DA, :], ACT.Copy).then_inc(s['a_o'], 1)

            for k in range(5):
                high(0, 0, 0, k, pb[3 + k])
            for half in range(2):
                minus(5, 0, half)
            step(0, 0, 7, True, False)
            with act.Fori(0, NH - 1) as i:
                step(i * 2 + 1, 1, i * (2 * USES) + (USES - 1), False, False)
                step(i * 2 + 2, 0, i * (2 * USES) + (2 * USES - 1), False, False)
            step(HEADS - 1, 1, (HEADS - 1) * USES - 1, False, True)

            root(T)
            with act.Fori(0, T // 4) as i:
                for u in range(4):
                    t = i * 4 + u
                    act.wait_ge(s['r_xT_full'], t + 1)
                    act.wait_ge(s['r_logit'], i * 4)
                    a(xnT[:, :, u * P:(u + 1) * P], pb[u][:, 0:D].rearrange("p (a b) -> p a b", a=KC), ACT.Copy).then_inc(s['r_xT'], 1)
            act.wait_ge(s['r_e'], 1)
            a(score[:], score[:], ACT.Exp).then_inc(s['r_exp'], 1)
            ready(ACT.Sigmoid)

            def mixture(k, n):
                def tokens(t, u):
                    act.wait_ge(m[k]['xinT_full'], t + 1)
                    a(x_inT[u][:].rearrange("p a b -> p (a b)"), pb[4][:, 0:D], ACT.Copy).then_inc(m[k]['xinT'], 1)

                def lifted(t, side):
                    act.wait_ge(m[k]['prod'], t * 2 + (1 + side))
                    act.wait_ge(m[k]['lined' if side else 'gated'], t)
                    a(lift[side], pb[2 * side + 1][:], ACT.Copy).then_inc(m[k]['lifted'], 1)

                def hidden(t):
                    act.wait_ge(m[k]['hT_full'], t + 1)
                    a(h_moeT[:].rearrange("p a b -> p (a b)"), pb[5][:], ACT.Copy).then_inc(m[k]['hT'], 1)

                def step(t, u, turn, first, more):
                    lifted(t, 0)
                    if not first:
                        hidden(t - 1)
                    act.wait_ge(m[k]['gated'], t + 1)
                    a(sig, gate, ACT.Sigmoid, scale=ALPHA).then_inc(m[k]['sigd'], 1)
                    lifted(t, 1)
                    if more:
                        tokens(t + 1, 1 - u)

                tokens(0, 0)
                step(0, 0, 0, True, True)
                pairs = (n - 2) // 2
                with act.Fori(0, pairs) as i:
                    for u in range(2):
                        step(i * 2 + (1 + u), 1 - u, i, False, True)
                for t in range(2 * pairs + 1, n):
                    step(t, t % 2, (t - 1) // 2, False, t + 1 < n)
                hidden(n - 1)

            mixture(0, T)
            mixture(1, SLOTS)

        @block.vector
        def _(ve):
            v = nc.vector
            link = Chain(ve, s['chain'])
            roots = [0]

            def norm(n, guard):
                ve.wait_ge(s['root_out'], roots[0] + 1)
                roots[0] += 1
                r, q, t_, d = root_a[:, 0:n], root_s[:, 0:n], root_t[:, 0:n], rstd[:, 0:n]
                link(v.tensor_scalar(t_, q, 1e-30, None, ALU.max))
                link(v.reciprocal(d, t_))
                link(v.tensor_tensor(t_, r, d, ALU.mult))
                link(v.tensor_tensor(t_, t_, q, ALU.add))
                link(v.tensor_scalar(t_, t_, 0.5, guard, ALU.mult, ALU.max))
                link(v.reciprocal(d, t_))

            ve.wait_ge(s['const'], 2)
            link(v.tensor_scalar(eno_i[:], eno_i[:], 31, None, ALU.bitwise_and))
            link(v.tensor_copy(eno[:], eno_i[:]))
            link(v.tensor_scalar(eno_sh[:], eno[:], float(SHARED), None, ALU.is_equal))
            v.tensor_copy(hot_sh[:], eno_sh[0:96, 0:1].to_broadcast([96, P])).then_inc(s['r_hot_sh'], 1)
            ve.wait_ge(s['ld_x'], NLD['ld_x'])
            for t in range(T):
                last = v.bn_stats(stats[:, t, :], x_sb[:, t, :])
            link(last)

            def aggregate(t0, t1):
                for t in range(t0, t1):
                    last = v.bn_aggr(mv[:, t, :], stats[:, t, :])
                link(last)

            aggregate(0, T)
            ve.wait_ge(s['ld_l0'], NLD['ld_l0'])
            for b in range(B):
                link(v.bn_stats(root_t[0:SK, 8 * b:8 * b + 6], ctx_sb[0:SK, b, :]))
                link(v.bn_aggr(mv[0:SK, T + b, :], root_t[0:SK, 8 * b:8 * b + 6]))
            v.tensor_scalar(root_a[:, 0:T + B], mv[:, :, 1], LN_EPS, None, ALU.add).then_inc(s['root_in'], 1)
            norm(T + B, 0.0)
            flat = lambda ap: ap.rearrange("p a b -> p (a b)")

            def tile(t):
                return x_sb[:, bass.ds(t, 1), :].rearrange("p a d -> p (a d)")

            def col(ap, t):
                return ap[:, bass.ds(t, 1)]

            def statistics(t):
                return v.bn_stats(stats[:, bass.ds(t, 1), :].rearrange("p a d -> p (a d)"), tile(t))

            def normalise(dst, t):
                return v.tensor_scalar(dst, tile(t), mv[:, bass.ds(t, 1), 0:1].rearrange("p a d -> p (a d)"), col(rstd, t),
                                       ALU.subtract, ALU.mult)

            def tokens0(it):
                if it > 0:
                    ve.wait_ge(s['g_xnT_full'], it)
                for u in range(4):
                    t = it * 4 + u
                    last = v.tensor_scalar(xn[:, u, :], x_sb[:, t, :], mv[:, t, 0:1], rstd[:, t:t + 1], ALU.subtract, ALU.mult)
                last.then_inc(s['g_xn'], 1)

            def magnitudes():
                for b in range(B):
                    last = v.tensor_scalar(ctx_sb[0:SK, b, :], ctx_sb[0:SK, b, :], mv[0:SK, T + b, 0:1], rstd[0:SK, T + b:T + b + 1],
                                           ALU.subtract, ALU.mult)
                last.then_inc(s['ctx_n'], 1)
                ve.wait_ge(s['ld_ffn'], NLD['ld_ffn'])
                v.tensor_reduce(wsum[:, 0:1], w1_raw[:], AX.XY, ALU.add, apply_absolute_value=True)
                v.tensor_reduce(wsum[:, 1:2], w2_raw[:], AX.XY, ALU.add, apply_absolute_value=True).then_inc(s['w_abs'], 1)

            def ternary(k):
                if k == 0:
                    ve.wait_ge(s['w_sum'], 1)
                    link(v.tensor_scalar(wsc, pb[2][:, 510:512], 1.0 / (HID * D), QEPS, ALU.mult, ALU.max))
                    link(v.reciprocal(winv, wsc))
                raw, q = ((w1_raw, w1_t), (w2_raw, w2_t))[k]
                link(v.tensor_scalar(raw[:], raw[:], winv[:, k:k + 1], MAGIC, ALU.mult, ALU.add))
                link(v.tensor_scalar(raw[:], raw[:], MAGIC, 1.0, ALU.subtract, ALU.min))
                v.tensor_scalar(q, raw[:], -1.0, None, ALU.max).then_inc(s['f_pre'], 1)

            def masks():
                ve.wait_ge(s['ld_l1'], NLD['ld_l1'])
                v.tensor_scalar(mask_row[:], mask_u[0:1, :], BIG, -BIG, ALU.mult, ALU.add)
                link(v.tensor_scalar(mask_col[:], maskc_u[:], BIG, -BIG, ALU.mult, ALU.add))

            between = [magnitudes, lambda: ternary(0), lambda: ternary(1), masks]
            tokens0(0)
            tokens0(1)
            for it in range(T // 4):
                ve.wait_ge(s['g_sc'], it + 1)
                sc = pb[2][:, 0:4 * SK].rearrange("p (a b) -> p a b", a=4)
                link(v.tensor_reduce(mx4, sc, AX.X, ALU.max))
                v.tensor_tensor(p0[:], sc, mx4.unsqueeze(2).to_broadcast([P, 4, SK]), ALU.subtract).then_inc(s['g_sh'], 1)
                if it + 2 < T // 4:
                    tokens0(it + 2)
                if it == T // 4 - 1:
                    aggregate(0, T - 4)
                ve.wait_ge(s['g_p'], it + 1)
                link(v.tensor_reduce(sums4, p0[:], AX.X, ALU.add))
                link(v.reciprocal(sums4, sums4))
                ve.wait_ge(s['g_pT_full'], it + 1)
                v.tensor_copy(p0T[0:SK, :], pb[3][0:SK, :]).then_inc(s['g_pT'], 1)
                between[it]()
                ve.wait_ge(s['g_av'], it + 1)
                for u in range(4):
                    t = it * 4 + u
                    last = v.scalar_tensor_tensor(x_sb[:, t, :], pb[4 + u // 2][:, (u % 2) * D:(u % 2 + 1) * D],
                                                  sums4[:, u:u + 1], x_sb[:, t, :], ALU.mult, ALU.add)
                link(last)
                for u in range(4):
                    t = it * 4 + u
                    last = v.bn_stats(stats[:, t, :], x_sb[:, t, :])
                link(last)
            aggregate(T - 4, T)
            v.tensor_scalar(root_a[:, 0:T], mv[:, 0:T, 1], LN_EPS, None, ALU.add).then_inc(s['root_in'], 1)
            norm(T, 0.0)

            def ffn_tokens(t, u):
                if not isinstance(t, int) or t >= 2:
                    ve.wait_ge(s['f_xq'], t - 1)
                link(normalise(xn[:, u, :], t))
                return v.tensor_reduce(f_max[:, 0:1], xn[:, u, :], AX.X, ALU.max, apply_absolute_value=True)

            def ffn_largest(t, u):
                ve.wait_ge(s['f_amax'], t + 1)
                return v.tensor_reduce(f_max[:, 1:2], h_f[u], AX.X, ALU.max, apply_absolute_value=True)

            def ffn_factors(u, c):
                link(v.tensor_scalar(f_max[:, c], f_max[:, c], QEPS, None, ALU.max))
                link(v.reciprocal(f_by[:, u, c], f_max[:, c]))
                v.tensor_scalar(f_by[:, u, c], f_by[:, u, c], QB, None, ALU.mult).then_inc(s['f_by'], 1)

            def ffn_hidden(t, u):
                ve.wait_ge(s['f_h'], t + 1)
                if not isinstance(t, int) or t >= 2:
                    ve.wait_ge(s['f_hq'], t - 1)
                for half in range(2):
                    c = slice(half * 512, (half + 1) * 512)
                    last = v.scalar_tensor_tensor(h_f[u][:, c], pb[2 * u + half][:], f_step[:, u, 0:1], b1_all[:, c], ALU.mult, ALU.add)
                last.then_inc(s['f_acc'], 1)

            def ffn_finish(t, u):
                ve.wait_ge(s['f_y'], t + 1)
                ve.wait_ge(s['f_b2'], t + 1)
                v.scalar_tensor_tensor(tile(t), pb[6][:, 0:D], f_step[:, 1 - u, 1:2], tile(t), ALU.mult, ALU.add)\
                    .then_inc(s['f_yout'], 1)
                ve.wait_ge(s['f_yout'], t + 1)
                link(statistics(t))

            def ffn_turn(i, u):
                if there(i - 1):
                    ffn_finish(i - 1, 1 - u)
                elif there(i + 1):
                    ve.wait_ge(s['f_acc'], i + 2)
                if there(i + 3) or there(i):
                    c = slice(0 if there(i + 3) else 1, 2 if there(i) else 1)
                    last = v.scalar_tensor_tensor(f_step[:, 1 - u, c], f_max[:, c], 1.0 / QB, wsc[:, c], ALU.mult, ALU.mult)
                    if not there(i + 4):
                        link(last)
                if there(i + 4):
                    last = ffn_tokens(i + 4, u)
                if there(i + 1):
                    last = ffn_largest(i + 1, 1 - u)
                c = slice(0 if there(i + 4) else 1, 2 if there(i + 1) else 1)
                if there(i + 4) or there(i + 1):
                    link(last)
                    ffn_factors(u, c)
                if there(i + 2):
                    ffn_hidden(i + 2, u)
                if isinstance(i, int) and i == T - 2:
                    aggregate(0, T - 3)

            ffn_turns(ve, ffn_turn, link, 5)
            aggregate(T - 3, T)

            v.tensor_scalar(root_a[:, 0:T], mv[:, 0:T, 1], 1.0 + LN_EPS, LN_EPS ** 2, ALU.mult, ALU.add).then_inc(s['root_in'], 1)
            norm(T, 0.0)
            sq = [oT[0][:, 0:512], oT[1][:, 0:512]]

            def proj_tokens(t, u):
                normalise(xn[:, u, :], t).then_inc(s['l_xh'], 1)

            def proj_kept(t, u):
                ve.wait_ge(s['l_qkv'], t + 1)
                v.tensor_copy(qkv[:, bass.ds(t, 1), 2 * D:QKV].rearrange("p a d -> p (a d)"), pb[2 + 2 * u][:, 0:D]).then_inc(s['l_v'], 1)
                ve.wait_ge(s['l_qk'], t + 1)
                qk = qkv[:, bass.ds(t, 1), 0:2 * D].rearrange("p a d -> p (a d)")
                link(v.tensor_tensor(sq[u], qk, qk, ALU.mult))
                v.tensor_reduce(ss_l[:, bass.ds(t * (2 * NH), 2 * NH)], sq[u].rearrange("p (a b) -> p a b", a=2 * NH), AX.X, ALU.add)

            ss_l = p0[:].rearrange("p a b -> p (a b)")
            NSS = T * 2 * NH + 2 * NH
            link(v.memset(ss_l[:, 0:NSS], 1.0))
            ve.wait_ge(s['prep_free'], NLD['prep'])
            for b in range(B):
                link(v.tensor_tensor(sq[b][0:SK, 0:D], ckv[0:SK, b, 0:D], ckv[0:SK, b, 0:D], ALU.mult))
                v.tensor_reduce(ss_l[0:SK, T * 2 * NH + b * NH:T * 2 * NH + (b + 1) * NH],
                                sq[b][0:SK, 0:D].rearrange("p (a b) -> p a b", a=NH), AX.X, ALU.add)
            proj_tokens(0, 0)
            proj_tokens(1, 1)
            with ve.Fori(0, (T - 2) // 2) as i:
                link.loop(i, 2)
                for u in range(2):
                    ve.wait_ge(s['l_xT'], i * 2 + (u + 1))
                    proj_tokens(i * 2 + (2 + u), u)
                    proj_kept(i * 2 + u, u)
            link.done((T - 2) // 2)
            proj_kept(T - 2, 0)
            proj_kept(T - 1, 1)
            v.tensor_copy(mx4[:, 1:2], f_max[:, 0:1]).then_inc(s['l_free'], 1)
            link(v.tensor_copy(mx4[:, 0:1], f_max[:, 0:1]))
            v.tensor_scalar(root_a[:, 0:NSS], ss_l[:, 0:NSS], 1.0 / DH, None, ALU.mult).then_inc(s['root_in'], 1)
            norm(NSS, RMS_EPS)
            rq = rstd[:, 0:T * 2 * NH].rearrange("p (a b) -> p a b", a=T)
            link(v.tensor_scalar(rq[:, :, 0:NH], rq[:, :, 0:NH], float(DH) ** -0.5, None, ALU.mult))

            HEADS, USES = B * NH, 5 + TB + 2
            ve.wait_ge(s['l_bo'], T)

            def scaled(h, b):
                for dst, a0, r0 in ((q_dup, 0, 0), (k_dup[:, 0:TB, :], D, NH)):
                    src = qkv[:, b * TB:(b + 1) * TB, bass.ds(h * DH + a0, DH)].unsqueeze(2).to_broadcast([P, TB, 2, DH])
                    r = rq[:, b * TB:(b + 1) * TB, bass.ds(h + r0, 1)].unsqueeze(2).to_broadcast([P, TB, 2, DH])
                    last = v.tensor_tensor(dst.rearrange("p t (a d) -> p t a d", a=2), src, r, ALU.mult)
                    if a0 == 0:
                        last.then_inc(s['a_q'], 1)
                rc = rstd[0:SK, bass.ds(h + (b * NH + T * 2 * NH), 1)]
                csrc = ckv[0:SK, b, bass.ds(h * DH, DH)].unsqueeze(1).to_broadcast([SK, 2, DH])
                v.tensor_scalar(k_dup[0:SK, TB, :].rearrange("p (a d) -> p a d", a=2), csrc, rc, None, ALU.mult)\
                    .then_inc(s['a_qk'], 1)

            TURNED = (0, 1, 2, 7, 0)

            def low(n, b, k, o=None):
                o = pb[TURNED[k]] if o is None else o
                ve.wait_ge(s['a_hi'], n * 5 + (k + 1))
                if k < 2:
                    hi, dst, src, gam = q_hi[b][0:DH], q_lo[b][0:DH], o[0:DH], qg[0:DH, :]
                else:
                    hi, dst, src, gam = k_hl[b][DH:P], k_hl[b][DH:P], o[DH:P], kg[DH:P, :]
                at = slice((k % 2) * 512, (k % 2 + 1) * 512) if k < 4 else slice(S, S + SK)
                v.scalar_tensor_tensor(dst[:, at], src[:, 0:at.stop - at.start], gam, hi[:, at].bitcast(f32), ALU.mult, ALU.subtract)\
                    .then_inc(s['t_free'], 1)

            def maximum(n, t, o=0):
                ve.wait_ge(s['a_mx_full'], n * TB + (t + 1))
                v.tensor_reduce(mx8[:, t:t + 1], banks[:, o:o + S + SK], AX.X, ALU.max).then_inc(s['a_mx_free'], 1)

            def minus(n):
                ve.wait_ge(s['a_mx_free'], n * TB + TB)
                v.tensor_scalar(negm, mx8, -1.0, None, ALU.mult).then_inc(s['a_negm'], 1)

            def joined(use, b, t, last, o=pb[7]):
                ve.wait_ge(s['t_full'], use + (t + 1))
                link(v.reciprocal(yden[:, 0:1], o[:, D:D + 1]))
                x_t = x_sb[:, b * TB + t, :]
                v.scalar_tensor_tensor(x_t, o[:, 0:D], yden[:, 0:1], x_t, ALU.mult, ALU.add).then_inc(s['t_free'], 1)
                if last:
                    ve.wait_ge(s['t_free'], use + (t + 1))
                    v.bn_stats(stats[:, b * TB + t, :], x_t)

            def step(n, b, use, h_next, first, last, more):
                if not last:
                    for k in range(5):
                        low(n + 1, 1 - b, k)
                for t in range(TB):
                    if not last:
                        maximum(n + 1, t)
                    if not first:
                        joined(use if last else use + 5, 1 - b, t, last)
                if not last:
                    minus(n + 1)
                if more:
                    scaled(h_next, b)

            scaled(0, 0)
            for k in range(5):
                low(0, 0, k, pb[3 + k])
            for t in range(TB):
                maximum(0, t, t % 2 * 3 * 512)
            minus(0)
            scaled(0, 1)
            step(0, 0, 7, 1, True, False, True)
            with ve.Fori(0, NH - 2) as i:
                link.loop(i, 2 * TB)
                step(i * 2 + 1, 1, i * (2 * USES) + (USES - 1), i + 1, False, False, True)
                step(i * 2 + 2, 0, i * (2 * USES) + (2 * USES - 1), i + 2, False, False, True)
            link.done(NH - 2)
            end = (HEADS - 3) * USES - 1
            step(HEADS - 3, 1, end, NH - 1, False, False, True)
            step(HEADS - 2, 0, end + USES, None, False, False, False)
            end += 2 * USES
            step(HEADS - 1, 1, end, None, False, True, False)
            link(v.tensor_copy(mx4[:, 0:1], yden[:, 0:1]))
            aggregate(0, TB)
            end += TB

            def inverse(t):
                ve.wait_ge(s['t_full'], end + (t + 1))
                return v.reciprocal(yden[:, t % 2:t % 2 + 1], pb[t][:, D:D + 1])

            link(inverse(0))
            for t in range(TB):
                x_t = x_sb[:, TB + t, :]
                v.scalar_tensor_tensor(x_t, pb[t][:, 0:D], yden[:, t % 2:t % 2 + 1], x_t, ALU.mult, ALU.add).then_inc(s['t_free'], 1)
                if t + 1 < TB:
                    inverse(t + 1)
                ve.wait_ge(s['t_free'], end + (t + 1))
                link(v.bn_stats(stats[:, TB + t, :], x_t))
            ve.sem_inc(s['a_oT'], 1)

            aggregate(TB, T)
            v.tensor_scalar(root_a[:, 0:T], mv[:, 0:T, 1], LN_EPS, None, ALU.add).then_inc(s['root_in'], 1)
            norm(T, 0.0)
            ve.wait_ge(s['r_bias'], 1)
            for t in range(T):
                if t >= 4:
                    ve.wait_ge(s['r_xm'], t - 3)
                    ve.wait_ge(s['r_xT_full'], t - 3)
                v.tensor_scalar(xn[:, t % 4, :], x_sb[:, t, :], mv[:, t, 0:1], rstd[:, t:t + 1], ALU.subtract, ALU.mult)\
                    .then_inc(s['r_x'], 1)

            wide = lambda ap: ap.unsqueeze(2).to_broadcast([P, T, E])
            ve.wait_ge(s['r_logit'], T)
            lg3 = pb[7][:, 0:T * E].rearrange("p (a b) -> p a b", a=T)
            link(v.tensor_reduce(den16, lg3, AX.X, ALU.max))
            v.tensor_tensor(score[:], lg3, wide(den16), ALU.subtract).then_inc(s['r_e'], 1)
            ve.wait_ge(s['r_exp'], 1)
            link(v.tensor_reduce(den16, score[:], AX.X, ALU.add))
            link(v.reciprocal(den16, den16))
            link(v.tensor_tensor(score[:], score[:], wide(den16), ALU.mult))
            link(v.tensor_tensor(biased[:], score[:], gateb[:].unsqueeze(1).to_broadcast([P, T, E]), ALU.add))
            ve.wait_ge(s['r_table'], 1)
            bg1 = big1.rearrange("p (t e) f -> p t e f", t=T)
            bg2 = big2.rearrange("p (t e) f -> p t e f", t=T)
            theirs = biased[:].unsqueeze(2).to_broadcast([P, T, E, E])
            mine = biased[:].unsqueeze(3).to_broadcast([P, T, E, E])
            v.tensor_tensor(bg1, theirs, mine, ALU.is_gt)
            link(v.tensor_tensor(bg2, theirs, mine, ALU.is_equal))
            link(v.tensor_tensor(bg2, bg2, lower[:].unsqueeze(1).to_broadcast([P, T, E, E]), ALU.mult))
            link(v.tensor_tensor(bg1, bg1, bg2, ALU.add))
            link(v.tensor_reduce(rank[:], bg1, AX.X, ALU.add))
            v.tensor_scalar(sel_b[:], rank[:], float(TOPK), None, ALU.is_lt).then_inc(s['r_sel'], 1)
            for c in range(TOPK):
                v.tensor_scalar(chosen[c][:], rank[:], float(c), None, ALU.is_equal)

            def places():
                ve.wait_ge(s['r_pos_full'], 1)
                link(v.tensor_copy(flat(pos[:]), pb[7][:, T * E:(2 * T + 1) * E]))
                link(v.tensor_scalar(ntile, pos[:, T, :], 1.0 / P, 0.5 - 0.5 / P, ALU.mult, ALU.add))
                link(v.tensor_scalar(ntile_r, ntile, MAGIC, None, ALU.add))
                link(v.tensor_scalar(ntile, ntile_r, MAGIC, None, ALU.subtract))
                link(v.tensor_tensor_scan(tend, ones[:, 0:E], ntile, 0.0, ALU.mult, ALU.add))
                link(v.tensor_tensor(tstart, tend, ntile, ALU.subtract))
                link(v.tensor_scalar(tstart, tstart, float(P), None, ALU.mult))
                v.tensor_copy(mx4[:, 0:1], tstart[:, 0:1]).then_inc(s['r_start'], 1)
                link(v.tensor_tensor(slot_cmp[:], tend.unsqueeze(1).to_broadcast([P, SLOTS, E]),
                                     slot_no.unsqueeze(2).to_broadcast([P, SLOTS, E]), ALU.is_le))
                link(v.tensor_reduce(slot_e[:], slot_cmp[:], AX.X, ALU.add))
                link(v.tensor_scalar(slot_e[:], slot_e[:], float(E - 1), None, ALU.min))
                link(v.tensor_copy(slot_i[:], slot_e[0:1, :]))
                v.tensor_scalar(hot[:], slot_e[0:96, :], eno[0:96, 0:1], None, ALU.is_equal).then_inc(s['r_slot'], 1)

            def mixture(k, n, split, between):
                def step(t):
                    ve.wait_ge(m[k]['lifted'], t * 2 + 1)
                    ve.wait_ge(m[k]['hid'], t)
                    link(v.tensor_tensor(gate, pb[0][:], lift[0], ALU.mult))
                    v.tensor_scalar(gate, gate, LIMIT, None, ALU.min).then_inc(m[k]['gated'], 1)
                    ve.wait_ge(m[k]['lifted'], t * 2 + 2)
                    link(v.tensor_tensor(line, pb[2][:], lift[1], ALU.mult))
                    v.tensor_scalar(line, line, LIMIT, -LIMIT, ALU.min, ALU.max).then_inc(m[k]['lined'], 1)
                    ve.wait_ge(m[k]['sigd'], t + 1)
                    link(v.tensor_tensor(sig, sig, gate, ALU.mult))
                    ve.wait_ge(m[k]['hT_full'], t)
                    v.scalar_tensor_tensor(h_moe, line, 1.0, sig, ALU.add, ALU.mult).then_inc(m[k]['hid'], 1)

                def result(t):
                    ve.wait_ge(m[k]['y'], t + 1)
                    if k == 0:
                        v.tensor_tensor(tile(t), tile(t), pb[6][:, 0:D], ALU.add).then_inc(m[k]['ysb'], 1)
                    else:
                        ve.wait_ge(c_prior, t * 16 + 16)
                        weight = meta[:, bass.ds(t, 1), 1:2].rearrange("p a b -> p (a b)")
                        v.scalar_tensor_tensor(y_sb, pb[6][:, 0:D], weight, prior, ALU.mult, ALU.add).then_inc(m[k]['ysb'], 1)

                step(0)
                for a0, a1 in ((0, split), (split, n - 1))[0:1 + (split < n - 1)]:
                    with ve.Fori(0, a1 - a0) as i:
                        link.loop(i, 3)
                        step(i + (a0 + 1))
                        result(i + a0)
                    link.done(a1 - a0)
                    if a1 < n - 1:
                        between()
                result(n - 1)

            mixture(0, T, 2 * PLACES_AT, places)
            mixture(1, SLOTS, SLOTS - 1, None)


def kernel(**inputs):
    import concourse.bacc as _bacc
    from concourse.bass_utils import run_bass_kernel_spmd as _run

    nc = _bacc.Bacc("TRN2", target_bir_lowering=False, num_devices=1)
    arrays, args = {}, {}
    for name in _INS:
        a = np.ascontiguousarray(inputs[name])
        if a.dtype == np.bool_:
            a = a.astype(np.int32)
        arrays[f"in_{name}"] = a
        args[name] = nc.dram_tensor(f"in_{name}", a.shape, mybir.dt.from_np(a.dtype), kind="ExternalInput").ap()
    out = nc.dram_tensor("out", inputs['x'].shape, mybir.dt.float32, kind="ExternalOutput").ap()
    program(nc, args, out)
    r = _run(nc, [arrays], core_ids=[0])
    return r.results[0]["out"]
```
